# Optimizing a Trainium2 kernel written in Bass

```python
import numpy as np
import jax
import jax.numpy as jnp

def _softmax(x, axis=-1):
    return jax.nn.softmax(x, axis=axis)

def _gelu(x):
    return jax.nn.gelu(x, approximate=True)

def _silu(x):
    return jax.nn.silu(x)

def _sigmoid(x):
    return jax.nn.sigmoid(x)

def _layernorm(x, axis=-1, eps=1e-05):
    m = jnp.mean(x, axis=axis, keepdims=True)
    v = jnp.var(x, axis=axis, keepdims=True)
    return (x - m) / jnp.sqrt(v + eps)

def _scatter_add(tgt, idx, src, axis=0):
    return tgt.at[idx].add(src)

def _segment_sum(src, seg, n):
    return jax.ops.segment_sum(src, seg, n)
kernel_name = 'mk_perceiver_d2_seqx_r4_218c50'

def setup_inputs(seed: int=0):
    np.random.seed(seed)
    _w = jnp.asarray

    def _rec_inputs():
        import jax
        import jax.numpy as jnp
        _rk = jax.random.key(seed)
        x = 7.22e-05 + 1 * jax.random.normal(jax.random.fold_in(_rk, 1), (8, 64, 512), jnp.float32)
        _lenS = 64 - jax.random.randint(jax.random.fold_in(_rk, 7), (8,), 0, max(1, 64 // 4) + 1, jnp.int32)
        _lenS2 = 1601 - jax.random.randint(jax.random.fold_in(_rk, 8), (8,), 0, max(1, 1601 // 4) + 1, jnp.int32)
        _ctx_512P = jax.random.normal(jax.random.fold_in(_rk, 11), (8, 16, 128), jnp.float32)
        _ctx_512c = jax.random.dirichlet(jax.random.fold_in(_rk, 511), 0.3 * jnp.ones((16,), jnp.float32), (8, 1601))
        _ctx_512t = jnp.einsum('bsk,bkd->bsd', _ctx_512c, _ctx_512P)
        _ctx_512t = _ctx_512t * jax.lax.rsqrt(jnp.mean(jnp.square(_ctx_512t)) + 1e-12) * 0.953939
        ctx_512 = -0.000514642 + 1.00011 * (_ctx_512t + 0.3 * jax.random.normal(jax.random.fold_in(_rk, 611), (8, 1601, 128), jnp.float32))
        return (x, ctx_512)
    x, ctx_512 = _rec_inputs()

    def _L0_xattn_setup():
        import jax, jax.numpy as jnp
        import numpy as np
        B, S, H, NH, L = (2, 512, 512, 16, 128)
        HD = H // NH
        key = jax.random.key(seed)
        k1, k2, k3, k4, k5 = jax.random.split(key, 5)
        scale = 0.02
        return {'q': jax.random.normal(k1, (B, S, H), dtype=jnp.float32), 'latent_kv': jax.random.normal(k2, (B, S, L), dtype=jnp.float32), 'Wq': jax.random.normal(k3, (H, H), dtype=jnp.float32) * scale, 'Wkv_expand': jax.random.normal(k4, (2 * H, L), dtype=jnp.float32) * scale, 'Wout': jax.random.normal(k5, (H, H), dtype=jnp.float32) * scale}
    _L0_xattn_all = _L0_xattn_setup()
    _L0_xattn_in = {k: v for k, v in _L0_xattn_all.items() if k in ('Wq', 'Wkv_expand', 'Wout')}
    del _L0_xattn_all

    def _L0_attn_setup():
        import jax, jax.numpy as jnp
        import numpy as np
        DIM = 512
        NUM_HEADS = 16
        HEAD_DIM = 128
        key = jax.random.key(seed)
        ks = jax.random.split(key, 9)
        B, S = (2, 512)
        s = lambda fan_in: 1.0 / np.sqrt(fan_in)
        return {'x': jax.random.normal(ks[0], (B, S, DIM), dtype=jnp.float32), 'Wq': jax.random.uniform(ks[1], (DIM, NUM_HEADS * HEAD_DIM), jnp.float32, -s(DIM), s(DIM)), 'bq': jax.random.uniform(ks[2], (NUM_HEADS * HEAD_DIM,), jnp.float32, -s(DIM), s(DIM)), 'Wk': jax.random.uniform(ks[3], (DIM, HEAD_DIM), jnp.float32, -s(DIM), s(DIM)), 'bk': jax.random.uniform(ks[4], (HEAD_DIM,), jnp.float32, -s(DIM), s(DIM)), 'Wv': jax.random.uniform(ks[5], (DIM, HEAD_DIM), jnp.float32, -s(DIM), s(DIM)), 'bv': jax.random.uniform(ks[6], (HEAD_DIM,), jnp.float32, -s(DIM), s(DIM)), 'Wo': jax.random.uniform(ks[7], (NUM_HEADS * HEAD_DIM, DIM), jnp.float32, -s(NUM_HEADS * HEAD_DIM), s(NUM_HEADS * HEAD_DIM)), 'bo': jax.random.uniform(ks[8], (DIM,), jnp.float32, -s(NUM_HEADS * HEAD_DIM), s(NUM_HEADS * HEAD_DIM))}
    _L0_attn_all = _L0_attn_setup()
    _L0_attn_in = {k: v for k, v in _L0_attn_all.items() if k in ('Wq', 'bq', 'Wk', 'bk', 'Wv', 'bv', 'Wo', 'bo')}
    del _L0_attn_all

    def _L0_ffn_setup():
        import jax, jax.numpy as jnp
        import numpy as np
        H = 512
        I = 256
        E = 32
        K = 4
        N_SHARED = 1
        EPS = 1e-06

        def _rmsnorm(x, w, eps=EPS):
            var = jnp.mean(jnp.square(x), axis=-1, keepdims=True)
            return x * jax.lax.rsqrt(var + eps) * w

        def _moe_core(x, gate_w, w13, w2):
            T = x.shape[0]
            N = T * K
            C = 2 * N // E
            logits = jnp.einsum('th,eh->te', x.astype(jnp.float32), gate_w.astype(jnp.float32))
            scores = jax.nn.softmax(logits, axis=-1)
            topk_w, topk_ids = jax.lax.top_k(scores, K)
            topk_w = topk_w / jnp.sum(topk_w, axis=-1, keepdims=True)
            flat_ids = topk_ids.reshape(-1)
            flat_w = topk_w.reshape(-1)
            order = jnp.argsort(flat_ids)
            sorted_eid = flat_ids[order]
            tok = order // K
            counts = jnp.zeros((E,), jnp.int32).at[flat_ids].add(1)
            starts = jnp.cumsum(counts) - counts
            pos = jnp.arange(N) - starts[sorted_eid]
            buf = jnp.zeros((E, C, x.shape[1]), x.dtype).at[sorted_eid, pos].set(x[tok], mode='drop')
            gu = jnp.einsum('ech,ehf->ecf', buf, w13)
            g, u = jnp.split(gu, 2, axis=-1)
            act = jax.nn.silu(g) * u
            eo = jnp.einsum('eci,eih->ech', act, w2)
            out_slots = eo[sorted_eid, pos]
            routed = jnp.zeros_like(x).at[tok].add(out_slots * flat_w[order][:, None])
            return routed
        key = jax.random.key(seed)
        ks = jax.random.split(key, 8)
        s = 1.0 / np.sqrt(H)
        si = 1.0 / np.sqrt(I)
        return {'hidden_states': jax.random.normal(ks[0], (1, 1024, H), jnp.float32), 'norm_w': jnp.ones((H,), jnp.float32), 'gate_w': jax.random.normal(ks[1], (E, H), jnp.float32) * s, 'w13': jax.random.normal(ks[2], (E, H, 2 * I), jnp.float32) * s, 'w2': jax.random.normal(ks[3], (E, I, H), jnp.float32) * si, 'shared_gate_w': jax.random.normal(ks[4], (H, I * N_SHARED), jnp.float32) * s, 'shared_up_w': jax.random.normal(ks[5], (H, I * N_SHARED), jnp.float32) * s, 'shared_down_w': jax.random.normal(ks[6], (I * N_SHARED, H), jnp.float32) * si}
    _L0_ffn_all = _L0_ffn_setup()
    _L0_ffn_in = {k: v for k, v in _L0_ffn_all.items() if k in ('norm_w', 'gate_w', 'w13', 'w2', 'shared_gate_w', 'shared_up_w', 'shared_down_w')}
    del _L0_ffn_all

    def _L1_xattn_setup():
        import jax, jax.numpy as jnp
        import numpy as np
        B, S, L = (2, 256, 256)
        DIM_Q, H, K, D_C, D_CQ, R = (512, 16, 128, 128, 384, 64)

        def _rope_tables(length, dim):
            inv = 1.0 / 10000.0 ** (jnp.arange(0, dim, 2, dtype=jnp.float32) / dim)
            f = jnp.arange(length, dtype=jnp.float32)[:, None] * inv[None, :]
            sin = jnp.repeat(jnp.sin(f), 2, axis=-1)
            cos = jnp.repeat(jnp.cos(f), 2, axis=-1)
            return (sin, cos)

        def _rotate_half(x):
            half = x.shape[-1] // 2
            return jnp.concatenate([-x[..., half:], x[..., :half]], axis=-1)

        def _apply_rope(x, sin, cos):
            return x * cos + _rotate_half(x) * sin
        key = jax.random.key(seed)
        ks = jax.random.split(key, 8)
        return {'hidden_q': jax.random.normal(ks[0], (B, S, DIM_Q), jnp.float32), 'kv_c': jax.random.normal(ks[1], (B, L, D_C), jnp.float32), 'Wq': jax.random.normal(ks[2], (H * K, DIM_Q), jnp.float32) / np.sqrt(DIM_Q).astype(np.float32), 'w_kc_q': jax.random.normal(ks[3], (H, K, D_CQ), jnp.float32) / np.sqrt(K).astype(np.float32), 'w_kc_kv': jax.random.normal(ks[4], (H, K, D_C), jnp.float32) / np.sqrt(K).astype(np.float32), 'W_qr': jax.random.normal(ks[5], (H, D_CQ, R), jnp.float32) / np.float32(np.sqrt(D_CQ) * np.sqrt(R)), 'W_kr': jax.random.normal(ks[6], (H, D_C, R), jnp.float32) / np.sqrt(D_C).astype(np.float32), 'Wo': jax.random.normal(ks[7], (DIM_Q, H * K), jnp.float32) / np.sqrt(H * K).astype(np.float32)}
    _L1_xattn_all = _L1_xattn_setup()
    _L1_xattn_in = {k: v for k, v in _L1_xattn_all.items() if k in ('Wq', 'w_kc_q', 'w_kc_kv', 'W_qr', 'W_kr', 'Wo')}
    del _L1_xattn_all

    def _L1_attn_setup():
        import jax, jax.numpy as jnp
        import numpy as np
        D_MODEL = 512
        HEADS = 16

        def _split(t, heads):
            b, s, d = t.shape
            return t.reshape(b, s, heads, d // heads).transpose(0, 2, 1, 3)
        key = jax.random.key(seed)
        ks = jax.random.split(key, 9)
        s = 1.0 / np.sqrt(D_MODEL)
        x = jax.random.normal(ks[0], (2, 512, D_MODEL), dtype=jnp.float32)
        wq = jax.random.uniform(ks[1], (D_MODEL, D_MODEL), jnp.float32, -s, s)
        wk = jax.random.uniform(ks[2], (D_MODEL, D_MODEL), jnp.float32, -s, s)
        wv = jax.random.uniform(ks[3], (D_MODEL, D_MODEL), jnp.float32, -s, s)
        wo = jax.random.uniform(ks[4], (D_MODEL, D_MODEL), jnp.float32, -s, s)
        bq = jax.random.uniform(ks[5], (D_MODEL,), jnp.float32, -s, s)
        bk = jax.random.uniform(ks[6], (D_MODEL,), jnp.float32, -s, s)
        bv = jax.random.uniform(ks[7], (D_MODEL,), jnp.float32, -s, s)
        bo = jax.random.uniform(ks[8], (D_MODEL,), jnp.float32, -s, s)
        return {'x': x, 'wq': wq, 'bq': bq, 'wk': wk, 'bk': bk, 'wv': wv, 'bv': bv, 'wo': wo, 'bo': bo}
    _L1_attn_all = _L1_attn_setup()
    _L1_attn_in = {k: v for k, v in _L1_attn_all.items() if k in ('wq', 'bq', 'wk', 'bk', 'wv', 'bv', 'wo', 'bo')}
    del _L1_attn_all

    def _L1_ffn_setup():
        import jax, jax.numpy as jnp
        import numpy as np
        EPS = 1e-05

        def rmsnorm(x, weight, eps=EPS):
            var = jnp.mean(x * x, axis=-1, keepdims=True)
            return x * jax.lax.rsqrt(var + eps) * weight

        def activation_quant(x):
            scale = 127.0 / jnp.clip(jnp.max(jnp.abs(x), axis=-1, keepdims=True), 1e-05, None)
            return jnp.clip(jnp.round(x * scale), -128, 127) / scale

        def weight_quant(w):
            scale = 1.0 / jnp.clip(jnp.mean(jnp.abs(w)), 1e-05, None)
            return jnp.clip(jnp.round(w * scale), -1, 1) / scale

        def bitlinear(x, w):
            xq = activation_quant(x)
            wq = weight_quant(w)
            return jnp.einsum('bsh,oh->bso', xq, wq)
        key = jax.random.key(seed)
        k1, k2, k3 = jax.random.split(key, 3)
        B, S, H, F = (4, 512, 512, 1408)
        x = jax.random.normal(k1, (B, S, H), dtype=jnp.float32)
        w_gate_up = jax.random.normal(k2, (2 * F, H), dtype=jnp.float32) * 0.02
        w_down = jax.random.normal(k3, (H, F), dtype=jnp.float32) * 0.02
        norm_weight = jnp.ones((H,), dtype=jnp.float32)
        return {'x': x, 'w_gate_up': w_gate_up, 'w_down': w_down, 'norm_weight': norm_weight}
    _L1_ffn_all = _L1_ffn_setup()
    _L1_ffn_in = {k: v for k, v in _L1_ffn_all.items() if k in ('w_gate_up', 'w_down', 'norm_weight')}
    del _L1_ffn_all
    return {'x': x, 'ctx_512': ctx_512, 'L0_xattn_Wq': _L0_xattn_in['Wq'], 'L0_xattn_Wkv_expand': _L0_xattn_in['Wkv_expand'], 'L0_xattn_Wout': _L0_xattn_in['Wout'], 'L0_attn_Wq': _L0_attn_in['Wq'], 'L0_attn_bq': _L0_attn_in['bq'], 'L0_attn_Wk': _L0_attn_in['Wk'], 'L0_attn_bk': _L0_attn_in['bk'], 'L0_attn_Wv': _L0_attn_in['Wv'], 'L0_attn_bv': _L0_attn_in['bv'], 'L0_attn_Wo': _L0_attn_in['Wo'], 'L0_attn_bo': _L0_attn_in['bo'], 'L0_ffn_norm_w': _L0_ffn_in['norm_w'], 'L0_ffn_gate_w': _L0_ffn_in['gate_w'], 'L0_ffn_w13': _L0_ffn_in['w13'], 'L0_ffn_w2': _L0_ffn_in['w2'], 'L0_ffn_shared_gate_w': _L0_ffn_in['shared_gate_w'], 'L0_ffn_shared_up_w': _L0_ffn_in['shared_up_w'], 'L0_ffn_shared_down_w': _L0_ffn_in['shared_down_w'], 'L1_xattn_Wq': _L1_xattn_in['Wq'], 'L1_xattn_w_kc_q': _L1_xattn_in['w_kc_q'], 'L1_xattn_w_kc_kv': _L1_xattn_in['w_kc_kv'], 'L1_xattn_W_qr': _L1_xattn_in['W_qr'], 'L1_xattn_W_kr': _L1_xattn_in['W_kr'], 'L1_xattn_Wo': _L1_xattn_in['Wo'], 'L1_attn_wq': _L1_attn_in['wq'], 'L1_attn_bq': _L1_attn_in['bq'], 'L1_attn_wk': _L1_attn_in['wk'], 'L1_attn_bk': _L1_attn_in['bk'], 'L1_attn_wv': _L1_attn_in['wv'], 'L1_attn_bv': _L1_attn_in['bv'], 'L1_attn_wo': _L1_attn_in['wo'], 'L1_attn_bo': _L1_attn_in['bo'], 'L1_ffn_w_gate_up': _L1_ffn_in['w_gate_up'], 'L1_ffn_w_down': _L1_ffn_in['w_down'], 'L1_ffn_norm_weight': _L1_ffn_in['norm_weight']}

def reference(x, ctx_512, L0_xattn_Wq, L0_xattn_Wkv_expand, L0_xattn_Wout, L0_attn_Wq, L0_attn_bq, L0_attn_Wk, L0_attn_bk, L0_attn_Wv, L0_attn_bv, L0_attn_Wo, L0_attn_bo, L0_ffn_norm_w, L0_ffn_gate_w, L0_ffn_w13, L0_ffn_w2, L0_ffn_shared_gate_w, L0_ffn_shared_up_w, L0_ffn_shared_down_w, L1_xattn_Wq, L1_xattn_w_kc_q, L1_xattn_w_kc_kv, L1_xattn_W_qr, L1_xattn_W_kr, L1_xattn_Wo, L1_attn_wq, L1_attn_bq, L1_attn_wk, L1_attn_bk, L1_attn_wv, L1_attn_bv, L1_attn_wo, L1_attn_bo, L1_ffn_w_gate_up, L1_ffn_w_down, L1_ffn_norm_weight):
    import jax
    import jax.numpy as jnp

    def _L0_xattn_ref(q, latent_kv, Wq, Wkv_expand, Wout):
        import jax, jax.numpy as jnp
        import numpy as np
        B, S, H, NH, L = (2, 512, 512, 16, 128)
        HD = H // NH
        b, sq, _ = q.shape
        sk = latent_kv.shape[1]
        qp = q @ Wq.T
        kv = latent_kv @ Wkv_expand.T
        k, v = jnp.split(kv, 2, axis=-1)
        qh = qp.reshape(b, sq, NH, HD).transpose(0, 2, 1, 3)
        kh = k.reshape(b, sk, NH, HD).transpose(0, 2, 1, 3)
        vh = v.reshape(b, sk, NH, HD).transpose(0, 2, 1, 3)
        inv_sqrt_d = 1.0 / jnp.sqrt(jnp.float32(HD))
        scores = jnp.einsum('bhqd,bhkd->bhqk', qh, kh) * inv_sqrt_d
        causal = jnp.tril(jnp.ones((sq, sk), dtype=bool))
        scores = jnp.where(causal, scores, jnp.finfo(scores.dtype).min)
        attn = jax.nn.softmax(scores, axis=-1)
        out = jnp.einsum('bhqk,bhkd->bhqd', attn, vh)
        out = out.transpose(0, 2, 1, 3).reshape(b, sq, H)
        return out @ Wout.T

    def _L0_attn_ref(x, Wq, bq, Wk, bk, Wv, bv, Wo, bo):
        import jax, jax.numpy as jnp
        import numpy as np
        DIM = 512
        NUM_HEADS = 16
        HEAD_DIM = 128
        B, S, _ = x.shape
        H, D = (NUM_HEADS, HEAD_DIM)
        q = (x @ Wq + bq).reshape(B, S, H, D)
        k = x @ Wk + bk
        v = x @ Wv + bv
        scale = 1.0 / np.sqrt(D).astype(np.float32)
        scores = jnp.einsum('bnhd,bmd->bnhm', q, k) * scale
        attn = jax.nn.softmax(scores, axis=-1)
        out = jnp.einsum('bnhm,bmd->bnhd', attn, v)
        out = out.reshape(B, S, H * D)
        return out @ Wo + bo

    def _L0_ffn_ref(hidden_states, norm_w, gate_w, w13, w2, shared_gate_w, shared_up_w, shared_down_w):
        import jax, jax.numpy as jnp
        import numpy as np
        H = 512
        I = 256
        E = 32
        K = 4
        N_SHARED = 1
        EPS = 1e-06

        def _rmsnorm(x, w, eps=EPS):
            var = jnp.mean(jnp.square(x), axis=-1, keepdims=True)
            return x * jax.lax.rsqrt(var + eps) * w

        def _moe_core(x, gate_w, w13, w2):
            T = x.shape[0]
            N = T * K
            C = 2 * N // E
            logits = jnp.einsum('th,eh->te', x.astype(jnp.float32), gate_w.astype(jnp.float32))
            scores = jax.nn.softmax(logits, axis=-1)
            topk_w, topk_ids = jax.lax.top_k(scores, K)
            topk_w = topk_w / jnp.sum(topk_w, axis=-1, keepdims=True)
            flat_ids = topk_ids.reshape(-1)
            flat_w = topk_w.reshape(-1)
            order = jnp.argsort(flat_ids)
            sorted_eid = flat_ids[order]
            tok = order // K
            counts = jnp.zeros((E,), jnp.int32).at[flat_ids].add(1)
            starts = jnp.cumsum(counts) - counts
            pos = jnp.arange(N) - starts[sorted_eid]
            buf = jnp.zeros((E, C, x.shape[1]), x.dtype).at[sorted_eid, pos].set(x[tok], mode='drop')
            gu = jnp.einsum('ech,ehf->ecf', buf, w13)
            g, u = jnp.split(gu, 2, axis=-1)
            act = jax.nn.silu(g) * u
            eo = jnp.einsum('eci,eih->ech', act, w2)
            out_slots = eo[sorted_eid, pos]
            routed = jnp.zeros_like(x).at[tok].add(out_slots * flat_w[order][:, None])
            return routed
        B, S, Hd = hidden_states.shape
        residual = hidden_states
        h = _rmsnorm(hidden_states, norm_w)
        x = h.reshape(-1, Hd)
        routed = _moe_core(x, gate_w, w13, w2)
        shared = jax.nn.silu(x @ shared_gate_w) * (x @ shared_up_w) @ shared_down_w
        out = residual + (routed + shared).reshape(B, S, Hd)
        return out

    def _L1_xattn_ref(hidden_q, kv_c, Wq, w_kc_q, w_kc_kv, W_qr, W_kr, Wo):
        import jax, jax.numpy as jnp
        import numpy as np
        B, S, L = (2, 256, 256)
        DIM_Q, H, K, D_C, D_CQ, R = (512, 16, 128, 128, 384, 64)

        def _rope_tables(length, dim):
            inv = 1.0 / 10000.0 ** (jnp.arange(0, dim, 2, dtype=jnp.float32) / dim)
            f = jnp.arange(length, dtype=jnp.float32)[:, None] * inv[None, :]
            sin = jnp.repeat(jnp.sin(f), 2, axis=-1)
            cos = jnp.repeat(jnp.cos(f), 2, axis=-1)
            return (sin, cos)

        def _rotate_half(x):
            half = x.shape[-1] // 2
            return jnp.concatenate([-x[..., half:], x[..., :half]], axis=-1)

        def _apply_rope(x, sin, cos):
            return x * cos + _rotate_half(x) * sin
        Bv, Sv, _ = hidden_q.shape
        _, Lv, _ = kv_c.shape
        q_hk = (hidden_q @ Wq.T).reshape(Bv, Sv, H, K)
        q_big = jnp.einsum('bshk,hkq->bshq', q_hk, w_kc_q)
        sin_q, cos_q = _rope_tables(Sv, D_CQ)
        q_big = _apply_rope(q_big, sin_q[None, :, None, :], cos_q[None, :, None, :])
        sin_k, cos_k = _rope_tables(Lv, D_C)
        kv_r = _apply_rope(kv_c, sin_k[None], cos_k[None])
        q_r = jnp.einsum('bshq,hqr->bhsr', q_big, W_qr)
        k_r = jnp.einsum('bld,hdr->bhlr', kv_r, W_kr)
        scores = jnp.einsum('bhsr,bhlr->bhsl', q_r, k_r)
        attn = jax.nn.softmax(scores, axis=-1)
        ctx_c = jnp.einsum('bhsl,bld->bhsd', attn, kv_r)
        ctx_lat = jnp.einsum('bhsd,hkd->bhsk', ctx_c, w_kc_kv)
        ctx = ctx_lat.transpose(0, 2, 1, 3).reshape(Bv, Sv, H * K)
        return ctx @ Wo.T

    def _L1_attn_ref(x, wq, bq, wk, bk, wv, bv, wo, bo):
        import jax, jax.numpy as jnp
        import numpy as np
        D_MODEL = 512
        HEADS = 16

        def _split(t, heads):
            b, s, d = t.shape
            return t.reshape(b, s, heads, d // heads).transpose(0, 2, 1, 3)
        q = x @ wq.T + bq
        k = x @ wk.T + bk
        v = x @ wv.T + bv
        q, k, v = (_split(q, HEADS), _split(k, HEADS), _split(v, HEADS))
        dh = q.shape[-1]
        scale = 1.0 / np.sqrt(dh).astype(np.float32)
        score = jnp.einsum('bhqd,bhkd->bhqk', q, k) * scale
        score = jax.nn.softmax(score.astype(jnp.float32), axis=-1).astype(q.dtype)
        out = jnp.einsum('bhqk,bhkd->bhqd', score, v)
        b, h, s, _ = out.shape
        out = out.transpose(0, 2, 1, 3).reshape(b, s, h * dh)
        return out @ wo.T + bo

    def _L1_ffn_ref(x, w_gate_up, w_down, norm_weight):
        import jax, jax.numpy as jnp
        import numpy as np
        EPS = 1e-05

        def rmsnorm(x, weight, eps=EPS):
            var = jnp.mean(x * x, axis=-1, keepdims=True)
            return x * jax.lax.rsqrt(var + eps) * weight

        def activation_quant(x):
            scale = 127.0 / jnp.clip(jnp.max(jnp.abs(x), axis=-1, keepdims=True), 1e-05, None)
            return jnp.clip(jnp.round(x * scale), -128, 127) / scale

        def weight_quant(w):
            scale = 1.0 / jnp.clip(jnp.mean(jnp.abs(w)), 1e-05, None)
            return jnp.clip(jnp.round(w * scale), -1, 1) / scale

        def bitlinear(x, w):
            xq = activation_quant(x)
            wq = weight_quant(w)
            return jnp.einsum('bsh,oh->bso', xq, wq)
        x_norm = rmsnorm(x, norm_weight)
        gate_up = bitlinear(x_norm, w_gate_up)
        gate, up = jnp.split(gate_up, 2, axis=-1)
        hidden = jnp.square(jax.nn.relu(gate)) * up
        return bitlinear(hidden, w_down)
    x = x + _L0_xattn_ref(_layernorm(x, axis=-1), ctx_512, L0_xattn_Wq, L0_xattn_Wkv_expand, L0_xattn_Wout)
    x = x + _L0_attn_ref(_layernorm(x, axis=-1), L0_attn_Wq, L0_attn_bq, L0_attn_Wk, L0_attn_bk, L0_attn_Wv, L0_attn_bv, L0_attn_Wo, L0_attn_bo)
    x = x + _L0_ffn_ref(_layernorm(x, axis=-1), L0_ffn_norm_w, L0_ffn_gate_w, L0_ffn_w13, L0_ffn_w2, L0_ffn_shared_gate_w, L0_ffn_shared_up_w, L0_ffn_shared_down_w)
    x = x + _L1_xattn_ref(_layernorm(x, axis=-1), ctx_512, L1_xattn_Wq, L1_xattn_w_kc_q, L1_xattn_w_kc_kv, L1_xattn_W_qr, L1_xattn_W_kr, L1_xattn_Wo)
    x = x + _L1_attn_ref(_layernorm(x, axis=-1), L1_attn_wq, L1_attn_bq, L1_attn_wk, L1_attn_bk, L1_attn_wv, L1_attn_bv, L1_attn_wo, L1_attn_bo)
    x = x + _L1_ffn_ref(_layernorm(x, axis=-1), L1_ffn_w_gate_up, L1_ffn_w_down, L1_ffn_norm_weight)
    return x

_drawn_inputs = setup_inputs


def setup_inputs(seed=0):
    import zlib

    import numpy as np

    out = dict(_drawn_inputs(seed))
    spreads = {'L0_ffn_norm_w': (1.0, 0.2), 'L1_ffn_norm_weight': (1.0, 0.6)}
    factors = {'L0_xattn_Wq': 8.0,
     'L0_attn_Wq': 2.821,
     'L0_attn_bq': 8.0,
     'L0_attn_Wk': 2.674,
     'L0_attn_bk': 64.0,
     'L0_attn_bo': 2.925,
     'L1_attn_wq': 6.4,
     'L1_attn_bq': 21.339,
     'L1_attn_wk': 5.478,
     'L1_attn_bk': 64.0,
     'L1_attn_bv': 8.0,
     'L1_attn_bo': 4.851}
    for name, (base, spread) in spreads.items():
        noise = np.random.default_rng([zlib.crc32(name.encode()), seed]).standard_normal(out[name].shape)
        drawn = base * np.exp(spread * noise) if base else spread * noise
        out[name] = jnp.asarray(drawn.astype(out[name].dtype))
    for name, factor in factors.items():
        out[name] = (out[name] * factor).astype(out[name].dtype)
    return out
```

```python
from contextlib import ExitStack

import concourse.bass as bass
from concourse import mybir

F32 = mybir.dt.float32
BF16 = mybir.dt.bfloat16
U32 = mybir.dt.uint32
ALU = mybir.AluOpType
ACT = mybir.ActivationFunctionType
AX = mybir.AxisListType.X

STAGES = 6

P = 128
B, S, DM = 8, 64, 512
TOK = B * S
NT = TOK // P
KC = DM // P
NH = 16
HD = DM // NH
LCTX = 1601
LT = 13
LFULL = LCTX // LT
LREST = LCTX - LFULL * LT
DC = 128
DCQ = 384
R = 64
NE, TOPK, FI = 32, 4, 256
CAP = 2 * TOK * TOPK // NE
FF = 1408
LN_EPS = 1e-5
MASKED = -3.0e38


def perceiver(nc, T, out, scratch):
    ctx = ExitStack()
    with ctx:
        def sb(name, shape, dt=F32):
            return ctx.enter_context(nc.sbuf_tensor(name, shape, dt))

        def sem(name):
            return ctx.enter_context(nc.semaphore(name))

        ps = ctx.enter_context(nc.psum_tensor("ps", [P, 8, 512], F32))

        x = sb("x", [P, NT, DM])
        xn = sb("xn", [P, NT, DM])
        xT = sb("xT", [P, KC, TOK])
        cst = sb("cst", [P, 5, P])
        ident, before, ones, iota = (cst[:, i, :] for i in range(4))
        causal = cst[:, 4, 0:S]
        vecs = sb("vecs", [P, 64])
        row_bias = sb("row_bias", [P, DM])
        stat = sb("stat", [P, 512])

        RA = sb("RA", [P, 8192])
        RB = sb("RB", [P, 8192])
        RC = sb("RC", [P, 5120])
        RQ = sb("RQ", [P, 8192])
        RR = sb("RR", [P, 8192])
        RE = sb("RE", [P, 6144])
        RG = sb("RG", [P, 1024])

        def cut(region, at, *shape):
            n = 1
            for s in shape:
                n *= s
            v = region[:, at:at + n]
            if len(shape) == 2:
                v = v.rearrange("p (a b) -> p a b", b=shape[1])
            if len(shape) == 3:
                v = v.rearrange("p (a b c) -> p a b c", b=shape[1], c=shape[2])
            return v

        class Chain:

            def __init__(self, eng, name):
                self.eng, self.sem, self.n, self.base = eng, sem(name), 0, 0

            def __call__(self, ins):
                self.n += 1
                ins.then_inc(self.sem, 1)
                self.eng.wait_ge(self.sem, self.n + self.base)

        bst = cut(stat, 0, NT, 6)
        mv = cut(stat, 24, NT, 2)
        rstd = stat[:, 32:36]
        vare = stat[:, 36:40]
        power = stat[:, 40:44]

        class Rounds:

            def __init__(self, prefix, per, sems=None, run=0):
                self.prefix, self.per, self.run = prefix, per, run
                self.sems = sems or {n: sem(f"{prefix}_{n}") for n in per}

            def again(self):
                return Rounds(self.prefix, self.per, self.sems, self.run + 1)

            def __getitem__(self, name):
                return self.sems[name]

            def wait(self, eng, name, value):
                assert 0 < value <= self.per[name]
                eng.wait_ge(self.sems[name], self.run * self.per[name] + value)

        norms = [Rounds("norm", {"var": 1, "rstd": 1, "xn": NT, "xT_ps": KC, "xT_act": 2, "xT_dve": 2})]
        for _ in range(5):
            norms.append(norms[-1].again())

        def norm_dve(dve, link, k):
            for t in range(NT):
                nc.vector.bn_stats(bst[:, t, :], x[:, t, :])
            link(nc.vector.memset(stat[:, 44:45], 0.0))
            for t in range(NT):
                i = nc.vector.bn_aggr(mv[:, t, :], bst[:, t, :])
            i.then_inc(norms[k]["var"], 1)
            norms[k].wait(dve, "rstd", 1)
            for t in range(NT):
                nc.vector.tensor_scalar(xn[:, t, :], x[:, t, :], mv[:, t, 0:1], rstd[:, t:t + 1],
                                        ALU.subtract, ALU.mult).then_inc(norms[k]["xn"], 1)

        def norm_pool(pool, link, k):
            norms[k].wait(pool, "var", 1)
            link(nc.gpsimd.tensor_scalar(vare, mv[:, :, 1], LN_EPS, None, ALU.add))
            nc.gpsimd.tensor_tensor(rstd, vare, power, ALU.pow).then_inc(norms[k]["rstd"], 1)

        def xT_pe(pe, k, rows=None, ready=None):
            rows = xn if rows is None else rows
            if ready is None:
                norms[k].wait(pe, "xn", NT)
            else:
                pe.wait_ge(ready, NT)
            for kc in range(KC):
                for t in range(NT):
                    i = nc.tensor.transpose(ps[:, kc, t * P:(t + 1) * P], rows[:, t, kc * P:(kc + 1) * P], ident)
                i.then_inc(norms[k]["xT_ps"], 1)

        def xT_act(act, k):
            for kc in (0, 1):
                norms[k].wait(act, "xT_ps", kc + 1)
                nc.scalar.copy(xT[:, kc, :], ps[:, kc, :]).then_inc(norms[k]["xT_act"], 1)

        def xT_dve(dve, k):
            for kc in (2, 3):
                norms[k].wait(dve, "xT_ps", kc + 1)
                nc.vector.tensor_copy(xT[:, kc, :], ps[:, kc, :]).then_inc(norms[k]["xT_dve"], 1)

        def xT_ready(pe, k):
            norms[k].wait(pe, "xT_act", 2)
            norms[k].wait(pe, "xT_dve", 2)

        mh_q = cut(RQ, 0, KC, TOK)
        mh_k = cut(RQ, 2048, KC, TOK)
        mh_v = cut(RQ, 4096, B, DM)
        mh_o = mh_q
        mh_p = cut(RR, 0, 2, 2048)
        mh_pT = cut(RR, 4096, 2, 4, 512)[:, :, :, :]
        mh_mx = stat[:, 64:128]
        mh_sm = stat[:, 128:192]
        mh_rs = stat[:, 192:256]

        H1 = Rounds("heads", {"q": KC, "k": KC, "v": B, "scores": 2, "shifted": 2, "exps": 2, "probs": 2, "pT_ps": 8,
                              "pT_act": 4, "pT_dve": 4, "o_ps": 1, "o": KC, "q_ps": KC, "k_ps": KC, "v_ps": B})
        projected = [Rounds("projected", {"rows": NT})]
        for _ in range(3):
            projected.append(projected[-1].again())

        def heads_pe(pe, H, w_out, values_ready, proj):
            H.wait(pe, "q", KC)
            H.wait(pe, "k", KC)
            for g in range(2):
                for pp in range(2):
                    for c in range(KC):
                        for b2 in range(2):
                            tok = (4 * g + 2 * pp + b2) * S
                            for r in range(4):
                                at = (pp * KC + c) * S
                                i = nc.tensor.matmul(ps[64 * b2:64 * b2 + S, 4 * g + r, at:at + S],
                                                     mh_q[32 * r:32 * r + HD, c, tok:tok + S],
                                                     mh_k[32 * r:32 * r + HD, c, tok:tok + S],
                                                     start=True, stop=True)
                i.then_inc(H["scores"], 1)
            for g in range(2):
                H.wait(pe, "probs", g + 1)
                for r in range(4):
                    for n in range(4):
                        i = nc.tensor.transpose(ps[:, 4 * g + r, n * P:(n + 1) * P],
                                                mh_p[:, g, r * 512 + n * P:r * 512 + (n + 1) * P], ident)
                    i.then_inc(H["pT_ps"], 1)
            values_ready()
            for g in range(2):
                H.wait(pe, "pT_act", 2 * g + 2)
                H.wait(pe, "pT_dve", 2 * g + 2)
                for pp in range(2):
                    for b2 in range(2):
                        b = 4 * g + 2 * pp + b2
                        for c in range(KC):
                            u = 64 * (c % 2)
                            for r in range(4):
                                at = (pp * 2 + c // 2) * P + b2 * S
                                h = 4 * c + r
                                i = nc.tensor.matmul(ps[32 * r:32 * r + HD, c, b * S:(b + 1) * S],
                                                     mh_v[u:u + S, b, h * HD:(h + 1) * HD],
                                                     mh_pT[u:u + S, g, r, at:at + S], start=True, stop=True)
            i.then_inc(H["o_ps"], 1)
            H.wait(pe, "o", KC)
            for t in range(NT):
                for kc in range(KC):
                    i = nc.tensor.matmul(ps[:, 4 + t, :], mh_o[:, kc, t * P:(t + 1) * P], w_out[:, kc, :],
                                         start=(kc == 0), stop=(kc == KC - 1))
                i.then_inc(proj["rows"], 1)

        def heads_dve(dve, link, H, masked):
            def group(g):
                return (mh_p[:, g, :].rearrange("p (n k) -> p n k", k=S),
                        ps[:, 4 * g:4 * g + 4, :].rearrange("p r (n k) -> p (r n) k", k=S),
                        [a[:, 32 * g:32 * g + 32] for a in (mh_mx, mh_sm, mh_rs)])
            for g in range(2):
                probs, scores, (mx, _, _) = group(g)
                H.wait(dve, "scores", g + 1)
                if masked:
                    link(nc.vector.tensor_tensor(probs, scores, causal.unsqueeze(1).broadcast_to([P, 32, S]), ALU.add))
                    scores = probs
                link(nc.vector.tensor_reduce(mx, scores, AX, ALU.max))
                nc.vector.tensor_tensor(probs, scores, mx.unsqueeze(2).broadcast_to([P, 32, S]),
                                        ALU.subtract).then_inc(H["shifted"], 1)
            for g in range(2):
                probs, _, (_, sm, rs) = group(g)
                H.wait(dve, "exps", g + 1)
                link(nc.vector.tensor_reduce(sm, probs, AX, ALU.add))
                link(nc.vector.reciprocal(rs, sm))
                nc.vector.tensor_tensor(probs, probs, rs.unsqueeze(2).broadcast_to([P, 32, S]),
                                        ALU.mult).then_inc(H["probs"], 1)
            for g in range(2):
                for r in (1, 3):
                    H.wait(dve, "pT_ps", 4 * g + r + 1)
                    nc.vector.tensor_copy(mh_pT[:, g, r, :], ps[:, 4 * g + r, :]).then_inc(H["pT_dve"], 1)

        def heads_act(act, H, bias):
            for g in range(2):
                H.wait(act, "shifted", g + 1)
                nc.scalar.activation(mh_p[:, g, :], mh_p[:, g, :], ACT.Exp, scale=HD ** -0.5).then_inc(H["exps"], 1)
            for g in range(2):
                for r in (0, 2):
                    H.wait(act, "pT_ps", 4 * g + r + 1)
                    nc.scalar.copy(mh_pT[:, g, r, :], ps[:, 4 * g + r, :]).then_inc(H["pT_act"], 1)
            H.wait(act, "o_ps", 1)
            for c in range(KC):
                if bias is None:
                    i = nc.scalar.copy(mh_o[:, c, :], ps[:, c, :])
                else:
                    i = nc.scalar.activation(mh_o[:, c, :], ps[:, c, :], ACT.Identity, bias=bias[:, c:c + 1])
                i.then_inc(H["o"], 1)

        x_loaded = sem("x_loaded")
        cst_loaded = sem("cst_loaded")
        c64_loaded = sem("c64_loaded")
        w1_loaded = sem("w1_loaded")
        w1q_loaded = sem("w1q_loaded")
        w1o_loaded = sem("w1o_loaded")
        out_stored = sem("out_stored")
        x_final = sem("x_final")

        w1q = cut(RC, 0, KC, DM)
        w1kv = cut(RC, 2048, 2 * DM)
        w1o = cut(RC, 3072, KC, DM)
        c64 = cut(RR, 0, B, P)
        c64T = cut(RR, 1024, B, P)
        c64T_ps, c64T_ready = sem("c64T_ps"), sem("c64T_ready")

        def s1_pe(pe):
            pe.wait_ge(cst_loaded, 16)
            pe.wait_ge(c64_loaded, 32)
            for b in range(B):
                i = nc.tensor.transpose(ps[:, 4 + b // 4, (b % 4) * P:(b % 4 + 1) * P], c64[:, b, :], ident)
                if b % 4 == 3:
                    i.then_inc(c64T_ps, 1)
            pe.wait_ge(c64T_ready, 2)
            pe.wait_ge(w1_loaded, 16)
            for c in range(KC):
                nc.tensor.matmul(ps[:, c, :], w1kv[:, c * P:(c + 1) * P], c64T[:, :, 0:S],
                                 start=True, stop=True).then_inc(H1["k_ps"], 1)
            for b in range(B):
                if b >= 4:
                    H1.wait(pe, "k", b - 3)
                nc.tensor.matmul(ps[:, (4 + b) % 8, :], c64T[:, b, :], w1kv[:, DM:2 * DM],
                                 start=True, stop=True).then_inc(H1["v_ps"], 1)
            H1.wait(pe, "v", B)
            xT_pe(pe, 0)
            xT_ready(pe, 0)
            pe.wait_ge(w1q_loaded, 16)
            for c in range(KC):
                for kc in range(KC):
                    i = nc.tensor.matmul(ps[:, 4 + c, :], w1q[:, kc, c * P:(c + 1) * P], xT[:, kc, :],
                                         start=(kc == 0), stop=(kc == KC - 1))
                i.then_inc(H1["q_ps"], 1)
            pe.wait_ge(w1o_loaded, 16)
            heads_pe(pe, H1, w1o, lambda: H1.wait(pe, "v", B), projected[0])

        def s1_act(act):
            for g in range(2):
                act.wait_ge(c64T_ps, g + 1)
                nc.scalar.copy(c64T[:, 4 * g:4 * g + 4, :], ps[:, 4 + g, :].rearrange("p (b n) -> p b n", b=4)).then_inc(c64T_ready, 1)
            for b in range(B):
                H1.wait(act, "v_ps", b + 1)
                nc.scalar.copy(mh_v[:, b, :], ps[:, (4 + b) % 8, :]).then_inc(H1["v"], 1)
            xT_act(act, 0)
            for c in range(KC):
                H1.wait(act, "q_ps", c + 1)
                nc.scalar.copy(mh_q[:, c, :], ps[:, 4 + c, :]).then_inc(H1["q"], 1)
            heads_act(act, H1, None)

        def s1_dve(dve, link):
            link(nc.vector.memset(power, -0.5))
            dve.wait_ge(x_loaded, 16)
            norm_dve(dve, link, 0)
            for c in range(KC):
                H1.wait(dve, "k_ps", c + 1)
                nc.vector.tensor_copy(mh_k[:, c, :], ps[:, c, :]).then_inc(H1["k"], 1)
            xT_dve(dve, 0)
            heads_dve(dve, link, H1, True)
            for t in range(NT):
                projected[0].wait(dve, "rows", t + 1)
                link(nc.vector.tensor_tensor(x[:, t, :], x[:, t, :], ps[:, 4 + t, :], ALU.add))

        w2q = cut(RA, 0, KC, 2048)
        w2o = cut(RB, 0, NH, DM)
        w2kv = cut(RG, 0, 2, KC, P)
        q2 = cut(RQ, 0, B, NH * S)
        o2 = cut(RQ, 0, NH, TOK)
        k2 = cut(RC, 0, TOK)
        v2 = cut(RC, 512, B, P)
        p2 = cut(RR, 0, B, 512)
        p2T = cut(RR, 4096, B, 512)
        b2q, b2k, b2v = vecs[:, 0:16], vecs[:, 16:17], vecs[:, 17:18]
        mx2, sm2, rs2 = (stat[:, 256 + 64 * i:320 + 64 * i] for i in range(3))
        w2_loaded = sem("w2_loaded")
        w2q_loaded = sem("w2q_loaded")
        w2o_loaded = sem("w2o_loaded")
        x_biased, k2_ps, k2_ready, v2_ps, v2_ready = (sem(n) for n in ("x_biased", "k2_ps", "k2_ready", "v2_ps", "v2_ready"))
        v2_swapped = sem("v2_swapped")
        q2_ps, q2_act, q2_dve = sem("q2_ps"), sem("q2_act"), sem("q2_dve")
        scores2, shifted2, exps2, probs2 = (sem(n) for n in ("scores2", "shifted2", "exps2", "probs2"))
        pT2_ps, pT2, o2_ps, o2_act, o2_dve = (sem(n) for n in ("pT2_ps", "pT2", "o2_ps", "o2_act", "o2_dve"))

        def by_batch(v):
            return v.rearrange("p (b s) -> p b s", s=S)

        def q2_bank(n):
            return (7 + n) % 8

        def s2_pe(pe):
            xT_pe(pe, 1)
            xT_ready(pe, 1)
            pe.wait_ge(w2_loaded, 48)
            for kc in range(KC):
                i = nc.tensor.matmul(ps[:, 4, :], w2kv[:, 0, kc, :], xT[:, kc, :], start=(kc == 0), stop=(kc == KC - 1))
            i.then_inc(k2_ps, 1)
            for t in range(NT):
                for kc in range(KC):
                    i = nc.tensor.matmul(ps[:, 5, t * P:(t + 1) * P], xT[:, kc, t * P:(t + 1) * P], w2kv[:, 1, kc, :],
                                         start=(kc == 0), stop=(kc == KC - 1))
            i.then_inc(v2_ps, 1)
            pe.wait_ge(w2q_loaded, 16)
            for h in range(NH):
                if h == 5:
                    pe.wait_ge(k2_ready, 1)
                if h == 6:
                    pe.wait_ge(v2_ready, 2)
                if h >= 8:
                    pe.wait_ge(q2_act if h % 2 == 0 else q2_dve, (h - 8) // 2 + 1)
                for kc in range(KC):
                    i = nc.tensor.matmul(ps[:, q2_bank(h), :], w2q[:, kc, h * P:(h + 1) * P], xT[:, kc, :],
                                         start=(kc == 0), stop=(kc == KC - 1))
                i.then_inc(q2_ps, 1)
            pe.wait_ge(q2_act, NH // 2)
            pe.wait_ge(q2_dve, NH // 2)
            for b in range(B):
                for hp in range(NH // 2):
                    i = nc.tensor.matmul(ps[:, b, hp * S:(hp + 1) * S], q2[:, b, hp * P:(hp + 1) * P],
                                         k2[:, b * S:(b + 1) * S], start=True, stop=True)
                i.then_inc(scores2, 1)
            for b in range(B):
                pe.wait_ge(probs2, b + 1)
                for j in range(4):
                    i = nc.tensor.transpose(ps[:, b, j * P:(j + 1) * P], p2[:, b, j * P:(j + 1) * P], ident)
                i.then_inc(pT2_ps, 1)
            pe.wait_ge(pT2, B)
            pe.wait_ge(v2_swapped, 32)
            for b in range(B):
                for e in range(2):
                    n = 2 * b + e
                    if n >= 8:
                        pe.wait_ge(o2_dve if e else o2_act, b - 3)
                    nc.tensor.matmul(ps[:, n % 8, :], v2[64 * e:64 * e + S, b, :], p2T[64 * e:64 * e + S, b, :],
                                     start=True, stop=True).then_inc(o2_ps, 1)
            pe.wait_ge(o2_act, B)
            pe.wait_ge(o2_dve, B)
            pe.wait_ge(w2o_loaded, 16)
            for t in range(NT):
                for h in range(NH):
                    i = nc.tensor.matmul(ps[:, t, :], o2[:, h, t * P:(t + 1) * P], w2o[:, h, :],
                                         start=(h == 0), stop=(h == NH - 1))
                i.then_inc(projected[1]["rows"], 1)

        def o2_rows(b, e):
            return (o2.rearrange("p (j e u) n -> p e j u n", e=2, u=2)[:, e, :, :, b * S:(b + 1) * S],
                    ps[:, (2 * b + e) % 8, :].rearrange("p (j u s) -> p j u s", u=2, s=S))

        def s2_act(act):
            xT_act(act, 1)
            act.wait_ge(k2_ps, 1)
            nc.scalar.activation(k2, ps[:, 4, :], ACT.Identity, bias=b2k).then_inc(k2_ready, 1)
            for h in range(0, NH, 2):
                act.wait_ge(q2_ps, h + 1)
                nc.scalar.activation(q2[:, :, h * S:(h + 1) * S], by_batch(ps[:, q2_bank(h), :]), ACT.Identity, bias=b2q[:, h:h + 1]).then_inc(q2_act, 1)
            for b in range(B):
                act.wait_ge(shifted2, b + 1)
                nc.scalar.activation(p2[:, b, :], p2[:, b, :], ACT.Exp, scale=P ** -0.5).then_inc(exps2, 1)
            for b in range(B):
                act.wait_ge(pT2_ps, b + 1)
                nc.scalar.copy(p2T[:, b, :], ps[:, b, :]).then_inc(pT2, 1)
            for b in range(B):
                act.wait_ge(o2_ps, 2 * b + 1)
                dst, src = o2_rows(b, 0)
                nc.scalar.activation(dst, src, ACT.Identity, bias=b2v).then_inc(o2_act, 1)

        def s2_dve(dve, link):
            norm_dve(dve, link, 1)
            xT_dve(dve, 1)
            dve.wait_ge(v2_ps, 1)
            for u in range(2):
                own = slice(64 * u, 64 * u + S)
                nc.vector.tensor_copy(v2.rearrange("p (t u) d -> p u t d", u=2)[own, u], ps[own, 5, :].rearrange("p (t d) -> p t d", d=P)).then_inc(v2_ready, 1)
            for h in range(1, NH, 2):
                dve.wait_ge(q2_ps, h + 1)
                nc.vector.tensor_scalar(q2[:, :, h * S:(h + 1) * S], by_batch(ps[:, q2_bank(h), :]), b2q[:, h:h + 1], None, ALU.add).then_inc(q2_dve, 1)
            for b in range(B + 1):
                if b < B:
                    dve.wait_ge(scores2, b + 1)
                    mx = mx2[:, 8 * b:8 * b + 8]
                    scores = ps[:, b, :].rearrange("p (n k) -> p n k", k=S)
                    link(nc.vector.tensor_reduce(mx, scores, AX, ALU.max))
                    nc.vector.tensor_tensor(p2[:, b, :].rearrange("p (n k) -> p n k", k=S), scores,
                                            mx.unsqueeze(2).broadcast_to([P, 8, S]), ALU.subtract).then_inc(shifted2, 1)
                if b:
                    dve.wait_ge(exps2, b)
                    probs = p2[:, b - 1, :].rearrange("p (n k) -> p n k", k=S)
                    sm, rs = sm2[:, 8 * b - 8:8 * b], rs2[:, 8 * b - 8:8 * b]
                    link(nc.vector.tensor_reduce(sm, probs, AX, ALU.add))
                    link(nc.vector.reciprocal(rs, sm))
                    nc.vector.tensor_tensor(probs, probs, rs.unsqueeze(2).broadcast_to([P, 8, S]), ALU.mult).then_inc(probs2, 1)
            for b in range(B):
                dve.wait_ge(o2_ps, 2 * b + 2)
                dst, src = o2_rows(b, 1)
                nc.vector.tensor_scalar(dst, src, b2v, None, ALU.add).then_inc(o2_dve, 1)
            dve.wait_ge(x_biased, 1)
            for t in range(NT):
                projected[1].wait(dve, "rows", t + 1)
                link(nc.vector.tensor_tensor(x[:, t, :], x[:, t, :], ps[:, t, :], ALU.add))

        ring = [cut(RE, 0, 6, DM), cut(RE, 3072, 6, DM), cut(RR, 0, 6, DM), cut(RR, 3072, 6, DM)]
        xe = [cut(RR, 6144 + 512 * i, DM) for i in range(2)]
        xeT = [cut(RR, 7168 + 512 * i, KC, P) for i in range(2)]
        hn = cut(RQ, 0, NT, DM)
        w3s = cut(RQ, 2048, 6, DM)
        sg = [cut(RQ, 5120 + 256 * i, FI) for i in range(2)]
        act3 = [cut(RQ, 5632 + 256 * i, FI) for i in range(2)]
        actT = [cut(RQ, 6144 + 256 * i, 2, P) for i in range(2)]
        eo = [cut(RQ, 6656 + 512 * i, DM) for i in range(2)]
        picked = [cut(RR, 512 * i, DM) for i in range(8)]
        onehot = [RG[:, 256 * i:256 * i + 256].bitcast(BF16).rearrange("p (t c) -> p t c", c=P) for i in range(2)]
        logits, pos, mask, place = (cut(RG, 512 + 128 * i, NT, NE) for i in range(4))
        choice = cut(RC, 4096, NT * TOPK, NE)
        choice_pos = cut(RC, 4608, NT * TOPK, NE)
        gate = sb("gate", [P, KC, NE])
        topv = cut(stat, 64, NT, 8)
        topi = cut(stat, 96, NT, 8).bitcast(U32)
        top_e = stat[:, 128:144]
        top_w = stat[:, 144:160]
        w_sum, w_rs = stat[:, 160:164], stat[:, 164:168]
        top_pos = stat[:, 168:184]
        slot = stat[:, 200:216].bitcast(U32)
        sq, rms_in, rms = stat[:, 216:220], stat[:, 220:224], stat[:, 224:228]
        token = stat[:, 228:260].bitcast(U32)
        token_at = [stat[:, 260 + i:261 + i].bitcast(U32) for i in range(2)]
        token_parts = stat[:, 264:268].bitcast(BF16)
        w3s_loaded, row_loaded, gate_loaded = sem("w3s_loaded"), sem("row_loaded"), sem("gate_loaded")
        ring_loaded = [sem(f"ring_loaded{i}") for i in range(4)]
        sq_ready, rms_ready, hn_ready, h_stored = (sem(n) for n in ("sq_ready", "rms_ready", "hn_ready", "h_stored"))
        logits_ps, mask_ready, pos_ps, places_done = (sem(n) for n in ("logits_ps", "mask_ready", "pos_ps", "places_done"))
        top_shifted, top_exp, onehot_ready, onehot_used, token_ready = (
            sem(n) for n in ("top_shifted", "top_exp", "onehot_ready", "onehot_used", "token_ready"))
        xe_loaded = [sem(f"xe_loaded{i}") for i in range(2)]
        xeT_ps, xeT_ready, gu_ps, sg_ready, act_ready, actT_ps, actT_ready, eo_ps, eo_ready = (
            sem(n) for n in ("xeT_ps", "xeT_ready", "gu_ps", "sg_ready", "act_ready", "actT_ps", "actT_ready", "eo_ps", "eo_ready"))
        eo_stored = [sem(f"eo_stored{i}") for i in range(2)]
        picked_loaded = [sem(f"picked_loaded{i}") for i in range(8)]
        picked_used = sem("picked_used")
        SH = NT
        JOBS = SH + NE

        def act_transpose_pe(pe, j, par):
            pe.wait_ge(act_ready, j + 1)
            for f in range(2):
                i = nc.tensor.transpose(ps[:, 4 + par, f * P:(f + 1) * P], act3[par][:, f * P:(f + 1) * P], ident)
            i.then_inc(actT_ps, 1)

        def rows_transpose_pe(pe, e, par):
            pe.wait_ge(xe_loaded[par], e * 8 + 16 - 8 * par)
            for kc in range(KC):
                i = nc.tensor.transpose(ps[:, par, kc * P:(kc + 1) * P], xe[par][:, kc * P:(kc + 1) * P], ident)
            i.then_inc(xeT_ps, 1)

        def down_pe(pe, j, par, w, first=False):
            pe.wait_ge(actT_ready, j + 1)
            if not first:
                pe.wait_ge(eo_ready, j)
            for f in range(2):
                i = nc.tensor.matmul(ps[:, 6, :], actT[par][:, f, :], w[:, 4 + f, :], start=(f == 0), stop=(f == 1))
            i.then_inc(eo_ps, 1)

        def up_pe(pe, par, w, rows):
            for kc in range(KC):
                i = nc.tensor.matmul(ps[:, 2 + par, :], rows(kc), w[:, kc, :], start=(kc == 0), stop=(kc == KC - 1))
            i.then_inc(gu_ps, 1)

        def expert_step_pe(pe, e, u, w_before, last=False):
            j, par = e + SH, u % 2
            act_transpose_pe(pe, j - 1, 1 - par)
            if not last:
                rows_transpose_pe(pe, e + 1, 1 - par)
            down_pe(pe, j - 1, 1 - par, w_before)
            pe.wait_ge(xeT_ready, e + 1)
            pe.wait_ge(ring_loaded[u], e * 4 + 16 - 4 * u)
            up_pe(pe, par, ring[u], lambda kc: xeT[par][:, kc, :])

        def s3_pe(pe):
            xT_pe(pe, 2, hn, hn_ready)
            xT_ready(pe, 2)
            pe.wait_ge(gate_loaded, 16)
            for t in range(NT):
                for kc in range(KC):
                    i = nc.tensor.matmul(ps[:, 7, t * NE:(t + 1) * NE], xT[:, kc, t * P:(t + 1) * P], gate[:, kc, :],
                                         start=(kc == 0), stop=(kc == KC - 1))
            i.then_inc(logits_ps, 1)
            pe.wait_ge(w3s_loaded, 16)

            def shared(j):
                up_pe(pe, j % 2, w3s, lambda kc: xT[:, kc, j * P:(j + 1) * P])
            shared(0)
            pe.wait_ge(mask_ready, 1)
            for t in range(NT):
                for t0 in range(t + 1):
                    i = nc.tensor.matmul(ps[:, 7, t * NE:(t + 1) * NE], before if t0 == t else ones, mask[:, t0, :],
                                         start=(t0 == 0), stop=(t0 == t))
            i.then_inc(pos_ps, 1)
            for j in range(SH):
                if j:
                    act_transpose_pe(pe, j - 1, (j - 1) % 2)
                    down_pe(pe, j - 1, (j - 1) % 2, w3s, first=(j == 1))
                    shared(j)
                for e in range(8 * j, 8 * j + 8):
                    pe.wait_ge(onehot_ready, e + 1)
                    for t in range(NT):
                        i = nc.tensor.matmul(ps[:, 7, 2 * e:2 * e + 2], onehot[e % 2][:, t, :],
                                             token_parts[:, 2 * t:2 * t + 2], start=(t == 0), stop=(t == NT - 1))
                    i.then_inc(onehot_used, 1)
            rows_transpose_pe(pe, 0, 0)
            for e in range(4):
                expert_step_pe(pe, e, e, ring[e - 1] if e else w3s)
            with pe.Fori(0, NE // 4 - 2) as i:
                for u in range(4):
                    expert_step_pe(pe, i * 4 + (4 + u), u, ring[(u - 1) % 4])
            for u in range(4):
                expert_step_pe(pe, NE - 4 + u, u, ring[(u - 1) % 4], last=(u == 3))
            act_transpose_pe(pe, JOBS - 1, 1)
            down_pe(pe, JOBS - 1, 1, ring[3])

        def s3_act(act):
            for t in range(NT):
                norms[2].wait(act, "xn", t + 1)
                nc.scalar.activation(hn[:, t, :], xn[:, t, :], ACT.Square, accum_out=sq[:, t:t + 1]).then_inc(sq_ready, 1)
            xT_act(act, 2)
            act.wait_ge(top_shifted, 1)
            nc.scalar.activation(top_w, top_w, ACT.Exp).then_inc(top_exp, 1)

            def silu(j, par, first=False):
                act.wait_ge(gu_ps, j + 1)
                if not first:
                    act.wait_ge(act_ready, j - 1)
                nc.scalar.activation(sg[par], ps[:, 2 + par, 0:FI], ACT.Silu).then_inc(sg_ready, 1)

            def rows(e, par):
                act.wait_ge(xeT_ps, e + 1)
                nc.scalar.copy(xeT[par].rearrange("p a b -> p (a b)"), ps[:, par, :]).then_inc(xeT_ready, 1)
            for j in range(SH):
                silu(j, j % 2, first=(j < 2))
            rows(0, 0)
            for e in range(4):
                rows(e + 1, 1 - e % 2)
                silu(e + SH, e % 2)
            with act.Fori(0, NE // 4 - 2) as i:
                for u in range(4):
                    rows(i * 4 + (5 + u), 1 - u % 2)
                    silu(i * 4 + (4 + u + SH), u % 2)
            for u in range(4):
                if u < 3:
                    rows(NE - 4 + u + 1, 1 - u % 2)
                silu(NE - 4 + u + SH, u % 2)

        def s3_dve(dve, link):
            norm_dve(dve, link, 2)
            dve.wait_ge(rms_ready, 1)
            dve.wait_ge(row_loaded, 16)
            for t in range(NT):
                nc.vector.scalar_tensor_tensor(hn[:, t, :], xn[:, t, :], rms[:, t:t + 1], row_bias[:], ALU.mult,
                                               ALU.mult).then_inc(hn_ready, 1)
            xT_dve(dve, 2)
            link(nc.vector.tensor_copy(token_parts, cst[:, 4, 64:72]))
            dve.wait_ge(logits_ps, 1)
            link(nc.vector.tensor_copy(logits.rearrange("p t e -> p (t e)"), ps[:, 7, 0:NT * NE]))
            for t in range(NT):
                i = nc.vector.max(topv[:, t, :], logits[:, t, :])
            link(i)
            for t in range(NT):
                i = nc.vector.max_index(topi[:, t, :], topv[:, t, :], logits[:, t, :])
            link(i)
            nc.vector.tensor_tensor(top_w.rearrange("p (t k) -> p t k", k=TOPK), topv[:, :, 0:TOPK],
                                    topv[:, :, 0:1].broadcast_to([P, NT, TOPK]), ALU.subtract).then_inc(top_shifted, 1)
            link(nc.vector.tensor_copy(top_e.rearrange("p (t k) -> p t k", k=TOPK), topi[:, :, 0:TOPK]))
            link(nc.vector.tensor_tensor(choice, iota[:, 0:NE].unsqueeze(1).broadcast_to([P, NT * TOPK, NE]),
                                         top_e.unsqueeze(2).broadcast_to([P, NT * TOPK, NE]), ALU.is_equal))
            nc.vector.tensor_reduce(mask, choice.rearrange("p (t k) e -> p t e k", k=TOPK), AX, ALU.add).then_inc(mask_ready, 1)
            dve.wait_ge(top_exp, 1)
            link(nc.vector.tensor_reduce(w_sum, top_w.rearrange("p (t k) -> p t k", k=TOPK), AX, ALU.add))
            link(nc.vector.reciprocal(w_rs, w_sum))
            link(nc.vector.tensor_tensor(top_w.rearrange("p (t k) -> p t k", k=TOPK),
                                         top_w.rearrange("p (t k) -> p t k", k=TOPK),
                                         w_rs.unsqueeze(2).broadcast_to([P, NT, TOPK]), ALU.mult))
            dve.wait_ge(pos_ps, 1)
            link(nc.vector.tensor_copy(pos.rearrange("p t e -> p (t e)"), ps[:, 7, 0:NT * NE]))
            link(nc.vector.scalar_tensor_tensor(place, pos, 1.0, mask, ALU.add, ALU.mult))
            link(nc.vector.tensor_scalar(place, place, -1.0, None, ALU.add))
            link(nc.vector.tensor_tensor(choice_pos.rearrange("p (t k) e -> p t k e", k=TOPK),
                                         choice.rearrange("p (t k) e -> p t k e", k=TOPK),
                                         pos.unsqueeze(2).broadcast_to([P, NT, TOPK, NE]), ALU.mult))
            link(nc.vector.tensor_reduce(top_pos, choice_pos, AX, ALU.add))
            link(nc.vector.tensor_scalar(top_pos, top_pos, float(CAP - 1), None, ALU.min))
            link(nc.vector.scalar_tensor_tensor(slot, top_e, float(CAP), top_pos, ALU.mult, ALU.add))

            def gated(j, par):
                dve.wait_ge(sg_ready, j + 1)
                nc.vector.tensor_tensor(act3[par], sg[par], ps[:, 2 + par, FI:2 * FI], ALU.mult).then_inc(act_ready, 1)

            def turned(j, par):
                dve.wait_ge(actT_ps, j + 1)
                nc.vector.tensor_copy(actT[par].rearrange("p a b -> p (a b)"), ps[:, 4 + par, 0:2 * P]).then_inc(actT_ready, 1)

            def shared_out(j):
                dve.wait_ge(eo_ps, j + 1)
                if j == 0:
                    dve.wait_ge(x_biased, 2)
                nc.vector.tensor_tensor(x[:, j, :], x[:, j, :], ps[:, 6, :], ALU.add).then_inc(eo_ready, 1)

            def routed_out(e, par, first=False):
                dve.wait_ge(eo_ps, e + (SH + 1))
                if not first:
                    dve.wait_ge(eo_stored[par], e * 8 - 8 * par)
                nc.vector.tensor_copy(eo[par], ps[:, 6, :]).then_inc(eo_ready, 1)

            for j in range(SH):
                gated(j, j % 2)
                for e in range(8 * j, 8 * j + 8):
                    if e >= 2:
                        dve.wait_ge(onehot_used, e - 1)
                    nc.vector.tensor_tensor(onehot[e % 2], iota.unsqueeze(1).broadcast_to([P, NT, P]),
                                            place[:, :, e].unsqueeze(2).broadcast_to([P, NT, P]),
                                            ALU.is_equal).then_inc(onehot_ready, 1)
                if j < SH - 1:
                    turned(j, j % 2)
                    shared_out(j)
            dve.wait_ge(onehot_used, NE)
            token_ps = ps[:, 7, 0:2 * NE].rearrange("p (e a) -> p e a", a=2)
            token_low = stat[:, 300:332]
            link(nc.vector.tensor_copy(token_low, token_ps[:, :, 0]))
            nc.vector.tensor_tensor(token, token_low, token_ps[:, :, 1], ALU.add).then_inc(token_ready, 1)
            turned(SH - 1, 1)
            shared_out(SH - 1)
            for e in range(4):
                gated(e + SH, e % 2)
                turned(e + SH, e % 2)
                routed_out(e, e % 2, first=(e < 2))
            with dve.Fori(0, NE // 4 - 1) as i:
                for u in range(4):
                    gated(i * 4 + (4 + u + SH), u % 2)
                    turned(i * 4 + (4 + u + SH), u % 2)
                    routed_out(i * 4 + (4 + u), u % 2)
            for n in range(NT * TOPK):
                k, t = n // NT, n % NT
                c = t * TOPK + k
                dve.wait_ge(picked_loaded[n % 8], 16 * (n // 8 + 1))
                if n >= NT:
                    dve.wait_ge(picked_used, n - NT + 1)
                nc.vector.scalar_tensor_tensor(x[:, t, :], picked[n % 8], top_w[:, c:c + 1], x[:, t, :], ALU.mult,
                                               ALU.add).then_inc(picked_used, 1)
            dve.wait_ge(picked_used, NT * TOPK)

        def s3_pool(pool, link):
            norm_pool(pool, link, 2)
            pool.wait_ge(sq_ready, NT)
            link(nc.gpsimd.tensor_scalar(rms_in, sq, 1.0 / DM, 1e-6, ALU.mult, ALU.add))
            nc.gpsimd.tensor_tensor(rms, rms_in, power, ALU.pow).then_inc(rms_ready, 1)
            nc.gpsimd.tensor_tensor(x[:], x[:], xn[:], ALU.add).then_inc(x_biased, 1)
            pool.wait_ge(token_ready, 1)
            pool.wait_ge(h_stored, 16)

            def gather(e, par, first=False):
                if not first:
                    pool.wait_ge(xeT_ps, e - 1)
                    pool.wait_ge(xe_loaded[par], e * 8 - 8 * par)
                col = token[:, e:e + 1] if type(e) is int else token[:, bass.ds(e, 1)]
                link(nc.gpsimd.tensor_copy(token_at[par], col))
                nc.gpsimd.tensor_tensor(stat[:, 262:263], power[:, 0:1], power[:, 0:1], ALU.add)
                nc.gpsimd.indirect_dma_start(xe[par], None, scratch["h_rows"],
                                             bass.IndirectOffsetOnAxis(token_at[par], 0)).then_inc(xe_loaded[par], 16)
            for e in range(4):
                gather(e, e % 2, first=(e < 2))
            steps = NE // 4 - 1
            n0 = link.n
            with pool.Fori(0, steps) as i:
                link.base = i * 4
                for u in range(4):
                    gather(i * 4 + (4 + u), u % 2)
            link.n, link.base = n0 + 4 * steps, 0
            for par in range(2):
                pool.wait_ge(eo_stored[par], 16 * NE // 2)
            for n in range(NT * TOPK):
                k, t = n // NT, n % NT
                c = t * TOPK + k
                if n >= 8:
                    pool.wait_ge(picked_used, n - 7)
                nc.gpsimd.indirect_dma_start(picked[n % 8], None, scratch["eo_rows"],
                                             bass.IndirectOffsetOnAxis(slot[:, c:c + 1], 0)).then_inc(picked_loaded[n % 8], 16)

        def s3_loads_early(sp):
            for e in range(2):
                sp.dma_start(ring[e], T["w3"][e]).then_inc(ring_loaded[e], 16)

        def s3_sp(sp):
            sp.wait_ge(x_biased, 1)
            sp.dma_start(row_bias[:], T["norm3"].unsqueeze(0).broadcast_to([P, DM])).then_inc(row_loaded, 16)
            projected[1].wait(sp, "rows", NT)
            sp.dma_start(w3s, T["w3s"]).then_inc(w3s_loaded, 16)
            for e in range(2, 4):
                sp.dma_start(ring[e], T["w3"][e]).then_inc(ring_loaded[e], 16)
            sp.wait_ge(hn_ready, NT)
            sp.dma_start(scratch["h_rows"].rearrange("(t p) h -> p t h", p=P), hn).then_inc(h_stored, 16)
            with sp.Fori(0, NE // 4 - 1) as i:
                for u in range(4):
                    e = i * 4 + u
                    sp.wait_ge(eo_ps, e + (SH + 1))
                    sp.dma_start(ring[u], T["w3"][bass.ds(e + 4, 1)].rearrange("a p c n -> p (a c) n")).then_inc(ring_loaded[u], 16)
                    sp.wait_ge(eo_ready, e + (SH + 1))
                    sp.dma_start(scratch["eo_rows"][bass.ds(e * CAP, CAP), :], eo[u % 2]).then_inc(eo_stored[u % 2], 16)
            if STAGES >= 4:
                s4_sp(sp)
            for e in range(NE - 4, NE):
                sp.wait_ge(eo_ready, e + SH + 1)
                sp.dma_start(scratch["eo_rows"][e * CAP:(e + 1) * CAP, :], eo[e % 2]).then_inc(eo_stored[e % 2], 16)

        w4q = cut(RA, 0, KC, 2048)
        w4kq = cut(RB, 0, NH, 4 * P)
        w4qr = cut(RC, 0, NH // 2, 3 * P)
        w4kr = cut(RC, 3072, NH // 2, P)
        w_abs = [cut(RC, 4096 + 384 * i, 3, P) for i in range(2)]
        q_hk = [cut(RR, 512 * i, TOK) for i in range(2)]
        by_cos = cut(RR, 1024, 3, TOK)
        by_sin = cut(RR, 2560, 3, TOK)
        q_rot = [cut(RR, 4096 + 1536 * i, 3, TOK) for i in range(2)]
        cos_q = cut(RR, 7168, 3, S)
        sin_q = cut(RR, 7360, 3, S)
        q4 = cut(RQ, 0, B, NH * S)
        w4q_loaded, w4kq_loaded, w4r_loaded, rope_q_loaded, rope_k_loaded, w4o_loaded = (
            sem(n) for n in ("w4q_loaded", "w4kq_loaded", "w4r_loaded", "rope_q_loaded", "rope_k_loaded", "w4o_loaded"))
        qhk_ps, qhk_ready, wabs_ps, wabs_ready, qbig_ps, rope_taken, qrot_ready, qabs_ps, qabs_ready = (
            sem(n) for n in ("qhk_ps", "qhk_ready", "wabs_ps", "wabs_ready", "qbig_ps", "rope_taken", "qrot_ready", "qabs_ps", "qabs_ready"))

        def heads4_pe(pe):
            def q_head(h):
                for kc in range(KC):
                    i = nc.tensor.matmul(ps[:, h % 2, :], w4q[:, kc, h * P:(h + 1) * P], xT[:, kc, :],
                                         start=(kc == 0), stop=(kc == KC - 1))
                i.then_inc(qhk_ps, 1)

            def w_product(h):
                if h:
                    pe.wait_ge(wabs_ready, h)
                half = slice(64 * (h // 8), 64 * (h // 8) + R)
                for c in range(3):
                    i = nc.tensor.matmul(ps[:, 2, c * P:(c + 1) * P], w4qr[half, h % 8, c * P:(c + 1) * P],
                                         w4kr[half, h % 8, :], start=True, stop=True)
                i.then_inc(wabs_ps, 1)

            def q_big(h):
                pe.wait_ge(qhk_ready, h + 1)
                if h:
                    pe.wait_ge(rope_taken, h)
                for c in range(4):
                    i = nc.tensor.matmul(ps[:, 4 + c, :], w4kq[:, h, c * P:(c + 1) * P], q_hk[h % 2], start=True, stop=True)
                i.then_inc(qbig_ps, 1)

            def q_abs(h):
                pe.wait_ge(qrot_ready, h + 1)
                pe.wait_ge(wabs_ready, h + 1)
                if h:
                    pe.wait_ge(qabs_ready, h)
                for c in range(3):
                    i = nc.tensor.matmul(ps[:, 3, :], w_abs[h % 2][:, c, :], q_rot[h % 2][:, c, :], start=(c == 0), stop=(c == 2))
                i.then_inc(qabs_ps, 1)
            xT_pe(pe, 3)
            xT_ready(pe, 3)
            pe.wait_ge(w4q_loaded, 16)
            q_head(0)
            pe.wait_ge(w4r_loaded, 32)
            w_product(0)
            pe.wait_ge(w4kq_loaded, 16)
            for h in range(NH):
                if h + 1 < NH:
                    q_head(h + 1)
                    w_product(h + 1)
                q_big(h)
                if h:
                    q_abs(h - 1)
            q_abs(NH - 1)

        def heads4_act(act):
            xT_act(act, 3)

            def q_out(h):
                act.wait_ge(qabs_ps, h + 1)
                nc.scalar.copy(q4[:, :, h * S:(h + 1) * S], by_batch(ps[:, 3, :])).then_inc(qabs_ready, 1)
            for h in range(NH):
                act.wait_ge(qhk_ps, h + 1)
                if h >= 2:
                    act.wait_ge(qbig_ps, h - 1)
                nc.scalar.copy(q_hk[h % 2], ps[:, h % 2, :]).then_inc(qhk_ready, 1)
                act.wait_ge(wabs_ps, h + 1)
                if h >= 2:
                    q_out(h - 2)
                nc.scalar.copy(w_abs[h % 2].rearrange("p c d -> p (c d)"), ps[:, 2, 0:3 * P]).then_inc(wabs_ready, 1)
                for n in range(3 * h, 3 * h + 3):
                    magnitude_act(act, n)
            q_out(NH - 2)
            q_out(NH - 1)

        def heads4_dve(dve, link):
            norm_dve(dve, link, 3)
            xT_dve(dve, 3)
            dve.wait_ge(rope_q_loaded, 16)
            all_batches = [P, 3, B, S]
            for h in range(NH):
                dve.wait_ge(qbig_ps, h + 1)
                if h:
                    dve.wait_ge(qrot_ready, h)
                nc.vector.tensor_tensor(by_cos.rearrange("p c (b s) -> p c b s", s=S),
                                        ps[:, 4:7, :].rearrange("p c (b s) -> p c b s", s=S),
                                        cos_q.unsqueeze(2).broadcast_to(all_batches), ALU.mult)
                for c, partner in ((0, 1), (1, 0), (2, 3)):
                    i = nc.vector.tensor_tensor(by_batch(by_sin[:, c, :]), by_batch(ps[:, 4 + partner, :]),
                                                sin_q[:, c, :].unsqueeze(1).broadcast_to([P, B, S]), ALU.mult)
                i.then_inc(rope_taken, 1)
                dve.wait_ge(rope_taken, h + 1)
                if h >= 2:
                    dve.wait_ge(qabs_ps, h - 1)
                nc.vector.tensor_tensor(q_rot[h % 2], by_cos, by_sin, ALU.add).then_inc(qrot_ready, 1)

        LO = [0, 124] + [248 + 123 * j for j in range(LT - 2)]
        LW = [LFULL + (j < LREST) for j in range(LT)]
        GROUPS = [range(0, 2), range(2, 6), range(6, 10), range(10, 13)]
        BANKS = [(c, min(512, LCTX - 512 * c)) for c in range(4)]
        keys = [RA[:, LCTX * i:LCTX * (i + 1)] for i in range(2)]
        p4 = [RA[:, 3202 + LCTX * i:3202 + LCTX * (i + 1)] for i in range(2)]
        q_now = [cut(RA, 6404, NH * S), cut(RG, 0, NH * S)]
        w4kv = cut(RC, 0, NH, P)
        p4T = [cut(RC, 2048 + 512 * g, 4, P) for g in range(4)]
        o_rows = [cut(RC, 4096 + P * i, P) for i in range(2)]
        vals = [cut(RE, 1664 * i, LT, DC) for i in range(2)]
        cos_k = cut(RE, 3328, LT, DC)
        turned_half = cut(RE, 4992, 7, DC)
        sin_k = xn[:].rearrange("p a b -> p (a b)")[:, 0:LT * DC].rearrange("p (j d) -> p j d", d=DC)
        o4 = cut(RR, 0, NH, TOK)
        l4 = cut(RQ, 0, NH, TOK)
        w4o = cut(RB, 0, NH, DM)
        mx4 = cut(stat, 340, 4)
        neg_mx = stat[:, 344:346]
        row_sum = stat[:, 346:348]
        row_rs = stat[:, 348:350]
        ctx_loaded = [sem(f"ctx_loaded{i}") for i in range(2)]
        vals_ready, q_now_ready, keys_ps, keys_ready, scores4, neg_mx_ready, exps4 = (
            sem(n) for n in ("vals_ready", "q_now_ready", "keys_ps", "keys_ready", "scores4", "neg_mx_ready", "exps4"))
        p4T_ps, p4T_act, p4T_dve, o_rows_ps, o_rows_ready, o4_ps, o4_ready = (
            sem(n) for n in ("p4T_ps", "p4T_act", "p4T_dve", "o_rows_ps", "o_rows_ready", "o4_ps", "o4_ready"))
        l4_ps, l4_act, l4_dve = (sem(n) for n in ("l4_ps", "l4_act", "l4_dve"))
        HP = NH // 2

        def keys_pe(pe, b, u, g, first=False):
            if g == 0:
                pe.wait_ge(vals_ready, b + 1)
            if not (first and g == 0):
                pe.wait_ge(keys_ready, b * 4 + g)
            for n, j in enumerate(GROUPS[g]):
                i = nc.tensor.transpose(ps[:, 7, n * P:n * P + LW[j]], vals[u][0:LW[j], j, :], ident[0:LW[j], 0:LW[j]])
            i.then_inc(keys_ps, 1)

        def keys_act(act, b, u, g):
            act.wait_ge(keys_ps, b * 4 + (g + 1))
            w, js = LW[GROUPS[g][0]], GROUPS[g]
            dst = keys[u][:, LO[js[0]]:LO[js[0]] + w * len(js)].rearrange("p (j w) -> p j w", w=w)
            nc.scalar.copy(dst, ps[:, 7, 0:P * len(js)].rearrange("p (j w) -> p j w", w=P)[:, :, 0:w]).then_inc(keys_ready, 1)

        def turn_out_pe(pe, n, par):
            pe.wait_ge(o_rows_ready, n + 1)
            nc.tensor.transpose(ps[:, 6, P:2 * P], o_rows[par], ident).then_inc(o4_ps, 1)

        def attend_pe(pe, n, u, par):
            def turn(g):
                if g >= 2:
                    pe.wait_ge(p4T_act, n * 2 + (g - 1))
                for k, j in enumerate(GROUPS[g]):
                    i = nc.tensor.transpose(ps[0:LW[j], 4 + g % 2, k * P:(k + 1) * P], p4[par][:, LO[j]:LO[j] + LW[j]], ident)
                i.then_inc(p4T_ps, 1)

            def values(g):
                if g < 2:
                    pe.wait_ge(p4T_act, n * 2 + (g + 1))
                else:
                    pe.wait_ge(p4T_dve, n * 2 + (g - 1))
                for k, j in enumerate(GROUPS[g]):
                    i = nc.tensor.matmul(ps[:, 6, 0:P], p4T[g][0:LW[j], k, :], vals[u][0:LW[j], j, :],
                                         start=(j == 0), stop=(j == LT - 1))
                if g == 3:
                    i.then_inc(o_rows_ps, 1)
            turn(0)
            turn(1)
            values(0)
            turn(2)
            values(1)
            turn(3)
            values(2)
            values(3)

        def tile_pe(pe, b, u, hp, back=2, more=True):
            n, par = b * HP + hp, hp % 2
            if hp == 0:
                pe.wait_ge(keys_ready, b * 4 + 4)
                pe.wait_ge(q_now_ready, b + 1)
            if back >= 1:
                pe.wait_ge(exps4, n)
            for c, w in BANKS:
                nc.tensor.matmul(ps[:, c, 0:w], q_now[u][:, hp * P:(hp + 1) * P], keys[u][:, 512 * c:512 * c + w],
                                 start=True, stop=True).then_inc(scores4, 1)
                if c == 1 and back >= 2:
                    turn_out_pe(pe, n - 2, par)
            if back >= 2:
                pe.wait_ge(o4_ready, n - 1)
            if back >= 1:
                attend_pe(pe, n - 1, u if hp else 1 - u, 1 - par)
            if more and 3 <= hp <= 6:
                keys_pe(pe, b + 1, 1 - u, hp - 3)

        def tile_act(act, b, u, hp, back=2, more=True):
            n, par = b * HP + hp, hp % 2
            if more and hp >= 4:
                keys_act(act, b + 1, 1 - u, hp - 4)
            if back >= 1:
                turned_act(act, n - 1)
            act.wait_ge(neg_mx_ready, n + 1)
            nc.scalar.activation(p4[par], ps[:, 0:4, :].rearrange("p a b -> p (a b)")[:, 0:LCTX], ACT.Exp,
                                 bias=neg_mx[:, par:par + 1], accum_out=row_sum[:, par:par + 1]).then_inc(exps4, 1)

        def turned_act(act, n):
            for g in range(2):
                act.wait_ge(p4T_ps, n * 4 + (g + 1))
                w, k = LW[GROUPS[g][0]], len(GROUPS[g])
                nc.scalar.copy(p4T[g][0:w, 0:k, :], ps[0:w, 4 + g % 2, 0:k * P].rearrange("p (k q) -> p k q", q=P)).then_inc(p4T_act, 1)

        def turned_dve(dve, n):
            for g in range(2, 4):
                dve.wait_ge(p4T_ps, n * 4 + (g + 1))
                w, k = LW[GROUPS[g][0]], len(GROUPS[g])
                nc.vector.tensor_copy(p4T[g][0:w, 0:k, :], ps[0:w, 4 + g % 2, 0:k * P].rearrange("p (k q) -> p k q", q=P)).then_inc(p4T_dve, 1)

        def rows_out_dve(dve, link, n, par):
            dve.wait_ge(exps4, n + 1)
            link(nc.vector.reciprocal(row_rs[:, par:par + 1], row_sum[:, par:par + 1]))
            dve.wait_ge(o_rows_ps, n + 1)
            nc.vector.tensor_scalar(o_rows[par], ps[:, 6, 0:P], row_rs[:, par:par + 1], None, ALU.mult).then_inc(o_rows_ready, 1)

        def head_out_dve(dve, b, hp):
            dve.wait_ge(o4_ps, b * HP + (hp + 1))
            tok = bass.ds(b * S, S)
            nc.vector.tensor_scalar(o4[:, 2 * hp:2 * hp + 2, tok], ps[:, 6, P:2 * P].rearrange("p (u s) -> p u s", s=S), 1.0,
                                    None, ALU.mult).then_inc(o4_ready, 1)

        def tile_dve(dve, link, b, u, hp, back=2):
            n, par = b * HP + hp, hp % 2
            if back >= 2:
                rows_out_dve(dve, link, n - 2, par)
            for c, w in BANKS:
                dve.wait_ge(scores4, n * 4 + (c + 1))
                i = nc.vector.tensor_reduce(mx4[:, c:c + 1], ps[:, c, 0:w], AX, ALU.max)
                if c == 1 and back >= 2:
                    head_out_dve(dve, b if hp >= 2 else b - 1, (hp - 2) % HP)
            link(i)
            nc.vector.tensor_reduce(neg_mx[:, par:par + 1], mx4, AX, ALU.max, negate=True).then_inc(neg_mx_ready, 1)
            if back >= 1:
                turned_dve(dve, n - 1)

        def all_tiles(eng, tile, links=None):
            for u in range(2):
                for hp in range(HP):
                    tile(u, u, hp, back=min(2, u * HP + hp))
            n0 = links.n if links else 0
            per = 16 * 2
            with eng.Fori(0, B // 2 - 2) as i:
                if links:
                    links.base = i * per
                for u in range(2):
                    for hp in range(HP):
                        tile(i * 2 + (2 + u), u, hp)
            if links:
                assert links.n == n0 + per
                links.n, links.base = n0 + per * (B // 2 - 2), 0
            for u in range(2):
                for hp in range(HP):
                    tile(B - 2 + u, u, hp, **({"more": False} if u and not links else {}))

        def s4_pe(pe):
            heads4_pe(pe)
            pe.wait_ge(qabs_ready, NH)
            weight_scales_pe(pe)
            for g in range(4):
                keys_pe(pe, 0, 0, g, first=True)
            all_tiles(pe, lambda b, u, hp, **kw: tile_pe(pe, b, u, hp, **kw))
            n = B * HP
            turn_out_pe(pe, n - 2, 0)
            pe.wait_ge(exps4, n)
            pe.wait_ge(o4_ready, n - 1)
            attend_pe(pe, n - 1, 1, 1)
            turn_out_pe(pe, n - 1, 1)
            pe.wait_ge(o4_ready, n)
            pe.wait_ge(w4o_loaded, 32)
            for h in range(NH):
                if h >= 8:
                    pe.wait_ge(l4_dve if h % 2 else l4_act, (h - 8) // 2 + 1)
                nc.tensor.matmul(ps[:, h % 8, :], w4kv[:, h, :], o4[:, h, :], start=True, stop=True).then_inc(l4_ps, 1)
            pe.wait_ge(l4_act, NH // 2)
            pe.wait_ge(l4_dve, NH // 2)
            for t in range(NT):
                for h in range(NH):
                    i = nc.tensor.matmul(ps[:, t, :], l4[:, h, t * P:(t + 1) * P], w4o[:, h, :],
                                         start=(h == 0), stop=(h == NH - 1))
                i.then_inc(projected[2]["rows"], 1)

        def s4_act(act):
            heads4_act(act)
            for g in range(4):
                keys_act(act, 0, 0, g)
            all_tiles(act, lambda b, u, hp, **kw: tile_act(act, b, u, hp, **kw))
            turned_act(act, B * HP - 1)
            for h in range(0, NH, 2):
                act.wait_ge(l4_ps, h + 1)
                nc.scalar.copy(l4[:, h, :], ps[:, h % 8, :]).then_inc(l4_act, 1)

        def s4_dve(dve, link):
            heads4_dve(dve, link)
            weight_scales_dve(dve, link)
            all_tiles(dve, lambda b, u, hp, **kw: tile_dve(dve, link, b, u, hp, **kw), link)
            n = B * HP
            rows_out_dve(dve, link, n - 2, 0)
            head_out_dve(dve, B - 1, HP - 2)
            turned_dve(dve, n - 1)
            rows_out_dve(dve, link, n - 1, 1)
            head_out_dve(dve, B - 1, HP - 1)
            for h in range(1, NH, 2):
                dve.wait_ge(l4_ps, h + 1)
                nc.vector.tensor_copy(l4[:, h, :], ps[:, h % 8, :]).then_inc(l4_dve, 1)
            for t in range(NT):
                projected[2].wait(dve, "rows", t + 1)
                link(nc.vector.tensor_tensor(x[:, t, :], x[:, t, :], ps[:, t, :], ALU.add))

        def s4_pool(pool, link):
            norm_pool(pool, link, 3)
            pool.wait_ge(rope_k_loaded, 32)
            rows = LFULL + 1

            def batch(b, u, back=2):
                pool.wait_ge(ctx_loaded[u], b * 16 + 32 - 16 * u)
                v = vals[u]
                for j0, j1 in ((0, 7), (7, LT)):
                    half, n = turned_half[0:rows, 0:j1 - j0, :], 64
                    part = v[0:rows, j0:j1, :]
                    link(nc.gpsimd.tensor_tensor(half[:, :, 0:n], part[:, :, n:DC], sin_k[0:rows, j0:j1, 0:n], ALU.mult))
                    link(nc.gpsimd.tensor_tensor(half[:, :, n:DC], part[:, :, 0:n], sin_k[0:rows, j0:j1, n:DC], ALU.mult))
                    link(nc.gpsimd.tensor_tensor(part, part, cos_k[0:rows, j0:j1, :], ALU.mult))
                    i = nc.gpsimd.tensor_tensor(part, part, half, ALU.add)
                    if j0 == 0:
                        link(i)
                i.then_inc(vals_ready, 1)
                pool.wait_ge(vals_ready, b + 1)
                if back < 2:
                    pool.wait_ge(qabs_ready, NH)
                    pool.wait_ge(magnitudes_taken, MAG)
                else:
                    pool.wait_ge(scores4, b * 32 - 32)
                    nc.gpsimd.tensor_tensor(stat[:, 262:263], power[:, 0:1], power[:, 0:1], ALU.add)
                q_b = q4[:, b, :] if type(b) is int else q4[:, bass.ds(b, 1), :].rearrange("p a n -> p (a n)")
                nc.gpsimd.tensor_copy(q_now[u], q_b).then_inc(q_now_ready, 1)
            for u in range(2):
                batch(u, u, back=u)
            n0, per = link.n, 2 * 7
            with pool.Fori(0, B // 2 - 1) as i:
                link.base = i * per
                for u in range(2):
                    batch(i * 2 + (2 + u), u)
            assert link.n == n0 + per
            link.n, link.base = n0 + per * (B // 2 - 1), 0

        def ctx_rows(b):
            rows = T["ctx"][b] if type(b) is int else T["ctx"][bass.ds(b, 1)].rearrange("a l d -> (a l) d")
            return (rows[0:LFULL * LT, :].rearrange("(p j) d -> p j d", j=LT),
                    rows[LFULL * LT:LCTX, :].unsqueeze(0))

        def ctx_sp(sp, b, u):
            full, rest = ctx_rows(b)
            sp.dma_start(vals[u][0:LFULL], full).then_inc(ctx_loaded[u], 16)
            sp.dma_start(vals[u][LFULL:LFULL + 1, 0:LREST, :], rest).then_inc(ctx_loaded[u], 16)

        def s4_loads_early(sp):
            sp.wait_ge(q2_ps, NH)
            sp.dma_start(w4q, T["w4q"]).then_inc(w4q_loaded, 16)

        def s4_sp(sp):
            sp.dma_start(w4qr, T["w4qr"]).then_inc(w4r_loaded, 16)
            sp.dma_start(w4kr, T["w4kr"]).then_inc(w4r_loaded, 16)
            sp.dma_start(w4kq, T["w4kq"]).then_inc(w4kq_loaded, 16)

        def s4_sp_main(sp):
            sp.wait_ge(picked_used, NT * TOPK)
            sp.dma_start(RR[:, 7168:7168 + 6 * S], T["rope_q"]).then_inc(rope_q_loaded, 16)
            for u in range(2):
                ctx_sp(sp, u, u)
            sp.dma_start(cos_k, T["rope_k"][0]).then_inc(rope_k_loaded, 16)
            norms[3].wait(sp, "xT_ps", KC)
            sp.dma_start(sin_k, T["rope_k"][1]).then_inc(rope_k_loaded, 16)
            for n in range(MAG):
                if n >= 2:
                    sp.wait_ge(magnitudes_taken, n - 1)
                sp.dma_start(mag[n % 2], T["w6"][:, n * MAGW:(n + 1) * MAGW]).then_inc(mag_loaded[n % 2], 16)
            sp.wait_ge(qbig_ps, NH)
            sp.dma_start(w4kv, T["w4kv"]).then_inc(w4o_loaded, 16)
            sp.dma_start(w4o, T["w4o"]).then_inc(w4o_loaded, 16)
            with sp.Fori(0, B // 2 - 1) as i:
                for u in range(2):
                    sp.wait_ge(o_rows_ps, i * 16 + (8 + 8 * u))
                    ctx_sp(sp, i * 2 + (2 + u), u)

        w5 = cut(RA, 0, 4, KC * DM).rearrange("p w (c n) -> p w c n", n=DM)
        b5q, b5k, b5v = (vecs[:, 18 + 4 * i:22 + 4 * i] for i in range(3))
        H5 = H1.again()
        w5_loaded, b5_loaded = sem("w5_loaded"), sem("b5_loaded")
        v5_act, v5_dve, v5_swapped = (sem(n) for n in ("v5_act", "v5_dve", "v5_swapped"))

        def s5_pe(pe):
            xT_pe(pe, 4)
            xT_ready(pe, 4)
            pe.wait_ge(w5_loaded, 16)
            for t in range(NT):
                for kc in range(KC):
                    i = nc.tensor.matmul(ps[:, 4 + t, :], xT[:, kc, t * P:(t + 1) * P], w5[:, 2, kc, :],
                                         start=(kc == 0), stop=(kc == KC - 1))
                i.then_inc(H5["v_ps"], 1)
            for which, base, done in ((0, 0, H5["q_ps"]), (1, 4, H5["k_ps"])):
                for c in range(KC):
                    if which:
                        pe.wait_ge(v5_act, c + 1)
                        pe.wait_ge(v5_dve, c + 1)
                    for kc in range(KC):
                        i = nc.tensor.matmul(ps[:, base + c, :], w5[:, which, kc, c * P:(c + 1) * P], xT[:, kc, :],
                                             start=(kc == 0), stop=(kc == KC - 1))
                    i.then_inc(done, 1)
            heads_pe(pe, H5, w5[:, 3], lambda: pe.wait_ge(v5_swapped, 32), projected[3])

        def v5_half(u, t):
            own = slice(64 * u, 64 * u + S)
            return mh_v[own, 2 * t + u, :], ps[own, 4 + t, :]

        def s5_act(act):
            xT_act(act, 4)
            for t in range(NT):
                H5.wait(act, "v_ps", t + 1)
                nc.scalar.copy(*v5_half(0, t)).then_inc(v5_act, 1)
            act.wait_ge(b5_loaded, 16)
            for c in range(KC):
                H5.wait(act, "q_ps", c + 1)
                nc.scalar.activation(mh_q[:, c, :], ps[:, c, :], ACT.Identity, bias=b5q[:, c:c + 1]).then_inc(H5["q"], 1)
            heads_act(act, H5, b5v)

        def s5_dve(dve, link):
            norm_dve(dve, link, 4)
            xT_dve(dve, 4)
            for t in range(NT):
                H5.wait(dve, "v_ps", t + 1)
                nc.vector.tensor_copy(*v5_half(1, t)).then_inc(v5_dve, 1)
            dve.wait_ge(b5_loaded, 16)
            for c in range(KC):
                H5.wait(dve, "k_ps", c + 1)
                nc.vector.tensor_scalar(mh_k[:, c, :], ps[:, 4 + c, :], b5k[:, c:c + 1], None, ALU.add).then_inc(H5["k"], 1)
            heads_dve(dve, link, H5, False)
            dve.wait_ge(x_biased, 3)
            for t in range(NT):
                projected[3].wait(dve, "rows", t + 1)
                link(nc.vector.tensor_tensor(x[:, t, :], x[:, t, :], ps[:, 4 + t, :], ALU.add))

        def s5_pool(pool, link):
            norm_pool(pool, link, 4)
            norms[4].wait(pool, "xn", NT)
            pool.wait_ge(row_loaded, 32)
            nc.gpsimd.tensor_tensor(x[:], x[:], row_bias[:].unsqueeze(1).broadcast_to([P, NT, DM]), ALU.add).then_inc(x_biased, 1)

        def s5_sp(sp):
            sp.wait_ge(row_loaded, 16)
            sp.wait_ge(hn_ready, NT)
            sp.dma_start(row_bias[:], T["b5o"].unsqueeze(0).broadcast_to([P, DM])).then_inc(row_loaded, 16)
            sp.dma_start(vecs[:, 18:30], T["vec5"]).then_inc(b5_loaded, 16)
            sp.wait_ge(o_rows_ps, B * HP)
            sp.dma_start(RA[:], T["w5"]).then_inc(w5_loaded, 16)

        def s5_sp_swap(sp):
            sp.wait_ge(v5_act, NT)
            sp.wait_ge(v5_dve, NT)
            pairs = mh_v.rearrange("p (t u) d -> p u t d", u=2)
            for u in range(2):
                sp.dma_start(pairs[64 * (1 - u):64 * (1 - u) + S, u], pairs[64 * u:64 * u + S, u]).then_inc(v5_swapped, 16)

        WGU, WDN = KC * 2 * FF, FF * DM // P
        MAG = 48
        MAGW = (WGU + WDN) // MAG
        MAG_GU = WGU // MAGW
        RAW = 12
        RAW_GU = WGU // FF
        mag = [cut(RG, MAGW * i, MAGW) for i in range(2)]
        raw = [cut(RE, FF * i, FF) for i in range(4)]
        mag_sum = stat[:, 350:350 + MAG]
        mag_total, w_mean, w_scale = stat[:, 400:402], stat[:, 494:496], stat[:, 492:494]
        ident16 = stat[:, 402:466].bitcast(BF16)
        w6gu = RB[:, 0:WGU // 2].bitcast(BF16)
        w6d = RC[:, 0:WDN // 2].bitcast(BF16)
        mag_loaded = ring_loaded[0:2]
        raw_loaded = ring_loaded
        BEFORE_MAG = 16 * NE // 4
        BEFORE_RAW = [BEFORE_MAG + 16 * MAG // 2] * 2 + [BEFORE_MAG] * 2
        magnitudes_taken, mag_total_ready, mag_ps, w_scale_ready, ternary_ready = (
            sem(n) for n in ("magnitudes_taken", "mag_total_ready", "mag_ps", "w_scale_ready", "ternary_ready"))
        ROUND = 1.5 * 2.0 ** 23

        def magnitude_act(act, n):
            act.wait_ge(mag_loaded[n % 2], BEFORE_MAG + 16 * (n // 2 + 1))
            nc.scalar.activation(mag[n % 2], mag[n % 2], ACT.Abs, accum_out=mag_sum[:, n:n + 1]).then_inc(magnitudes_taken, 1)

        def weight_scales_pe(pe):
            pe.wait_ge(mag_total_ready, 1)
            nc.tensor.matmul(ps[:, 3, 0:2], ones, mag_total, start=True, stop=True).then_inc(mag_ps, 1)
            pe.wait_ge(w_scale_ready, 1)

        def weight_scales_dve(dve, link):
            dve.wait_ge(magnitudes_taken, MAG)
            nc.vector.tensor_reduce(mag_total[:, 0:1], mag_sum[:, 0:MAG_GU], AX, ALU.add)
            link(nc.vector.tensor_reduce(mag_total[:, 1:2], mag_sum[:, MAG_GU:MAG], AX, ALU.add))
            nc.vector.tensor_copy(ident16, ident).then_inc(mag_total_ready, 1)
            dve.wait_ge(mag_ps, 1)
            nc.vector.tensor_scalar(w_mean[:, 0:1], ps[:, 3, 0:1], 1.0 / (P * WGU), 1e-5, ALU.mult, ALU.max)
            link(nc.vector.tensor_scalar(w_mean[:, 1:2], ps[:, 3, 1:2], 1.0 / (P * WDN), 1e-5, ALU.mult, ALU.max))
            nc.vector.reciprocal(w_scale, w_mean).then_inc(w_scale_ready, 1)

        def ternary(pool, link, m, n):
            i = int(n >= RAW_GU)
            pool.wait_ge(raw_loaded[m % 4], BEFORE_RAW[m % 4] + 16 * (m // 4 + 1))
            r, dst = raw[m % 4], (w6d[:, (n - RAW_GU) * FF:(n - RAW_GU + 1) * FF] if i else w6gu[:, n * FF:(n + 1) * FF])
            link(nc.gpsimd.tensor_scalar(r, r, w_scale[:, i:i + 1], 1.0, ALU.mult, ALU.min))
            link(nc.gpsimd.tensor_scalar(r, r, -1.0, ROUND, ALU.max, ALU.add))
            nc.gpsimd.tensor_scalar(dst, r, -ROUND, None, ALU.add).then_inc(ternary_ready, 1)

        PIECES = list(range(RAW_GU, RAW)) + list(range(RAW_GU))

        def s6_pool_down(pool, link):
            pool.wait_ge(w_scale_ready, 1)
            pool.wait_ge(l4_ps, NH)
            for m in range(RAW - RAW_GU):
                ternary(pool, link, m, PIECES[m])

        def s6_pool_up(pool, link):
            for m in range(RAW - RAW_GU, RAW):
                ternary(pool, link, m, PIECES[m])
            norm_pool(pool, link, 5)
            pool.wait_ge(sq_ready, 2 * NT)
            link(nc.gpsimd.tensor_scalar(rms_in, sq, 1.0 / DM, 1e-5, ALU.mult, ALU.add))
            nc.gpsimd.tensor_tensor(rms, rms_in, power, ALU.pow).then_inc(rms_ready, 1)

        h6 = cut(RR, 0, NT, DM)
        xq = RR[:, 2048:3072].bitcast(BF16).rearrange("p (t n) -> p t n", t=NT)
        xqT = RR[:, 3072:4096].bitcast(BF16).rearrange("p (c n) -> p c n", c=KC)
        relu6 = [cut(RQ, 512 * i, 512) for i in range(2)]
        relu2 = [cut(RQ, 1024 + 512 * i, 512) for i in range(2)]
        hid = [cut(RQ, 2048 + FF * i, FF) for i in range(2)]
        hq = [RQ[:, 4864 + FF // 2 * i:4864 + FF // 2 * (i + 1)].bitcast(BF16) for i in range(2)]
        FC = FF // P
        hqT = [RQ[:, 6272 + FF // 2 * i:6272 + FF // 2 * (i + 1)].bitcast(BF16).rearrange("p (c n) -> p c n", n=P) for i in range(2)]
        top6, scale6, alpha6 = stat[:, 466:470], stat[:, 470:474], stat[:, 474:478]
        toph, scaleh, deltah = stat[:, 478:482], stat[:, 482:486], stat[:, 486:490]
        PIECE6 = [(512 * i, min(512, FF - 512 * i)) for i in range(3)]
        xq_ready, xqT_ps, xqT_ready, alpha_ready, gu6_ps, relu_ready, hid_ready, hq_ready, hqT_ps, hqT_ready, down6_ps = (
            sem(n) for n in ("xq_ready", "xqT_ps", "xqT_ready", "alpha_ready", "gu6_ps", "relu_ready",
                             "hid_ready", "hq_ready", "hqT_ps", "hqT_ready", "down6_ps"))

        def s6_pe(pe):
            pe.wait_ge(xq_ready, NT)
            for kc in range(KC):
                bank = ps[:, kc, :].bitcast(BF16)
                for t in range(NT):
                    i = nc.tensor.transpose(bank[:, t * P:(t + 1) * P], xq[:, t, kc * P:(kc + 1) * P], ident16)
                i.then_inc(xqT_ps, 1)
            pe.wait_ge(xqT_ready, KC)
            pe.wait_ge(ternary_ready, RAW)

            def down(t):
                pe.wait_ge(hq_ready, t + 1)
                for c in range(FC):
                    bank = ps[:, 4 + c // 8, :].bitcast(BF16)
                    i = nc.tensor.transpose(bank[:, (c % 8) * P:(c % 8 + 1) * P], hq[t % 2][:, c * P:(c + 1) * P], ident16)
                i.then_inc(hqT_ps, 1)
                pe.wait_ge(hqT_ready, t + 1)
                if t:
                    pe.wait_ge(x_final, t)
                for c in range(FC):
                    i = nc.tensor.matmul(ps[:, 6, :], hqT[t % 2][:, c, :], w6d[:, c * DM:(c + 1) * DM],
                                         start=(c == 0), stop=(c == FC - 1))
                i.then_inc(down6_ps, 1)
            for t in range(NT):
                for n, (at, w) in enumerate(PIECE6):
                    m = 3 * t + n
                    if m >= 2:
                        pe.wait_ge(hid_ready, m - 1)
                    for up in range(2):
                        for kc in range(KC):
                            col = (2 * kc + up) * FF + at
                            i = nc.tensor.matmul(ps[:, 2 * (m % 2) + up, 0:w], xqT[:, kc, t * P:(t + 1) * P], w6gu[:, col:col + w],
                                                 start=(kc == 0), stop=(kc == KC - 1))
                    i.then_inc(gu6_ps, 1)
                if t:
                    down(t - 1)
            down(NT - 1)

        def s6_act(act):
            for t in range(NT):
                norms[5].wait(act, "xn", t + 1)
                nc.scalar.activation(h6[:, t, :], xn[:, t, :], ACT.Square, accum_out=sq[:, t:t + 1]).then_inc(sq_ready, 1)
            act.wait_ge(alpha_ready, 1)
            for m in range(3 * NT):
                t, w = m // 3, PIECE6[m % 3][1]
                act.wait_ge(gu6_ps, m + 1)
                if m >= 2:
                    act.wait_ge(hid_ready, m - 1)
                    act.wait_ge(relu_ready, m - 1)
                nc.scalar.activation(relu6[m % 2][:, 0:w], ps[:, 2 * (m % 2), 0:w], ACT.Relu, scale=alpha6[:, t:t + 1]).then_inc(relu_done, 1)
                act.wait_ge(relu_done, m + 1)
                nc.scalar.activation(relu2[m % 2][:, 0:w], relu6[m % 2][:, 0:w], ACT.Square).then_inc(relu_ready, 1)

        relu_done = sem("relu_done")

        def quantise(link, dst, v, scale, last):
            link(nc.vector.tensor_scalar(v, v, scale, 127.0, ALU.mult, ALU.min))
            link(nc.vector.tensor_scalar(v, v, -128.0, ROUND, ALU.max, ALU.add))
            nc.vector.tensor_scalar(dst, v, -ROUND, None, ALU.add).then_inc(last, 1)

        def s6_dve(dve, link):
            norm_dve(dve, link, 5)
            dve.wait_ge(rms_ready, 2)
            dve.wait_ge(row_loaded, 48)
            for t in range(NT):
                i = nc.vector.scalar_tensor_tensor(h6[:, t, :], xn[:, t, :], rms[:, t:t + 1], row_bias[:], ALU.mult, ALU.mult)
            link(i)
            link(nc.vector.tensor_reduce(top6, h6, AX, ALU.max, apply_absolute_value=True))
            link(nc.vector.tensor_scalar(top6, top6, 1e-5, None, ALU.max))
            link(nc.vector.reciprocal(scale6, top6))
            link(nc.vector.tensor_scalar(scale6, scale6, 127.0, None, ALU.mult))
            nc.vector.tensor_scalar(alpha6, top6, 1.0 / 127.0, w_mean[:, 0:1], ALU.mult, ALU.mult).then_inc(alpha_ready, 1)
            for t in range(NT):
                quantise(link, xq[:, t, :], h6[:, t, :], scale6[:, t:t + 1], xq_ready)
            for kc in range(KC):
                dve.wait_ge(xqT_ps, kc + 1)
                nc.vector.tensor_copy(xqT[:, kc, :], ps[:, kc, :].bitcast(BF16)[:, 0:TOK]).then_inc(xqT_ready, 1)
            dve.wait_ge(alpha_ready, 1)

            def down(t):
                dve.wait_ge(hqT_ps, t + 1)
                flat = hqT[t % 2].rearrange("p c n -> p (c n)")
                nc.vector.tensor_copy(flat[:, 0:8 * P], ps[:, 4, :].bitcast(BF16))
                nc.vector.tensor_copy(flat[:, 8 * P:FF], ps[:, 5, :].bitcast(BF16)[:, 0:FF - 8 * P]).then_inc(hqT_ready, 1)
                dve.wait_ge(down6_ps, t + 1)
                nc.vector.scalar_tensor_tensor(x[:, t, :], ps[:, 6, :], deltah[:, t:t + 1], x[:, t, :], ALU.mult,
                                               ALU.add).then_inc(x_final, 1)
            for t in range(NT):
                v = hid[t % 2]
                for n, (at, w) in enumerate(PIECE6):
                    m = 3 * t + n
                    dve.wait_ge(relu_ready, m + 1)
                    nc.vector.scalar_tensor_tensor(v[:, at:at + w], ps[:, 2 * (m % 2) + 1, 0:w], alpha6[:, t:t + 1],
                                                   relu2[m % 2][:, 0:w], ALU.mult, ALU.mult).then_inc(hid_ready, 1)
                dve.wait_ge(hid_ready, 3 * t + 3)
                link(nc.vector.tensor_reduce(toph[:, t:t + 1], v, AX, ALU.max, apply_absolute_value=True))
                link(nc.vector.tensor_scalar(toph[:, t:t + 1], toph[:, t:t + 1], 1e-5, None, ALU.max))
                link(nc.vector.reciprocal(scaleh[:, t:t + 1], toph[:, t:t + 1]))
                link(nc.vector.tensor_scalar(scaleh[:, t:t + 1], scaleh[:, t:t + 1], 127.0, None, ALU.mult))
                link(nc.vector.tensor_scalar(deltah[:, t:t + 1], toph[:, t:t + 1], 1.0 / 127.0, w_mean[:, 1:2], ALU.mult, ALU.mult))
                quantise(link, hq[t % 2], v, scaleh[:, t:t + 1], hq_ready)
                if t:
                    down(t - 1)
            down(NT - 1)

        def s6_sp(sp):
            for m in range(RAW):
                n = PIECES[m]
                if m >= 4:
                    sp.wait_ge(ternary_ready, m - 3)
                sp.dma_start(raw[m % 4], T["w6"][:, n * FF:(n + 1) * FF]).then_inc(raw_loaded[m % 4], 16)
                if m == 3:
                    s5_sp_swap(sp)
            sp.wait_ge(x_biased, 3)
            sp.dma_start(row_bias[:], T["norm6"].unsqueeze(0).broadcast_to([P, DM])).then_inc(row_loaded, 16)

        block = ctx.enter_context(nc.Block())

        @block.sync
        def _(sp):
            sp.dma_start(x[:], T["x"].rearrange("b s h -> (b s) h").rearrange("(t p) h -> p t h", p=P)).then_inc(x_loaded, 16)
            sp.dma_start(cst[:], T["cst"]).then_inc(cst_loaded, 16)
            c64_rows = T["ctx"][:, 0:S, :].rearrange("b l d -> l b d")
            for u in range(2):
                sp.dma_start(c64[64 * u:64 * u + S, :, :], c64_rows).then_inc(c64_loaded, 16)
            sp.dma_start(w1kv, T["w1kv"]).then_inc(w1_loaded, 16)
            sp.dma_start(w1q, T["w1q"]).then_inc(w1q_loaded, 16)
            sp.dma_start(w1o, T["w1o"]).then_inc(w1o_loaded, 16)
            sp.dma_start(vecs[:, 0:18], T["vec2"]).then_inc(w2_loaded, 16)
            sp.dma_start(w2kv, T["w2kv"]).then_inc(w2_loaded, 16)
            sp.dma_start(w2q, T["w2q"]).then_inc(w2q_loaded, 16)
            sp.dma_start(row_bias[:], T["b2o"].unsqueeze(0).broadcast_to([P, DM])).then_inc(w2_loaded, 16)
            sp.dma_start(w2o, T["w2o"]).then_inc(w2o_loaded, 16)
            sp.dma_start(gate[:], T["gate"]).then_inc(gate_loaded, 16)
            if STAGES >= 3:
                s3_loads_early(sp)
            sp.wait_ge(v2_ready, 2)
            for u in range(2):
                pairs = v2.rearrange("p (t u) d -> p u t d", u=2)
                sp.dma_start(pairs[64 * (1 - u):64 * (1 - u) + S, u], pairs[64 * u:64 * u + S, u]).then_inc(v2_swapped, 16)
            if STAGES >= 4:
                s4_loads_early(sp)
            if STAGES >= 3:
                s3_sp(sp)
            if STAGES >= 4:
                s4_sp_main(sp)
            if STAGES >= 5:
                s5_sp(sp)
            if STAGES == 5:
                s5_sp_swap(sp)
            if STAGES >= 6:
                s6_sp(sp)
            for t in range(NT):
                sp.wait_ge(x_final, t + 1)
                sp.dma_start(out.rearrange("b s h -> (b s) h").rearrange("(t p) h -> p t h", p=P)[:, t, :], x[:, t, :]).then_inc(out_stored, 16)
            sp.wait_ge(out_stored, 16 * NT)

        @block.gpsimd
        def _(pool):
            link = Chain(pool, "pool_chain")
            norm_pool(pool, link, 0)
            if STAGES >= 2:
                norm_pool(pool, link, 1)
                norms[1].wait(pool, "xn", NT)
                pool.wait_ge(w2_loaded, 48)
                nc.gpsimd.tensor_tensor(x[:], x[:], row_bias[:].unsqueeze(1).broadcast_to([P, NT, DM]), ALU.add).then_inc(x_biased, 1)
            if STAGES >= 3:
                s3_pool(pool, link)
            if STAGES >= 4:
                s4_pool(pool, link)
            if STAGES >= 6:
                s6_pool_down(pool, link)
            if STAGES >= 5:
                s5_pool(pool, link)
            if STAGES >= 6:
                s6_pool_up(pool, link)

        @block.tensor
        def _(pe):
            s1_pe(pe)
            if STAGES >= 2:
                s2_pe(pe)
            if STAGES >= 3:
                s3_pe(pe)
            if STAGES >= 4:
                s4_pe(pe)
            if STAGES >= 5:
                s5_pe(pe)
            if STAGES >= 6:
                s6_pe(pe)

        @block.scalar
        def _(act):
            s1_act(act)
            if STAGES >= 2:
                s2_act(act)
            if STAGES >= 3:
                s3_act(act)
            if STAGES >= 4:
                s4_act(act)
            if STAGES >= 5:
                s5_act(act)
            if STAGES >= 6:
                s6_act(act)

        @block.vector
        def _(dve):
            link = Chain(dve, "dve_chain")
            s1_dve(dve, link)
            if STAGES >= 2:
                s2_dve(dve, link)
            if STAGES >= 3:
                s3_dve(dve, link)
            if STAGES >= 4:
                s4_dve(dve, link)
            if STAGES >= 5:
                s5_dve(dve, link)
            if STAGES >= 6:
                s6_dve(dve, link)
            if STAGES < 6:
                for t in range(4):
                    nc.vector.memset(stat[:, 45:46], 0.0).then_inc(x_final, 1)


def constants():
    import numpy as np
    n = np.arange(P)
    c = np.zeros((P, 5, P), np.float32)
    c[:, 0] = n[:, None] == n[None, :]
    c[:, 1] = n[:, None] < n[None, :]
    c[:, 2] = 1.0
    c[:, 3] = n[None, :]
    for t in range(NT):
        c[:, 4, S + 2 * t], c[:, 4, S + 2 * t + 1] = n, t * P
    c[:, 4, 0:S] = np.where(n[None, :S] <= n[:, None] % S, 0.0, MASKED)
    return c


def rope_tables(length, dim):
    import numpy as np
    f32 = np.float32
    inv = f32(1.0) / f32(10000.0) ** (np.arange(0, dim, 2, dtype=f32) / f32(dim))
    f = np.arange(length, dtype=f32)[:, None] * inv[None, :]
    return np.repeat(np.sin(f), 2, -1), np.repeat(np.cos(f), 2, -1)


def rope_queries():
    import numpy as np
    sin, cos = rope_tables(S, DCQ)
    sin = np.where(np.arange(DCQ) < DCQ // 2, -sin, sin)
    cols = query_columns()[:3]
    return np.stack([tab[:, c].T for tab in (cos, sin) for c in cols], 1).reshape(P, 6 * S)


def rope_context():
    import numpy as np
    sin, cos = rope_tables(LCTX, DC)
    sin = np.where(np.arange(DC) < DC // 2, -sin, sin)
    tabs = np.zeros((2, P * LT, DC), np.float32)
    tabs[0, :LCTX], tabs[1, :LCTX] = cos, sin
    return tabs.reshape(2, P, LT, DC)


def query_columns():
    import numpy as np
    h = DCQ // 2
    return [np.arange(P), np.arange(h, h + P), np.r_[P:h, h + P:DCQ], np.r_[h + P:DCQ, P:h]]


def kernel(**inputs):
    import numpy as np
    import concourse.bacc as bacc
    from concourse.bass_utils import run_bass_kernel_spmd as run

    def chunks(w):
        return w.reshape(w.shape[0] // P, P, w.shape[1]).transpose(1, 0, 2)

    I = {k: np.asarray(v) for k, v in inputs.items()}
    T = {
        "x": I["x"], "ctx": I["ctx_512"], "cst": constants(),
        "w1q": chunks(I["L0_xattn_Wq"].T), "w1kv": I["L0_xattn_Wkv_expand"].T, "w1o": chunks(I["L0_xattn_Wout"].T),
        "vec2": np.concatenate([I["L0_attn_bq"].reshape(NH, P).T, I["L0_attn_bk"][:, None], I["L0_attn_bv"][:, None]], 1),
        "w2kv": np.stack([chunks(I["L0_attn_Wk"]), chunks(I["L0_attn_Wv"])], 1),
        "w2q": chunks(I["L0_attn_Wq"]), "w2o": chunks(I["L0_attn_Wo"]), "b2o": I["L0_attn_bo"],
        "norm3": I["L0_ffn_norm_w"], "gate": chunks(I["L0_ffn_gate_w"].T),
        "w3": np.concatenate([I["L0_ffn_w13"].reshape(NE, KC, P, DM), I["L0_ffn_w2"].reshape(NE, 2, P, DM)], 1).transpose(0, 2, 1, 3),
        "w3s": np.concatenate([chunks(np.concatenate([I["L0_ffn_shared_gate_w"], I["L0_ffn_shared_up_w"]], 1)),
                               chunks(I["L0_ffn_shared_down_w"])], 1),
        "w4q": chunks(I["L1_xattn_Wq"].T),
        "w4kq": I["L1_xattn_w_kc_q"][:, :, np.concatenate(query_columns())].transpose(1, 0, 2),
        "w4qr": I["L1_xattn_W_qr"][:, np.concatenate(query_columns()[:3]), :].transpose(0, 2, 1)
                .reshape(2, NH // 2, R, DCQ).transpose(0, 2, 1, 3).reshape(P, NH // 2, DCQ),
        "w4kr": I["L1_xattn_W_kr"].transpose(0, 2, 1).reshape(2, NH // 2, R, DC).transpose(0, 2, 1, 3).reshape(P, NH // 2, DC),
        "w4kv": I["L1_xattn_w_kc_kv"].transpose(2, 0, 1), "w4o": chunks(I["L1_xattn_Wo"].T),
        "rope_q": rope_queries(), "rope_k": rope_context(),
        "w5": np.stack([chunks(I["L1_attn_" + n].T) for n in ("wq", "wk", "wv", "wo")], 1).reshape(P, 4 * KC * DM),
        "vec5": np.concatenate([I["L1_attn_" + n].reshape(KC, P).T for n in ("bq", "bk", "bv")], 1), "b5o": I["L1_attn_bo"],
        "w6": np.concatenate([chunks(I["L1_ffn_w_gate_up"].T).reshape(P, KC * 2 * FF),
                              chunks(I["L1_ffn_w_down"].T).reshape(P, FF * DM // P)], 1),
        "norm6": I["L1_ffn_norm_weight"],
    }
    nc = bacc.Bacc("TRN2", target_bir_lowering=False, num_devices=1)
    arrays, aps = {}, {}
    for name, a in T.items():
        a = np.ascontiguousarray(a)
        arrays["in_" + name] = a
        aps[name] = nc.dram_tensor("in_" + name, a.shape, mybir.dt.from_np(a.dtype), kind="ExternalInput").ap()
    o = nc.dram_tensor("out_0", (B, S, DM), F32, kind="ExternalOutput").ap()
    scratch = {"h_rows": nc.dram_tensor("h_rows", (TOK, DM), F32, kind="Internal").ap(),
               "eo_rows": nc.dram_tensor("eo_rows", (NE * CAP, DM), F32, kind="Internal").ap()}
    perceiver(nc, aps, o, scratch)
    r = run(nc, [arrays], core_ids=[0])
    return r.results[0]["out_0"]
```

```python
from contextlib import ExitStack

import concourse.bass as bass
from concourse import mybir

F32 = mybir.dt.float32
BF16 = mybir.dt.bfloat16
U32 = mybir.dt.uint32
ALU = mybir.AluOpType
ACT = mybir.ActivationFunctionType
AX = mybir.AxisListType.X

STAGES = 6

P = 128
B, S, DM = 8, 64, 512
TOK = B * S
NT = TOK // P
KC = DM // P
NH = 16
HD = DM // NH
LCTX = 1601
LT = -(-LCTX // P)
LAST = LCTX - (LT - 1) * P
DC = 128
DCQ = 384
R = 64
NE, TOPK, FI = 32, 4, 256
CAP = 2 * TOK * TOPK // NE
FF = 1408
LN_EPS = 1e-5
MASKED = -3.0e38


def perceiver(nc, T, out, scratch):
    ctx = ExitStack()
    with ctx:
        def sb(name, shape, dt=F32):
            return ctx.enter_context(nc.sbuf_tensor(name, shape, dt))

        def sem(name):
            return ctx.enter_context(nc.semaphore(name))

        ps = ctx.enter_context(nc.psum_tensor("ps", [P, 8, 512], F32))

        x = sb("x", [P, NT, DM])
        xn = sb("xn", [P, NT, DM])
        xT = sb("xT", [P, KC, TOK])
        cst = sb("cst", [P, 5, P])
        ident, before, ones, iota = (cst[:, i, :] for i in range(4))
        causal = cst[:, 4, 0:S]
        vecs = sb("vecs", [P, 64])
        row_bias = sb("row_bias", [P, DM])
        stat = sb("stat", [P, 512])

        RA = sb("RA", [P, 8192])
        RB = sb("RB", [P, 8192])
        RC = sb("RC", [P, 5120])
        RQ = sb("RQ", [P, 8192])
        RR = sb("RR", [P, 8192])
        RE = sb("RE", [P, 6144])
        RG = sb("RG", [P, 1024])

        def cut(region, at, *shape):
            n = 1
            for s in shape:
                n *= s
            v = region[:, at:at + n]
            if len(shape) == 2:
                v = v.rearrange("p (a b) -> p a b", b=shape[1])
            if len(shape) == 3:
                v = v.rearrange("p (a b c) -> p a b c", b=shape[1], c=shape[2])
            return v

        class Chain:

            def __init__(self, eng, name):
                self.eng, self.sem, self.n, self.base = eng, sem(name), 0, 0

            def __call__(self, ins):
                self.n += 1
                ins.then_inc(self.sem, 1)
                self.eng.wait_ge(self.sem, self.n + self.base)

        bst = cut(stat, 0, NT, 6)
        mv = cut(stat, 24, NT, 2)
        rstd = stat[:, 32:36]
        vare = stat[:, 36:40]
        power = stat[:, 40:44]

        class Rounds:

            def __init__(self, prefix, per, sems=None, run=0):
                self.prefix, self.per, self.run = prefix, per, run
                self.sems = sems or {n: sem(f"{prefix}_{n}") for n in per}

            def again(self):
                return Rounds(self.prefix, self.per, self.sems, self.run + 1)

            def __getitem__(self, name):
                return self.sems[name]

            def wait(self, eng, name, value):
                assert 0 < value <= self.per[name]
                eng.wait_ge(self.sems[name], self.run * self.per[name] + value)

        norms = [Rounds("norm", {"var": 1, "rstd": 1, "xn": NT, "xT_ps": KC, "xT_act": 2, "xT_dve": 2})]
        for _ in range(5):
            norms.append(norms[-1].again())

        def norm_dve(dve, link, k):
            for t in range(NT):
                nc.vector.bn_stats(bst[:, t, :], x[:, t, :])
            link(nc.vector.memset(stat[:, 44:45], 0.0))
            for t in range(NT):
                i = nc.vector.bn_aggr(mv[:, t, :], bst[:, t, :])
            i.then_inc(norms[k]["var"], 1)
            norms[k].wait(dve, "rstd", 1)
            for t in range(NT):
                nc.vector.tensor_scalar(xn[:, t, :], x[:, t, :], mv[:, t, 0:1], rstd[:, t:t + 1],
                                        ALU.subtract, ALU.mult).then_inc(norms[k]["xn"], 1)

        def norm_pool(pool, link, k):
            norms[k].wait(pool, "var", 1)
            link(nc.gpsimd.tensor_scalar(vare, mv[:, :, 1], LN_EPS, None, ALU.add))
            nc.gpsimd.tensor_tensor(rstd, vare, power, ALU.pow).then_inc(norms[k]["rstd"], 1)

        def xT_pe(pe, k, rows=None, ready=None):
            rows = xn if rows is None else rows
            if ready is None:
                norms[k].wait(pe, "xn", NT)
            else:
                pe.wait_ge(ready, NT)
            for kc in range(KC):
                for t in range(NT):
                    i = nc.tensor.transpose(ps[:, kc, t * P:(t + 1) * P], rows[:, t, kc * P:(kc + 1) * P], ident)
                i.then_inc(norms[k]["xT_ps"], 1)

        def xT_act(act, k):
            for kc in (0, 1):
                norms[k].wait(act, "xT_ps", kc + 1)
                nc.scalar.copy(xT[:, kc, :], ps[:, kc, :]).then_inc(norms[k]["xT_act"], 1)

        def xT_dve(dve, k):
            for kc in (2, 3):
                norms[k].wait(dve, "xT_ps", kc + 1)
                nc.vector.tensor_copy(xT[:, kc, :], ps[:, kc, :]).then_inc(norms[k]["xT_dve"], 1)

        def xT_ready(pe, k):
            norms[k].wait(pe, "xT_act", 2)
            norms[k].wait(pe, "xT_dve", 2)

        mh_q = cut(RQ, 0, KC, TOK)
        mh_k = cut(RQ, 2048, KC, TOK)
        mh_v = cut(RQ, 4096, B, DM)
        mh_o = mh_q
        mh_p = cut(RR, 0, 2, 2048)
        mh_pT = cut(RR, 4096, 2, 4, 512)[:, :, :, :]
        mh_mx = stat[:, 64:128]
        mh_sm = stat[:, 128:192]
        mh_rs = stat[:, 192:256]

        H1 = Rounds("heads", {"q": KC, "k": KC, "v": B, "scores": 2, "shifted": 2, "exps": 2, "probs": 2, "pT_ps": 8,
                              "pT_act": 4, "pT_dve": 4, "o_ps": 1, "o": KC, "q_ps": KC, "k_ps": KC, "v_ps": B})
        projected = [Rounds("projected", {"rows": NT})]
        for _ in range(3):
            projected.append(projected[-1].again())

        def heads_pe(pe, H, w_out, values_ready, proj):
            H.wait(pe, "q", KC)
            H.wait(pe, "k", KC)
            for g in range(2):
                for pp in range(2):
                    for c in range(KC):
                        for b2 in range(2):
                            tok = (4 * g + 2 * pp + b2) * S
                            for r in range(4):
                                at = (pp * KC + c) * S
                                i = nc.tensor.matmul(ps[64 * b2:64 * b2 + S, 4 * g + r, at:at + S],
                                                     mh_q[32 * r:32 * r + HD, c, tok:tok + S],
                                                     mh_k[32 * r:32 * r + HD, c, tok:tok + S],
                                                     start=True, stop=True)
                i.then_inc(H["scores"], 1)
            for g in range(2):
                H.wait(pe, "probs", g + 1)
                for r in range(4):
                    for n in range(4):
                        i = nc.tensor.transpose(ps[:, 4 * g + r, n * P:(n + 1) * P],
                                                mh_p[:, g, r * 512 + n * P:r * 512 + (n + 1) * P], ident)
                    i.then_inc(H["pT_ps"], 1)
            values_ready()
            for g in range(2):
                H.wait(pe, "pT_act", 2 * g + 2)
                H.wait(pe, "pT_dve", 2 * g + 2)
                for pp in range(2):
                    for b2 in range(2):
                        b = 4 * g + 2 * pp + b2
                        for c in range(KC):
                            u = 64 * (c % 2)
                            for r in range(4):
                                at = (pp * 2 + c // 2) * P + b2 * S
                                h = 4 * c + r
                                i = nc.tensor.matmul(ps[32 * r:32 * r + HD, c, b * S:(b + 1) * S],
                                                     mh_v[u:u + S, b, h * HD:(h + 1) * HD],
                                                     mh_pT[u:u + S, g, r, at:at + S], start=True, stop=True)
            i.then_inc(H["o_ps"], 1)
            H.wait(pe, "o", KC)
            for t in range(NT):
                for kc in range(KC):
                    i = nc.tensor.matmul(ps[:, 4 + t, :], mh_o[:, kc, t * P:(t + 1) * P], w_out[:, kc, :],
                                         start=(kc == 0), stop=(kc == KC - 1))
                i.then_inc(proj["rows"], 1)

        def heads_dve(dve, link, H, masked):
            def group(g):
                return (mh_p[:, g, :].rearrange("p (n k) -> p n k", k=S),
                        ps[:, 4 * g:4 * g + 4, :].rearrange("p r (n k) -> p (r n) k", k=S),
                        [a[:, 32 * g:32 * g + 32] for a in (mh_mx, mh_sm, mh_rs)])
            for g in range(2):
                probs, scores, (mx, _, _) = group(g)
                H.wait(dve, "scores", g + 1)
                if masked:
                    link(nc.vector.tensor_tensor(probs, scores, causal.unsqueeze(1).broadcast_to([P, 32, S]), ALU.add))
                    scores = probs
                link(nc.vector.tensor_reduce(mx, scores, AX, ALU.max))
                nc.vector.tensor_tensor(probs, scores, mx.unsqueeze(2).broadcast_to([P, 32, S]),
                                        ALU.subtract).then_inc(H["shifted"], 1)
            for g in range(2):
                probs, _, (_, sm, rs) = group(g)
                H.wait(dve, "exps", g + 1)
                link(nc.vector.tensor_reduce(sm, probs, AX, ALU.add))
                link(nc.vector.reciprocal(rs, sm))
                nc.vector.tensor_tensor(probs, probs, rs.unsqueeze(2).broadcast_to([P, 32, S]),
                                        ALU.mult).then_inc(H["probs"], 1)
            for g in range(2):
                for r in (1, 3):
                    H.wait(dve, "pT_ps", 4 * g + r + 1)
                    nc.vector.tensor_copy(mh_pT[:, g, r, :], ps[:, 4 * g + r, :]).then_inc(H["pT_dve"], 1)

        def heads_act(act, H, bias):
            for g in range(2):
                H.wait(act, "shifted", g + 1)
                nc.scalar.activation(mh_p[:, g, :], mh_p[:, g, :], ACT.Exp, scale=HD ** -0.5).then_inc(H["exps"], 1)
            for g in range(2):
                for r in (0, 2):
                    H.wait(act, "pT_ps", 4 * g + r + 1)
                    nc.scalar.copy(mh_pT[:, g, r, :], ps[:, 4 * g + r, :]).then_inc(H["pT_act"], 1)
            H.wait(act, "o_ps", 1)
            for c in range(KC):
                if bias is None:
                    i = nc.scalar.copy(mh_o[:, c, :], ps[:, c, :])
                else:
                    i = nc.scalar.activation(mh_o[:, c, :], ps[:, c, :], ACT.Identity, bias=bias[:, c:c + 1])
                i.then_inc(H["o"], 1)

        x_loaded = sem("x_loaded")
        cst_loaded = sem("cst_loaded")
        c64_loaded = sem("c64_loaded")
        w1_loaded = sem("w1_loaded")
        w1q_loaded = sem("w1q_loaded")
        w1o_loaded = sem("w1o_loaded")
        out_stored = sem("out_stored")
        x_final = sem("x_final")

        w1q = cut(RC, 0, KC, DM)
        w1kv = cut(RC, 2048, 2 * DM)
        w1o = cut(RC, 3072, KC, DM)
        c64 = cut(RR, 0, B, P)
        c64T = cut(RR, 1024, B, P)
        c64T_ps, c64T_ready = sem("c64T_ps"), sem("c64T_ready")

        def s1_pe(pe):
            pe.wait_ge(cst_loaded, 16)
            pe.wait_ge(c64_loaded, 32)
            for b in range(B):
                i = nc.tensor.transpose(ps[:, 4 + b // 4, (b % 4) * P:(b % 4 + 1) * P], c64[:, b, :], ident)
                if b % 4 == 3:
                    i.then_inc(c64T_ps, 1)
            pe.wait_ge(c64T_ready, 2)
            pe.wait_ge(w1_loaded, 16)
            for c in range(KC):
                nc.tensor.matmul(ps[:, c, :], w1kv[:, c * P:(c + 1) * P], c64T[:, :, 0:S],
                                 start=True, stop=True).then_inc(H1["k_ps"], 1)
            for b in range(B):
                if b >= 4:
                    H1.wait(pe, "k", b - 3)
                nc.tensor.matmul(ps[:, (4 + b) % 8, :], c64T[:, b, :], w1kv[:, DM:2 * DM],
                                 start=True, stop=True).then_inc(H1["v_ps"], 1)
            H1.wait(pe, "v", B)
            xT_pe(pe, 0)
            xT_ready(pe, 0)
            pe.wait_ge(w1q_loaded, 16)
            for c in range(KC):
                for kc in range(KC):
                    i = nc.tensor.matmul(ps[:, 4 + c, :], w1q[:, kc, c * P:(c + 1) * P], xT[:, kc, :],
                                         start=(kc == 0), stop=(kc == KC - 1))
                i.then_inc(H1["q_ps"], 1)
            pe.wait_ge(w1o_loaded, 16)
            heads_pe(pe, H1, w1o, lambda: H1.wait(pe, "v", B), projected[0])

        def s1_act(act):
            for g in range(2):
                act.wait_ge(c64T_ps, g + 1)
                nc.scalar.copy(c64T[:, 4 * g:4 * g + 4, :], ps[:, 4 + g, :].rearrange("p (b n) -> p b n", b=4)).then_inc(c64T_ready, 1)
            for b in range(B):
                H1.wait(act, "v_ps", b + 1)
                nc.scalar.copy(mh_v[:, b, :], ps[:, (4 + b) % 8, :]).then_inc(H1["v"], 1)
            xT_act(act, 0)
            for c in range(KC):
                H1.wait(act, "q_ps", c + 1)
                nc.scalar.copy(mh_q[:, c, :], ps[:, 4 + c, :]).then_inc(H1["q"], 1)
            heads_act(act, H1, None)

        def s1_dve(dve, link):
            link(nc.vector.memset(power, -0.5))
            dve.wait_ge(x_loaded, 16)
            norm_dve(dve, link, 0)
            for c in range(KC):
                H1.wait(dve, "k_ps", c + 1)
                nc.vector.tensor_copy(mh_k[:, c, :], ps[:, c, :]).then_inc(H1["k"], 1)
            xT_dve(dve, 0)
            heads_dve(dve, link, H1, True)
            for t in range(NT):
                projected[0].wait(dve, "rows", t + 1)
                link(nc.vector.tensor_tensor(x[:, t, :], x[:, t, :], ps[:, 4 + t, :], ALU.add))

        w2q = cut(RA, 0, KC, 2048)
        w2o = cut(RB, 0, NH, DM)
        w2kv = cut(RG, 0, 2, KC, P)
        q2 = cut(RQ, 0, B, NH * S)
        o2 = cut(RQ, 0, NH, TOK)
        k2 = cut(RC, 0, TOK)
        v2 = cut(RC, 512, B, P)
        p2 = cut(RR, 0, B, 512)
        p2T = cut(RR, 4096, B, 512)
        b2q, b2k, b2v = vecs[:, 0:16], vecs[:, 16:17], vecs[:, 17:18]
        mx2, sm2, rs2 = (stat[:, 256 + 64 * i:320 + 64 * i] for i in range(3))
        w2_loaded = sem("w2_loaded")
        w2q_loaded = sem("w2q_loaded")
        w2o_loaded = sem("w2o_loaded")
        x_biased, k2_ps, k2_ready, v2_ps, v2_ready = (sem(n) for n in ("x_biased", "k2_ps", "k2_ready", "v2_ps", "v2_ready"))
        v2_swapped = sem("v2_swapped")
        q2_ps, q2_act, q2_dve = sem("q2_ps"), sem("q2_act"), sem("q2_dve")
        scores2, shifted2, exps2, probs2 = (sem(n) for n in ("scores2", "shifted2", "exps2", "probs2"))
        pT2_ps, pT2, o2_ps, o2_act, o2_dve = (sem(n) for n in ("pT2_ps", "pT2", "o2_ps", "o2_act", "o2_dve"))

        def by_batch(v):
            return v.rearrange("p (b s) -> p b s", s=S)

        def q2_bank(n):
            return (7 + n) % 8

        def s2_pe(pe):
            xT_pe(pe, 1)
            xT_ready(pe, 1)
            pe.wait_ge(w2_loaded, 48)
            for kc in range(KC):
                i = nc.tensor.matmul(ps[:, 4, :], w2kv[:, 0, kc, :], xT[:, kc, :], start=(kc == 0), stop=(kc == KC - 1))
            i.then_inc(k2_ps, 1)
            for t in range(NT):
                for kc in range(KC):
                    i = nc.tensor.matmul(ps[:, 5, t * P:(t + 1) * P], xT[:, kc, t * P:(t + 1) * P], w2kv[:, 1, kc, :],
                                         start=(kc == 0), stop=(kc == KC - 1))
            i.then_inc(v2_ps, 1)
            pe.wait_ge(w2q_loaded, 16)
            for h in range(NH):
                if h == 5:
                    pe.wait_ge(k2_ready, 1)
                if h == 6:
                    pe.wait_ge(v2_ready, 2)
                if h >= 8:
                    pe.wait_ge(q2_act if h % 2 == 0 else q2_dve, (h - 8) // 2 + 1)
                for kc in range(KC):
                    i = nc.tensor.matmul(ps[:, q2_bank(h), :], w2q[:, kc, h * P:(h + 1) * P], xT[:, kc, :],
                                         start=(kc == 0), stop=(kc == KC - 1))
                i.then_inc(q2_ps, 1)
            pe.wait_ge(q2_act, NH // 2)
            pe.wait_ge(q2_dve, NH // 2)
            for b in range(B):
                for hp in range(NH // 2):
                    i = nc.tensor.matmul(ps[:, b, hp * S:(hp + 1) * S], q2[:, b, hp * P:(hp + 1) * P],
                                         k2[:, b * S:(b + 1) * S], start=True, stop=True)
                i.then_inc(scores2, 1)
            for b in range(B):
                pe.wait_ge(probs2, b + 1)
                for j in range(4):
                    i = nc.tensor.transpose(ps[:, b, j * P:(j + 1) * P], p2[:, b, j * P:(j + 1) * P], ident)
                i.then_inc(pT2_ps, 1)
            pe.wait_ge(pT2, B)
            pe.wait_ge(v2_swapped, 32)
            for b in range(B):
                for e in range(2):
                    n = 2 * b + e
                    if n >= 8:
                        pe.wait_ge(o2_dve if e else o2_act, b - 3)
                    nc.tensor.matmul(ps[:, n % 8, :], v2[64 * e:64 * e + S, b, :], p2T[64 * e:64 * e + S, b, :],
                                     start=True, stop=True).then_inc(o2_ps, 1)
            pe.wait_ge(o2_act, B)
            pe.wait_ge(o2_dve, B)
            pe.wait_ge(w2o_loaded, 16)
            for t in range(NT):
                for h in range(NH):
                    i = nc.tensor.matmul(ps[:, t, :], o2[:, h, t * P:(t + 1) * P], w2o[:, h, :],
                                         start=(h == 0), stop=(h == NH - 1))
                i.then_inc(projected[1]["rows"], 1)

        def o2_rows(b, e):
            return (o2.rearrange("p (j e u) n -> p e j u n", e=2, u=2)[:, e, :, :, b * S:(b + 1) * S],
                    ps[:, (2 * b + e) % 8, :].rearrange("p (j u s) -> p j u s", u=2, s=S))

        def s2_act(act):
            xT_act(act, 1)
            act.wait_ge(k2_ps, 1)
            nc.scalar.activation(k2, ps[:, 4, :], ACT.Identity, bias=b2k).then_inc(k2_ready, 1)
            for h in range(0, NH, 2):
                act.wait_ge(q2_ps, h + 1)
                nc.scalar.activation(q2[:, :, h * S:(h + 1) * S], by_batch(ps[:, q2_bank(h), :]), ACT.Identity, bias=b2q[:, h:h + 1]).then_inc(q2_act, 1)
            for b in range(B):
                act.wait_ge(shifted2, b + 1)
                nc.scalar.activation(p2[:, b, :], p2[:, b, :], ACT.Exp, scale=P ** -0.5).then_inc(exps2, 1)
            for b in range(B):
                act.wait_ge(pT2_ps, b + 1)
                nc.scalar.copy(p2T[:, b, :], ps[:, b, :]).then_inc(pT2, 1)
            for b in range(B):
                act.wait_ge(o2_ps, 2 * b + 1)
                dst, src = o2_rows(b, 0)
                nc.scalar.activation(dst, src, ACT.Identity, bias=b2v).then_inc(o2_act, 1)

        def s2_dve(dve, link):
            norm_dve(dve, link, 1)
            xT_dve(dve, 1)
            dve.wait_ge(v2_ps, 1)
            for u in range(2):
                own = slice(64 * u, 64 * u + S)
                nc.vector.tensor_copy(v2.rearrange("p (t u) d -> p u t d", u=2)[own, u], ps[own, 5, :].rearrange("p (t d) -> p t d", d=P)).then_inc(v2_ready, 1)
            for h in range(1, NH, 2):
                dve.wait_ge(q2_ps, h + 1)
                nc.vector.tensor_scalar(q2[:, :, h * S:(h + 1) * S], by_batch(ps[:, q2_bank(h), :]), b2q[:, h:h + 1], None, ALU.add).then_inc(q2_dve, 1)
            for b in range(B + 1):
                if b < B:
                    dve.wait_ge(scores2, b + 1)
                    mx = mx2[:, 8 * b:8 * b + 8]
                    scores = ps[:, b, :].rearrange("p (n k) -> p n k", k=S)
                    link(nc.vector.tensor_reduce(mx, scores, AX, ALU.max))
                    nc.vector.tensor_tensor(p2[:, b, :].rearrange("p (n k) -> p n k", k=S), scores,
                                            mx.unsqueeze(2).broadcast_to([P, 8, S]), ALU.subtract).then_inc(shifted2, 1)
                if b:
                    dve.wait_ge(exps2, b)
                    probs = p2[:, b - 1, :].rearrange("p (n k) -> p n k", k=S)
                    sm, rs = sm2[:, 8 * b - 8:8 * b], rs2[:, 8 * b - 8:8 * b]
                    link(nc.vector.tensor_reduce(sm, probs, AX, ALU.add))
                    link(nc.vector.reciprocal(rs, sm))
                    nc.vector.tensor_tensor(probs, probs, rs.unsqueeze(2).broadcast_to([P, 8, S]), ALU.mult).then_inc(probs2, 1)
            for b in range(B):
                dve.wait_ge(o2_ps, 2 * b + 2)
                dst, src = o2_rows(b, 1)
                nc.vector.tensor_scalar(dst, src, b2v, None, ALU.add).then_inc(o2_dve, 1)
            dve.wait_ge(x_biased, 1)
            for t in range(NT):
                projected[1].wait(dve, "rows", t + 1)
                link(nc.vector.tensor_tensor(x[:, t, :], x[:, t, :], ps[:, t, :], ALU.add))

        ring = [cut(RE, 0, 6, DM), cut(RE, 3072, 6, DM), cut(RR, 0, 6, DM), cut(RR, 3072, 6, DM)]
        xe = [cut(RR, 6144 + 512 * i, DM) for i in range(2)]
        xeT = [cut(RR, 7168 + 512 * i, KC, P) for i in range(2)]
        hn = cut(RQ, 0, NT, DM)
        w3s = cut(RQ, 2048, 6, DM)
        sg = [cut(RQ, 5120 + 256 * i, FI) for i in range(2)]
        act3 = [cut(RQ, 5632 + 256 * i, FI) for i in range(2)]
        actT = [cut(RQ, 6144 + 256 * i, 2, P) for i in range(2)]
        eo = [cut(RQ, 6656 + 512 * i, DM) for i in range(2)]
        picked = [cut(RR, 512 * i, DM) for i in range(8)]
        onehot = [RG[:, 256 * i:256 * i + 256].bitcast(BF16).rearrange("p (t c) -> p t c", c=P) for i in range(2)]
        logits, pos, mask, place = (cut(RG, 512 + 128 * i, NT, NE) for i in range(4))
        choice = cut(RC, 4096, NT * TOPK, NE)
        choice_pos = cut(RC, 4608, NT * TOPK, NE)
        gate = sb("gate", [P, KC, NE])
        topv = cut(stat, 64, NT, 8)
        topi = cut(stat, 96, NT, 8).bitcast(U32)
        top_e = stat[:, 128:144]
        top_w = stat[:, 144:160]
        w_sum, w_rs = stat[:, 160:164], stat[:, 164:168]
        top_pos = stat[:, 168:184]
        slot = stat[:, 200:216].bitcast(U32)
        sq, rms_in, rms = stat[:, 216:220], stat[:, 220:224], stat[:, 224:228]
        token = stat[:, 228:260].bitcast(U32)
        token_at = [stat[:, 260 + i:261 + i].bitcast(U32) for i in range(2)]
        token_parts = stat[:, 264:268].bitcast(BF16)
        w3s_loaded, row_loaded, gate_loaded = sem("w3s_loaded"), sem("row_loaded"), sem("gate_loaded")
        ring_loaded = [sem(f"ring_loaded{i}") for i in range(4)]
        sq_ready, rms_ready, hn_ready, h_stored = (sem(n) for n in ("sq_ready", "rms_ready", "hn_ready", "h_stored"))
        logits_ps, mask_ready, pos_ps, places_done = (sem(n) for n in ("logits_ps", "mask_ready", "pos_ps", "places_done"))
        top_shifted, top_exp, onehot_ready, onehot_used, token_ready = (
            sem(n) for n in ("top_shifted", "top_exp", "onehot_ready", "onehot_used", "token_ready"))
        xe_loaded = [sem(f"xe_loaded{i}") for i in range(2)]
        xeT_ps, xeT_ready, gu_ps, sg_ready, act_ready, actT_ps, actT_ready, eo_ps, eo_ready = (
            sem(n) for n in ("xeT_ps", "xeT_ready", "gu_ps", "sg_ready", "act_ready", "actT_ps", "actT_ready", "eo_ps", "eo_ready"))
        eo_stored = [sem(f"eo_stored{i}") for i in range(2)]
        picked_loaded = [sem(f"picked_loaded{i}") for i in range(8)]
        picked_used = sem("picked_used")
        SH = NT
        JOBS = SH + NE

        def act_transpose_pe(pe, j, par):
            pe.wait_ge(act_ready, j + 1)
            for f in range(2):
                i = nc.tensor.transpose(ps[:, 4 + par, f * P:(f + 1) * P], act3[par][:, f * P:(f + 1) * P], ident)
            i.then_inc(actT_ps, 1)

        def rows_transpose_pe(pe, e, par):
            pe.wait_ge(xe_loaded[par], e * 8 + 16 - 8 * par)
            for kc in range(KC):
                i = nc.tensor.transpose(ps[:, par, kc * P:(kc + 1) * P], xe[par][:, kc * P:(kc + 1) * P], ident)
            i.then_inc(xeT_ps, 1)

        def down_pe(pe, j, par, w, first=False):
            pe.wait_ge(actT_ready, j + 1)
            if not first:
                pe.wait_ge(eo_ready, j)
            for f in range(2):
                i = nc.tensor.matmul(ps[:, 6, :], actT[par][:, f, :], w[:, 4 + f, :], start=(f == 0), stop=(f == 1))
            i.then_inc(eo_ps, 1)

        def up_pe(pe, par, w, rows, between=None):
            for kc in range(KC):
                if kc == KC // 2 and between:
                    between()
                i = nc.tensor.matmul(ps[:, 2 + par, :], rows(kc), w[:, kc, :], start=(kc == 0), stop=(kc == KC - 1))
            i.then_inc(gu_ps, 1)

        def expert_step_pe(pe, e, u, w_before, last=False):
            j, par = e + SH, u % 2

            def between():
                act_transpose_pe(pe, j - 1, 1 - par)
                if not last:
                    rows_transpose_pe(pe, e + 1, 1 - par)
            pe.wait_ge(xeT_ready, e + 1)
            pe.wait_ge(ring_loaded[u], e * 4 + 16 - 4 * u)
            pe.wait_ge(act_ready, j - 1)
            up_pe(pe, par, ring[u], lambda kc: xeT[par][:, kc, :], between)
            down_pe(pe, j - 1, 1 - par, w_before)

        def s3_pe(pe):
            xT_pe(pe, 2, hn, hn_ready)
            xT_ready(pe, 2)
            pe.wait_ge(gate_loaded, 16)
            for t in range(NT):
                for kc in range(KC):
                    i = nc.tensor.matmul(ps[:, 7, t * NE:(t + 1) * NE], xT[:, kc, t * P:(t + 1) * P], gate[:, kc, :],
                                         start=(kc == 0), stop=(kc == KC - 1))
            i.then_inc(logits_ps, 1)
            pe.wait_ge(w3s_loaded, 16)

            def shared(j):
                up_pe(pe, j % 2, w3s, lambda kc: xT[:, kc, j * P:(j + 1) * P])
            shared(0)
            pe.wait_ge(mask_ready, 1)
            for t in range(NT):
                for t0 in range(t + 1):
                    i = nc.tensor.matmul(ps[:, 7, t * NE:(t + 1) * NE], before if t0 == t else ones, mask[:, t0, :],
                                         start=(t0 == 0), stop=(t0 == t))
            i.then_inc(pos_ps, 1)
            for j in range(SH):
                if j:
                    act_transpose_pe(pe, j - 1, (j - 1) % 2)
                    down_pe(pe, j - 1, (j - 1) % 2, w3s, first=(j == 1))
                    shared(j)
                for e in range(8 * j, 8 * j + 8):
                    pe.wait_ge(onehot_ready, e + 1)
                    for t in range(NT):
                        i = nc.tensor.matmul(ps[:, 7, 2 * e:2 * e + 2], onehot[e % 2][:, t, :],
                                             token_parts[:, 2 * t:2 * t + 2], start=(t == 0), stop=(t == NT - 1))
                    i.then_inc(onehot_used, 1)
            rows_transpose_pe(pe, 0, 0)
            for e in range(4):
                expert_step_pe(pe, e, e, ring[e - 1] if e else w3s)
            with pe.Fori(0, NE // 4 - 2) as i:
                for u in range(4):
                    expert_step_pe(pe, i * 4 + (4 + u), u, ring[(u - 1) % 4])
            for u in range(4):
                expert_step_pe(pe, NE - 4 + u, u, ring[(u - 1) % 4], last=(u == 3))
            act_transpose_pe(pe, JOBS - 1, 1)
            down_pe(pe, JOBS - 1, 1, ring[3])

        def s3_act(act):
            for t in range(NT):
                norms[2].wait(act, "xn", t + 1)
                nc.scalar.activation(hn[:, t, :], xn[:, t, :], ACT.Square, accum_out=sq[:, t:t + 1]).then_inc(sq_ready, 1)
            xT_act(act, 2)
            act.wait_ge(top_shifted, 1)
            nc.scalar.activation(top_w, top_w, ACT.Exp).then_inc(top_exp, 1)

            def silu(j, par, first=False):
                act.wait_ge(gu_ps, j + 1)
                if not first:
                    act.wait_ge(act_ready, j - 1)
                nc.scalar.activation(sg[par], ps[:, 2 + par, 0:FI], ACT.Silu).then_inc(sg_ready, 1)

            def rows(e, par):
                act.wait_ge(xeT_ps, e + 1)
                nc.scalar.copy(xeT[par].rearrange("p a b -> p (a b)"), ps[:, par, :]).then_inc(xeT_ready, 1)
            for j in range(SH):
                silu(j, j % 2, first=(j < 2))
            rows(0, 0)
            for e in range(4):
                rows(e + 1, 1 - e % 2)
                silu(e + SH, e % 2)
            with act.Fori(0, NE // 4 - 2) as i:
                for u in range(4):
                    rows(i * 4 + (5 + u), 1 - u % 2)
                    silu(i * 4 + (4 + u + SH), u % 2)
            for u in range(4):
                if u < 3:
                    rows(NE - 4 + u + 1, 1 - u % 2)
                silu(NE - 4 + u + SH, u % 2)

        def s3_dve(dve, link):
            norm_dve(dve, link, 2)
            dve.wait_ge(rms_ready, 1)
            dve.wait_ge(row_loaded, 16)
            for t in range(NT):
                nc.vector.scalar_tensor_tensor(hn[:, t, :], xn[:, t, :], rms[:, t:t + 1], row_bias[:], ALU.mult,
                                               ALU.mult).then_inc(hn_ready, 1)
            xT_dve(dve, 2)
            link(nc.vector.tensor_copy(token_parts, cst[:, 4, 64:72]))
            dve.wait_ge(logits_ps, 1)
            link(nc.vector.tensor_copy(logits.rearrange("p t e -> p (t e)"), ps[:, 7, 0:NT * NE]))
            for t in range(NT):
                i = nc.vector.max(topv[:, t, :], logits[:, t, :])
            link(i)
            for t in range(NT):
                i = nc.vector.max_index(topi[:, t, :], topv[:, t, :], logits[:, t, :])
            link(i)
            nc.vector.tensor_tensor(top_w.rearrange("p (t k) -> p t k", k=TOPK), topv[:, :, 0:TOPK],
                                    topv[:, :, 0:1].broadcast_to([P, NT, TOPK]), ALU.subtract).then_inc(top_shifted, 1)
            link(nc.vector.tensor_copy(top_e.rearrange("p (t k) -> p t k", k=TOPK), topi[:, :, 0:TOPK]))
            link(nc.vector.tensor_tensor(choice, iota[:, 0:NE].unsqueeze(1).broadcast_to([P, NT * TOPK, NE]),
                                         top_e.unsqueeze(2).broadcast_to([P, NT * TOPK, NE]), ALU.is_equal))
            nc.vector.tensor_reduce(mask, choice.rearrange("p (t k) e -> p t e k", k=TOPK), AX, ALU.add).then_inc(mask_ready, 1)
            dve.wait_ge(top_exp, 1)
            link(nc.vector.tensor_reduce(w_sum, top_w.rearrange("p (t k) -> p t k", k=TOPK), AX, ALU.add))
            link(nc.vector.reciprocal(w_rs, w_sum))
            link(nc.vector.tensor_tensor(top_w.rearrange("p (t k) -> p t k", k=TOPK),
                                         top_w.rearrange("p (t k) -> p t k", k=TOPK),
                                         w_rs.unsqueeze(2).broadcast_to([P, NT, TOPK]), ALU.mult))
            dve.wait_ge(pos_ps, 1)
            link(nc.vector.tensor_copy(pos.rearrange("p t e -> p (t e)"), ps[:, 7, 0:NT * NE]))
            link(nc.vector.scalar_tensor_tensor(place, pos, 1.0, mask, ALU.add, ALU.mult))
            link(nc.vector.tensor_scalar(place, place, -1.0, None, ALU.add))
            link(nc.vector.tensor_tensor(choice_pos.rearrange("p (t k) e -> p t k e", k=TOPK),
                                         choice.rearrange("p (t k) e -> p t k e", k=TOPK),
                                         pos.unsqueeze(2).broadcast_to([P, NT, TOPK, NE]), ALU.mult))
            link(nc.vector.tensor_reduce(top_pos, choice_pos, AX, ALU.add))
            link(nc.vector.tensor_scalar(top_pos, top_pos, float(CAP - 1), None, ALU.min))
            link(nc.vector.scalar_tensor_tensor(slot, top_e, float(CAP), top_pos, ALU.mult, ALU.add))

            def gated(j, par):
                dve.wait_ge(sg_ready, j + 1)
                nc.vector.tensor_tensor(act3[par], sg[par], ps[:, 2 + par, FI:2 * FI], ALU.mult).then_inc(act_ready, 1)

            def turned(j, par):
                dve.wait_ge(actT_ps, j + 1)
                nc.vector.tensor_copy(actT[par].rearrange("p a b -> p (a b)"), ps[:, 4 + par, 0:2 * P]).then_inc(actT_ready, 1)

            def shared_out(j):
                dve.wait_ge(eo_ps, j + 1)
                if j == 0:
                    dve.wait_ge(x_biased, 2)
                nc.vector.tensor_tensor(x[:, j, :], x[:, j, :], ps[:, 6, :], ALU.add).then_inc(eo_ready, 1)

            def routed_out(e, par, first=False):
                dve.wait_ge(eo_ps, e + (SH + 1))
                if not first:
                    dve.wait_ge(eo_stored[par], e * 8 - 8 * par)
                nc.vector.tensor_copy(eo[par], ps[:, 6, :]).then_inc(eo_ready, 1)

            for j in range(SH):
                gated(j, j % 2)
                for e in range(8 * j, 8 * j + 8):
                    if e >= 2:
                        dve.wait_ge(onehot_used, e - 1)
                    nc.vector.tensor_tensor(onehot[e % 2], iota.unsqueeze(1).broadcast_to([P, NT, P]),
                                            place[:, :, e].unsqueeze(2).broadcast_to([P, NT, P]),
                                            ALU.is_equal).then_inc(onehot_ready, 1)
                if j < SH - 1:
                    turned(j, j % 2)
                    shared_out(j)
            dve.wait_ge(onehot_used, NE)
            token_ps = ps[:, 7, 0:2 * NE].rearrange("p (e a) -> p e a", a=2)
            token_low = stat[:, 300:332]
            link(nc.vector.tensor_copy(token_low, token_ps[:, :, 0]))
            nc.vector.tensor_tensor(token, token_low, token_ps[:, :, 1], ALU.add).then_inc(token_ready, 1)
            for e in range(4):
                turned(e + (SH - 1), 1 - e % 2)
                gated(e + SH, e % 2)
                if e:
                    routed_out(e - 1, 1 - e % 2, first=(e < 3))
                else:
                    shared_out(SH - 1)
            with dve.Fori(0, NE // 4 - 1) as i:
                for u in range(4):
                    turned(i * 4 + (u + 4 + SH - 1), 1 - u % 2)
                    gated(i * 4 + (u + 4 + SH), u % 2)
                    routed_out(i * 4 + (u + 3), 1 - u % 2)
            turned(JOBS - 1, 1)
            routed_out(NE - 1, 1)
            for n in range(NT * TOPK):
                k, t = n // NT, n % NT
                c = t * TOPK + k
                dve.wait_ge(picked_loaded[n % 8], 16 * (n // 8 + 1))
                if n >= NT:
                    dve.wait_ge(picked_used, n - NT + 1)
                nc.vector.scalar_tensor_tensor(x[:, t, :], picked[n % 8], top_w[:, c:c + 1], x[:, t, :], ALU.mult,
                                               ALU.add).then_inc(picked_used, 1)
            dve.wait_ge(picked_used, NT * TOPK)

        def s3_pool(pool, link):
            norm_pool(pool, link, 2)
            pool.wait_ge(sq_ready, NT)
            link(nc.gpsimd.tensor_scalar(rms_in, sq, 1.0 / DM, 1e-6, ALU.mult, ALU.add))
            nc.gpsimd.tensor_tensor(rms, rms_in, power, ALU.pow).then_inc(rms_ready, 1)
            nc.gpsimd.tensor_tensor(x[:], x[:], xn[:], ALU.add).then_inc(x_biased, 1)
            pool.wait_ge(token_ready, 1)
            pool.wait_ge(h_stored, 16)

            def gather(e, par, first=False):
                if not first:
                    pool.wait_ge(xeT_ps, e - 1)
                    pool.wait_ge(xe_loaded[par], e * 8 - 8 * par)
                col = token[:, e:e + 1] if type(e) is int else token[:, bass.ds(e, 1)]
                link(nc.gpsimd.tensor_copy(token_at[par], col))
                nc.gpsimd.tensor_tensor(stat[:, 262:263], power[:, 0:1], power[:, 0:1], ALU.add)
                nc.gpsimd.indirect_dma_start(xe[par], None, scratch["h_rows"],
                                             bass.IndirectOffsetOnAxis(token_at[par], 0)).then_inc(xe_loaded[par], 16)
            for e in range(4):
                gather(e, e % 2, first=(e < 2))
            steps = NE // 4 - 1
            n0 = link.n
            with pool.Fori(0, steps) as i:
                link.base = i * 4
                for u in range(4):
                    gather(i * 4 + (4 + u), u % 2)
            link.n, link.base = n0 + 4 * steps, 0
            for par in range(2):
                pool.wait_ge(eo_stored[par], 16 * NE // 2)
            for n in range(NT * TOPK):
                k, t = n // NT, n % NT
                c = t * TOPK + k
                if n >= 8:
                    pool.wait_ge(picked_used, n - 7)
                nc.gpsimd.indirect_dma_start(picked[n % 8], None, scratch["eo_rows"],
                                             bass.IndirectOffsetOnAxis(slot[:, c:c + 1], 0)).then_inc(picked_loaded[n % 8], 16)

        def s3_loads_early(sp):
            for e in range(2):
                sp.dma_start(ring[e], T["w3"][e]).then_inc(ring_loaded[e], 16)

        def s3_sp(sp):
            sp.wait_ge(x_biased, 1)
            sp.dma_start(row_bias[:], T["norm3"].unsqueeze(0).broadcast_to([P, DM])).then_inc(row_loaded, 16)
            projected[1].wait(sp, "rows", NT)
            sp.dma_start(w3s, T["w3s"]).then_inc(w3s_loaded, 16)
            for e in range(2, 4):
                sp.dma_start(ring[e], T["w3"][e]).then_inc(ring_loaded[e], 16)
            sp.wait_ge(hn_ready, NT)
            sp.dma_start(scratch["h_rows"].rearrange("(t p) h -> p t h", p=P), hn).then_inc(h_stored, 16)
            with sp.Fori(0, NE // 4 - 1) as i:
                for u in range(4):
                    e = i * 4 + u
                    sp.wait_ge(eo_ps, e + (SH + 1))
                    sp.dma_start(ring[u], T["w3"][bass.ds(e + 4, 1)].rearrange("a p c n -> p (a c) n")).then_inc(ring_loaded[u], 16)
                    sp.wait_ge(eo_ready, e + (SH + 1))
                    sp.dma_start(scratch["eo_rows"][bass.ds(e * CAP, CAP), :], eo[u % 2]).then_inc(eo_stored[u % 2], 16)
            if STAGES >= 4:
                s4_sp(sp)
            for e in range(NE - 4, NE):
                sp.wait_ge(eo_ready, e + SH + 1)
                sp.dma_start(scratch["eo_rows"][e * CAP:(e + 1) * CAP, :], eo[e % 2]).then_inc(eo_stored[e % 2], 16)

        w4q = cut(RA, 0, KC, 2048)
        w4kq = cut(RB, 0, NH, 4 * P)
        w4qr = cut(RC, 0, NH // 2, 3 * P)
        w4kr = cut(RC, 3072, NH // 2, P)
        w_abs = [cut(RC, 4096 + 384 * i, 3, P) for i in range(2)]
        q_hk = [cut(RR, 512 * i, TOK) for i in range(2)]
        by_cos = cut(RR, 1024, 3, TOK)
        by_sin = cut(RR, 2560, 3, TOK)
        q_rot = [cut(RR, 4096 + 1536 * i, 3, TOK) for i in range(2)]
        cos_q = cut(RR, 7168, 3, S)
        sin_q = cut(RR, 7360, 3, S)
        q4 = cut(RQ, 0, B, NH * S)
        w4q_loaded, w4kq_loaded, w4r_loaded, rope_q_loaded, rope_k_loaded, w4o_loaded = (
            sem(n) for n in ("w4q_loaded", "w4kq_loaded", "w4r_loaded", "rope_q_loaded", "rope_k_loaded", "w4o_loaded"))
        qhk_ps, qhk_ready, wabs_ps, wabs_ready, qbig_ps, rope_taken, qrot_ready, qabs_ps, qabs_ready = (
            sem(n) for n in ("qhk_ps", "qhk_ready", "wabs_ps", "wabs_ready", "qbig_ps", "rope_taken", "qrot_ready", "qabs_ps", "qabs_ready"))

        def heads4_pe(pe):
            def q_head(h):
                for kc in range(KC):
                    i = nc.tensor.matmul(ps[:, h % 2, :], w4q[:, kc, h * P:(h + 1) * P], xT[:, kc, :],
                                         start=(kc == 0), stop=(kc == KC - 1))
                i.then_inc(qhk_ps, 1)

            def w_product(h):
                if h:
                    pe.wait_ge(wabs_ready, h)
                half = slice(64 * (h // 8), 64 * (h // 8) + R)
                for c in range(3):
                    i = nc.tensor.matmul(ps[:, 2, c * P:(c + 1) * P], w4qr[half, h % 8, c * P:(c + 1) * P],
                                         w4kr[half, h % 8, :], start=True, stop=True)
                i.then_inc(wabs_ps, 1)

            def q_big(h):
                pe.wait_ge(qhk_ready, h + 1)
                if h:
                    pe.wait_ge(rope_taken, h)
                for c in range(4):
                    i = nc.tensor.matmul(ps[:, 4 + c, :], w4kq[:, h, c * P:(c + 1) * P], q_hk[h % 2], start=True, stop=True)
                i.then_inc(qbig_ps, 1)

            def q_abs(h):
                pe.wait_ge(qrot_ready, h + 1)
                pe.wait_ge(wabs_ready, h + 1)
                if h:
                    pe.wait_ge(qabs_ready, h)
                for c in range(3):
                    i = nc.tensor.matmul(ps[:, 3, :], w_abs[h % 2][:, c, :], q_rot[h % 2][:, c, :], start=(c == 0), stop=(c == 2))
                i.then_inc(qabs_ps, 1)
            xT_pe(pe, 3)
            xT_ready(pe, 3)
            pe.wait_ge(w4q_loaded, 16)
            q_head(0)
            pe.wait_ge(w4r_loaded, 32)
            w_product(0)
            pe.wait_ge(w4kq_loaded, 16)
            for h in range(NH):
                if h + 1 < NH:
                    q_head(h + 1)
                    w_product(h + 1)
                q_big(h)
                if h:
                    q_abs(h - 1)
            q_abs(NH - 1)

        def heads4_act(act):
            xT_act(act, 3)

            def q_out(h):
                act.wait_ge(qabs_ps, h + 1)
                nc.scalar.copy(q4[:, :, h * S:(h + 1) * S], by_batch(ps[:, 3, :])).then_inc(qabs_ready, 1)
            for h in range(NH):
                act.wait_ge(qhk_ps, h + 1)
                if h >= 2:
                    act.wait_ge(qbig_ps, h - 1)
                nc.scalar.copy(q_hk[h % 2], ps[:, h % 2, :]).then_inc(qhk_ready, 1)
                act.wait_ge(wabs_ps, h + 1)
                if h >= 2:
                    q_out(h - 2)
                nc.scalar.copy(w_abs[h % 2].rearrange("p c d -> p (c d)"), ps[:, 2, 0:3 * P]).then_inc(wabs_ready, 1)
                for n in range(3 * h, 3 * h + 3):
                    magnitude_act(act, n)
            q_out(NH - 2)
            q_out(NH - 1)

        def heads4_dve(dve, link):
            norm_dve(dve, link, 3)
            xT_dve(dve, 3)
            dve.wait_ge(rope_q_loaded, 16)
            all_batches = [P, 3, B, S]
            for h in range(NH):
                dve.wait_ge(qbig_ps, h + 1)
                if h:
                    dve.wait_ge(qrot_ready, h)
                nc.vector.tensor_tensor(by_cos.rearrange("p c (b s) -> p c b s", s=S),
                                        ps[:, 4:7, :].rearrange("p c (b s) -> p c b s", s=S),
                                        cos_q.unsqueeze(2).broadcast_to(all_batches), ALU.mult)
                for c, partner in ((0, 1), (1, 0), (2, 3)):
                    i = nc.vector.tensor_tensor(by_batch(by_sin[:, c, :]), by_batch(ps[:, 4 + partner, :]),
                                                sin_q[:, c, :].unsqueeze(1).broadcast_to([P, B, S]), ALU.mult)
                i.then_inc(rope_taken, 1)
                dve.wait_ge(rope_taken, h + 1)
                if h >= 2:
                    dve.wait_ge(qabs_ps, h - 1)
                nc.vector.tensor_tensor(q_rot[h % 2], by_cos, by_sin, ALU.add).then_inc(qrot_ready, 1)

        keys = [RA[:, P * LT * i:P * LT * (i + 1)] for i in range(2)]
        p4 = [cut(RA, P * LT * (2 + i), LT, P) for i in range(2)]
        key_max = [cut(RA, P * (4 * LT + i), P) for i in range(2)]
        diag = cut(RA, P * (4 * LT + 2), P)
        shift = cut(RA, P * (4 * LT + 3), P)
        w4kv = cut(RC, 0, NH, P)
        o_rows = [cut(RC, 4864 + P * i, P) for i in range(2)]
        vals = [cut(RE, LT * (DC + 1) * i, LT, DC + 1) for i in range(2)]
        cos_k = cut(RE, 2 * LT * (DC + 1), LT, DC)
        turned_half = cut(RE, 2 * LT * (DC + 1) + LT * DC, 7, DC)
        sin_k = xn[:].rearrange("p a b -> p (a b)")[:, 0:LT * DC].rearrange("p (j d) -> p j d", d=DC)
        o4 = cut(RR, 0, NH, TOK)
        l4 = cut(RQ, 0, NH, TOK)
        w4o = cut(RA, 0, NH, DM)
        row_rs = stat[:, 348:350]
        query_max = stat[:, 340:341]
        last_ps = ps[0:LAST, 6, 0:P]
        turn_ps = ps[:, 6, P:2 * P]
        max_ps = ps[:, 6, P:3 * P]
        o_ps = ps[:, 7, 0:DC + 1]
        keys_at = [ps[:, 7, :], ps[:, 6, 2 * P:4 * P]]
        ctx_loaded = [sem(f"ctx_loaded{i}") for i in range(2)]
        vals_ready, keys_ps, keys_ready, scores4, key_max_ready, max_turned, diag_ready, shift_ps, shift_ready, shifted4, exps4 = (
            sem(n) for n in ("vals_ready", "keys_ps", "keys_ready", "scores4", "key_max_ready", "max_turned", "diag_ready",
                             "shift_ps", "shift_ready", "shifted4", "exps4"))
        o_rows_ps, row_rs_ready, o_rows_ready, o4_ps, o4_ready = (sem(n) for n in ("o_rows_ps", "row_rs_ready", "o_rows_ready", "o4_ps", "o4_ready"))
        l4_ps, l4_act, l4_dve = (sem(n) for n in ("l4_ps", "l4_act", "l4_dve"))
        HP = NH // 2
        SPLIT = 6
        MAXIMA_AFTER = 7
        KEYS = [range(0, 4), range(4, 6), range(6, 10), range(10, 12), range(12, 13)]
        KG = len(KEYS)
        KEYS_AT = {5: (0, 1), 6: (2, 3), 7: (4,)}

        def key_rows(j):
            return P if j < LT - 1 else LAST

        def keys_pe(pe, b, u, g, k=0):
            if g == 0:
                pe.wait_ge(vals_ready, b + 1)
            if type(b) is int and b == 0 and g:
                pe.wait_ge(keys_ready, g)
            for n, j in enumerate(KEYS[g]):
                r = key_rows(j)
                i = nc.tensor.transpose(keys_at[k][:, n * P:n * P + r], vals[u][0:r, j, 0:DC], ident[0:r, 0:r])
            i.then_inc(keys_ps, 1)

        def keys_act(act, b, u, g, k=0):
            act.wait_ge(keys_ps, b * KG + (g + 1))
            at, w = P * KEYS[g][0], P * len(KEYS[g]) if g < KG - 1 else LAST
            nc.scalar.copy(keys[u][:, at:at + w], keys_at[k][:, 0:w]).then_inc(keys_ready, 1)

        def turn_out_pe(pe, n, par):
            pe.wait_ge(o_rows_ready, n + 1)
            nc.tensor.transpose(turn_ps, o_rows[par], ident).then_inc(o4_ps, 1)

        def values_pe(pe, n, u, par, js):
            if 0 in js:
                pe.wait_ge(exps4, n * 2 + 1)
            for j in js:
                if j == SPLIT:
                    pe.wait_ge(exps4, n * 2 + 2)
                r = key_rows(j)
                i = nc.tensor.matmul(o_ps, p4[par][0:r, j, :], vals[u][0:r, j, :], start=(j == 0), stop=(j == LT - 1))
            if LT - 1 in js:
                i.then_inc(o_rows_ps, 1)

        def tile_pe(pe, b, u, hp, back=2, more=True):
            n, par = b * HP + hp, hp % 2
            turns = KEYS_AT.get(hp, ()) if more else ()
            before = (n - 1, u if hp else 1 - u, 1 - par)
            if hp == 0:
                pe.wait_ge(keys_ready, b * KG + KG)
            if back >= 2:
                pe.wait_ge(shifted4, n * 3 - 3)
            q = q4[:, b, hp * P:(hp + 1) * P] if type(b) is int else q4[:, bass.ds(b, 1), hp * P:(hp + 1) * P].rearrange("p a n -> p (a n)")
            for j in range(LT - 1):
                i = nc.tensor.matmul(ps[:, 3 * par + j // 4, (j % 4) * P:(j % 4 + 1) * P], keys[u][:, j * P:(j + 1) * P], q,
                                     start=True, stop=True)
                if j == 7:
                    i.then_inc(scores4, 1)
                if j == 3 and turns:
                    pe.wait_ge(o_rows_ready, n - 1)
                    keys_pe(pe, b + 1, 1 - u, turns[0], 0)
                if j == 4 and back >= 2:
                    pe.wait_ge(shifted4, n * 3 - 2)
                    if turns[1:]:
                        keys_pe(pe, b + 1, 1 - u, turns[1], 1)
                    turn_out_pe(pe, n - 2, par)
            if back >= 1:
                pe.wait_ge(shifted4, n * 3 - 2)
            if back >= 2:
                pe.wait_ge(o4_ready, n - 1)
            if turns:
                pe.wait_ge(keys_ready, b * KG + (KG + turns[-1] + 1))
            nc.tensor.matmul(last_ps, keys[u][:, LCTX - LAST:LCTX], q, start=True, stop=True).then_inc(scores4, 1)
            if back >= 1:
                values_pe(pe, *before, range(0, MAXIMA_AFTER))
            pe.wait_ge(key_max_ready, n + 1)
            nc.tensor.transpose(max_ps[:, 0:P], key_max[0], ident)
            nc.tensor.transpose(max_ps[:, P:2 * P], key_max[1], ident).then_inc(max_turned, 1)
            if back >= 1:
                values_pe(pe, *before, range(MAXIMA_AFTER, LT))
            pe.wait_ge(diag_ready, n + 1)
            nc.tensor.matmul(turn_ps, ones, diag, start=True, stop=True).then_inc(shift_ps, 1)

        def head_out_act(act, b, hp):
            act.wait_ge(o4_ps, b * HP + (hp + 1))
            nc.scalar.activation(o4[:, 2 * hp:2 * hp + 2, bass.ds(b * S, S)], turn_ps.rearrange("p (u s) -> p u s", s=S),
                                 ACT.Copy).then_inc(o4_ready, 1)

        def tile_act(act, b, u, hp, back=2, more=True):
            n, par = b * HP + hp, hp % 2
            turns = KEYS_AT.get(hp + 1, ()) if more else ()
            if type(b) is int and n in ROUND_AT:
                round_act(act, ROUND_AT[n])
            act.wait_ge(shift_ps, n + 1)
            nc.scalar.copy(shift, turn_ps).then_inc(shift_ready, 1)
            if back >= 1:
                rows_out_act(act, n - 1, 1 - par)
            for k, g in enumerate(turns[0:1]):
                keys_act(act, b + 1, 1 - u, g, k)
            act.wait_ge(shifted4, n * 3 + 2)
            nc.scalar.activation(p4[par][:, 0:SPLIT, :], p4[par][:, 0:SPLIT, :], ACT.Exp)
            nc.scalar.activation(p4[par][0:LAST, LT - 1, :], p4[par][0:LAST, LT - 1, :], ACT.Exp).then_inc(exps4, 1)
            if back >= 1:
                head_out_act(act, b if hp >= 1 else b - 1, (hp - 1) % HP)
            for k, g in enumerate(turns[1:]):
                keys_act(act, b + 1, 1 - u, g, k + 1)
            act.wait_ge(shifted4, n * 3 + 3)
            nc.scalar.activation(p4[par][:, SPLIT:LT - 1, :], p4[par][:, SPLIT:LT - 1, :], ACT.Exp).then_inc(exps4, 1)
            if type(b) is int and n in ROUND_AT:
                ternary_act(act, ROUND_AT[n])

        def sums_dve(dve, n, par):
            dve.wait_ge(o_rows_ps, n + 1)
            nc.vector.reciprocal(row_rs[:, par:par + 1], o_ps[:, DC:DC + 1]).then_inc(row_rs_ready, 1)

        def rows_out_act(act, n, par):
            act.wait_ge(row_rs_ready, n + 1)
            nc.scalar.activation(o_rows[par], o_ps[:, 0:DC], ACT.Copy, scale=row_rs[:, par:par + 1]).then_inc(o_rows_ready, 1)

        def tile_dve(dve, link, b, u, hp, back=2):
            n, par = b * HP + hp, hp % 2
            scores = ps[:, 3 * par:3 * par + 3, :].rearrange("p a (j q) -> p (a j) q", q=P)
            by_query = scores.rearrange("p j q -> p q j")
            if back >= 1:
                dve.wait_ge(max_turned, n)
            dve.wait_ge(scores4, n * 2 + 1)
            nc.vector.tensor_reduce(key_max[0], by_query[:, :, 0:8], AX, ALU.max)
            dve.wait_ge(scores4, n * 2 + 2)
            link(nc.vector.tensor_reduce(key_max[1], by_query[:, :, 8:LT - 1], AX, ALU.max))
            nc.vector.tensor_tensor(key_max[1][0:LAST], key_max[1][0:LAST], last_ps, ALU.max).then_inc(key_max_ready, 1)
            if type(b) is int and n in ROUND_AT:
                clip_dve(dve, ROUND_AT[n])
            dve.wait_ge(max_turned, n + 1)
            link(nc.vector.tensor_reduce(query_max, max_ps, AX, ALU.max))
            nc.vector.tensor_scalar(diag, ident, query_max, None, ALU.mult).then_inc(diag_ready, 1)
            if back >= 1:
                sums_dve(dve, n - 1, 1 - par)
            dve.wait_ge(shift_ready, n + 1)
            if back >= 2:
                dve.wait_ge(o_rows_ps, n - 1)
            nc.vector.tensor_tensor(p4[par][0:LAST, LT - 1, :], last_ps, shift[0:LAST], ALU.subtract).then_inc(shifted4, 1)
            for j0, j1 in ((0, SPLIT), (SPLIT, LT - 1)):
                nc.vector.tensor_tensor(p4[par][:, j0:j1, :], scores[:, j0:j1, :],
                                        shift.unsqueeze(1).broadcast_to([P, j1 - j0, P]), ALU.subtract).then_inc(shifted4, 1)

        def all_tiles(eng, tile, links=None):
            for u in range(2):
                for hp in range(HP):
                    tile(u, u, hp, back=min(2, u * HP + hp))
            n0 = links.n if links else 0
            per = LINKS * 2 * HP
            with eng.Fori(0, B // 2 - 2) as i:
                if links:
                    links.base = i * per
                for u in range(2):
                    for hp in range(HP):
                        tile(i * 2 + (2 + u), u, hp)
            if links:
                assert links.n == n0 + per
                links.n, links.base = n0 + per * (B // 2 - 2), 0
            for u in range(2):
                for hp in range(HP):
                    tile(B - 2 + u, u, hp, **({"more": False} if u and not links else {}))
        LINKS = 2

        def s4_pe(pe):
            heads4_pe(pe)
            pe.wait_ge(qabs_ready, NH)
            weight_scales_pe(pe)
            for g in range(KG):
                keys_pe(pe, 0, 0, g)
            all_tiles(pe, lambda b, u, hp, **kw: tile_pe(pe, b, u, hp, **kw))
            n = B * HP
            pe.wait_ge(shifted4, n * 3 - 2)
            turn_out_pe(pe, n - 2, 0)
            values_pe(pe, n - 1, 1, 1, range(LT))
            pe.wait_ge(o4_ready, n - 1)
            turn_out_pe(pe, n - 1, 1)
            pe.wait_ge(o4_ready, n)
            pe.wait_ge(w4r_loaded, 48)
            for h in range(NH):
                if h >= 8:
                    pe.wait_ge(l4_dve if h % 2 else l4_act, (h - 8) // 2 + 1)
                nc.tensor.matmul(ps[:, h % 8, :], w4kv[:, h, :], o4[:, h, :], start=True, stop=True).then_inc(l4_ps, 1)
            pe.wait_ge(l4_act, NH // 2)
            pe.wait_ge(l4_dve, NH // 2)
            pe.wait_ge(w4o_loaded, 16)
            for t in range(NT):
                for h in range(NH):
                    i = nc.tensor.matmul(ps[:, t, :], l4[:, h, t * P:(t + 1) * P], w4o[:, h, :],
                                         start=(h == 0), stop=(h == NH - 1))
                i.then_inc(projected[2]["rows"], 1)

        def s4_act(act):
            heads4_act(act)
            for g in range(KG):
                keys_act(act, 0, 0, g)
            all_tiles(act, lambda b, u, hp, **kw: tile_act(act, b, u, hp, **kw))
            rows_out_act(act, B * HP - 1, 1)
            head_out_act(act, B - 1, HP - 1)
            for h in range(0, NH, 2):
                act.wait_ge(l4_ps, h + 1)
                nc.scalar.copy(l4[:, h, :], ps[:, h % 8, :]).then_inc(l4_act, 1)

        def s4_dve(dve, link):
            heads4_dve(dve, link)
            weight_scales_dve(dve, link)
            all_tiles(dve, lambda b, u, hp, **kw: tile_dve(dve, link, b, u, hp, **kw), link)
            n = B * HP
            sums_dve(dve, n - 1, 1)
            for h in range(1, NH, 2):
                dve.wait_ge(l4_ps, h + 1)
                nc.vector.tensor_copy(l4[:, h, :], ps[:, h % 8, :]).then_inc(l4_dve, 1)
            for t in range(NT):
                projected[2].wait(dve, "rows", t + 1)
                link(nc.vector.tensor_tensor(x[:, t, :], x[:, t, :], ps[:, t, :], ALU.add))

        def s4_pool(pool, link):
            norm_pool(pool, link, 3)
            pool.wait_ge(rope_k_loaded, 32)

            def batch(b, u, first=False):
                pool.wait_ge(ctx_loaded[u], b * 16 + 32 - 16 * u)
                v = vals[u]
                if first:
                    nc.gpsimd.memset(v[:, :, DC:DC + 1], 1.0)
                for j0, j1 in ((0, 7), (7, LT)):
                    half, n = turned_half[:, 0:j1 - j0, :], DC // 2
                    part = v[:, j0:j1, 0:DC]
                    link(nc.gpsimd.tensor_tensor(half[:, :, 0:n], part[:, :, n:DC], sin_k[:, j0:j1, 0:n], ALU.mult))
                    link(nc.gpsimd.tensor_tensor(half[:, :, n:DC], part[:, :, 0:n], sin_k[:, j0:j1, n:DC], ALU.mult))
                    link(nc.gpsimd.tensor_tensor(part, part, cos_k[:, j0:j1, :], ALU.mult))
                    i = nc.gpsimd.tensor_tensor(part, part, half, ALU.add)
                    if j0 == 0:
                        link(i)
                i.then_inc(vals_ready, 1)
                pool.wait_ge(vals_ready, b + 1)
            for u in range(2):
                batch(u, u, first=True)
            n0, per = link.n, 2 * 7
            with pool.Fori(0, B // 2 - 1) as i:
                link.base = i * per
                for u in range(2):
                    batch(i * 2 + (2 + u), u)
            assert link.n == n0 + per
            link.n, link.base = n0 + per * (B // 2 - 1), 0

        def ctx_rows(b):
            rows = T["ctx"][b] if type(b) is int else T["ctx"][bass.ds(b, 1)].rearrange("a l d -> (a l) d")
            return (rows[0:(LT - 1) * P, :].rearrange("(j p) d -> p j d", p=P), rows[(LT - 1) * P:LCTX, :])

        def ctx_sp(sp, b, u):
            full, rest = ctx_rows(b)
            sp.dma_start(vals[u][:, 0:LT - 1, 0:DC], full).then_inc(ctx_loaded[u], 16)
            sp.dma_start(vals[u][0:LAST, LT - 1, 0:DC], rest).then_inc(ctx_loaded[u], 16)

        def s4_loads_early(sp):
            sp.wait_ge(q2_ps, NH)
            sp.dma_start(w4q, T["w4q"]).then_inc(w4q_loaded, 16)

        def s4_sp(sp):
            sp.dma_start(w4qr, T["w4qr"]).then_inc(w4r_loaded, 16)
            sp.dma_start(w4kr, T["w4kr"]).then_inc(w4r_loaded, 16)
            sp.dma_start(w4kq, T["w4kq"]).then_inc(w4kq_loaded, 16)

        def s4_sp_main(sp):
            sp.wait_ge(picked_used, NT * TOPK)
            sp.dma_start(RR[:, 7168:7168 + 6 * S], T["rope_q"]).then_inc(rope_q_loaded, 16)
            for u in range(2):
                ctx_sp(sp, u, u)
            sp.dma_start(cos_k, T["rope_k"][0]).then_inc(rope_k_loaded, 16)
            norms[3].wait(sp, "xT_ps", KC)
            sp.dma_start(sin_k, T["rope_k"][1]).then_inc(rope_k_loaded, 16)
            for n in range(MAG):
                if n >= 2:
                    sp.wait_ge(magnitudes_taken, n - 1)
                sp.dma_start(mag[n % 2], T["w6"][:, n * MAGW:(n + 1) * MAGW]).then_inc(mag_loaded[n % 2], 16)
            sp.wait_ge(qbig_ps, NH)
            sp.dma_start(w4kv, T["w4kv"]).then_inc(w4r_loaded, 16)
            sp.wait_ge(magnitudes_taken, MAG)
            for m in range(0, 11):
                raw_sp(sp, m)
            for u in range(2):
                sp.wait_ge(o_rows_ps, 8 + 8 * u)
                ctx_sp(sp, 2 + u, u)
                if u == 0:
                    for m in range(11, 19):
                        raw_sp(sp, m)
            with sp.Fori(0, B // 2 - 2) as i:
                for u in range(2):
                    sp.wait_ge(o_rows_ps, i * 16 + (24 + 8 * u))
                    ctx_sp(sp, i * 2 + (4 + u), u)
            for m in range(19, RAW):
                raw_sp(sp, m)
            sp.wait_ge(o_rows_ps, B * HP)
            sp.dma_start(w4o, T["w4o"]).then_inc(w4o_loaded, 16)

        w5 = cut(RE, 0, 3, KC * DM).rearrange("p w (c n) -> p w c n", n=DM)
        w5o = cut(RC, 0, KC, DM)
        b5q, b5k, b5v = (vecs[:, 18 + 4 * i:22 + 4 * i] for i in range(3))
        H5 = H1.again()
        w5_loaded, b5_loaded = sem("w5_loaded"), sem("b5_loaded")
        v5_act, v5_dve, v5_swapped = (sem(n) for n in ("v5_act", "v5_dve", "v5_swapped"))

        def s5_pe(pe):
            xT_pe(pe, 4)
            xT_ready(pe, 4)
            pe.wait_ge(w5_loaded, 16)
            for t in range(NT):
                for kc in range(KC):
                    i = nc.tensor.matmul(ps[:, 4 + t, :], xT[:, kc, t * P:(t + 1) * P], w5[:, 2, kc, :],
                                         start=(kc == 0), stop=(kc == KC - 1))
                i.then_inc(H5["v_ps"], 1)
            for which, base, done in ((0, 0, H5["q_ps"]), (1, 4, H5["k_ps"])):
                for c in range(KC):
                    if which:
                        pe.wait_ge(v5_act, c + 1)
                        pe.wait_ge(v5_dve, c + 1)
                    for kc in range(KC):
                        i = nc.tensor.matmul(ps[:, base + c, :], w5[:, which, kc, c * P:(c + 1) * P], xT[:, kc, :],
                                             start=(kc == 0), stop=(kc == KC - 1))
                    i.then_inc(done, 1)
            heads_pe(pe, H5, w5o, lambda: [pe.wait_ge(v5_swapped, 32), pe.wait_ge(w5_loaded, 32)], projected[3])

        def v5_half(u, t):
            own = slice(64 * u, 64 * u + S)
            return mh_v[own, 2 * t + u, :], ps[own, 4 + t, :]

        def s5_act(act):
            xT_act(act, 4)
            for t in range(NT):
                H5.wait(act, "v_ps", t + 1)
                nc.scalar.copy(*v5_half(0, t)).then_inc(v5_act, 1)
            act.wait_ge(b5_loaded, 16)
            for c in range(KC):
                H5.wait(act, "q_ps", c + 1)
                nc.scalar.activation(mh_q[:, c, :], ps[:, c, :], ACT.Identity, bias=b5q[:, c:c + 1]).then_inc(H5["q"], 1)
            heads_act(act, H5, b5v)

        def s5_dve(dve, link):
            norm_dve(dve, link, 4)
            xT_dve(dve, 4)
            for t in range(NT):
                H5.wait(dve, "v_ps", t + 1)
                nc.vector.tensor_copy(*v5_half(1, t)).then_inc(v5_dve, 1)
            dve.wait_ge(b5_loaded, 16)
            for c in range(KC):
                H5.wait(dve, "k_ps", c + 1)
                nc.vector.tensor_scalar(mh_k[:, c, :], ps[:, 4 + c, :], b5k[:, c:c + 1], None, ALU.add).then_inc(H5["k"], 1)
            heads_dve(dve, link, H5, False)
            dve.wait_ge(x_biased, 3)
            for t in range(NT):
                projected[3].wait(dve, "rows", t + 1)
                link(nc.vector.tensor_tensor(x[:, t, :], x[:, t, :], ps[:, 4 + t, :], ALU.add))

        def s5_pool(pool, link):
            norm_pool(pool, link, 4)
            norms[4].wait(pool, "xn", NT)
            pool.wait_ge(row_loaded, 32)
            nc.gpsimd.tensor_tensor(x[:], x[:], row_bias[:].unsqueeze(1).broadcast_to([P, NT, DM]), ALU.add).then_inc(x_biased, 1)

        def s5_sp(sp):
            sp.wait_ge(row_loaded, 16)
            sp.wait_ge(hn_ready, NT)
            sp.dma_start(row_bias[:], T["b5o"].unsqueeze(0).broadcast_to([P, DM])).then_inc(row_loaded, 16)
            sp.dma_start(vecs[:, 18:30], T["vec5"]).then_inc(b5_loaded, 16)
            sp.dma_start(RE[:], T["w5"][:, 0:3 * KC * DM]).then_inc(w5_loaded, 16)
            sp.wait_ge(w5_loaded, 16)
            sp.wait_ge(l4_ps, NH)
            sp.dma_start(RC[:, 0:KC * DM], T["w5"][:, 3 * KC * DM:]).then_inc(w5_loaded, 16)

        def s5_sp_swap(sp):
            sp.wait_ge(v5_act, NT)
            sp.wait_ge(v5_dve, NT)
            pairs = mh_v.rearrange("p (t u) d -> p u t d", u=2)
            for u in range(2):
                sp.dma_start(pairs[64 * (1 - u):64 * (1 - u) + S, u], pairs[64 * u:64 * u + S, u]).then_inc(v5_swapped, 16)

        WGU, WDN = KC * 2 * FF, FF * DM // P
        MAG = 48
        MAGW = (WGU + WDN) // MAG
        MAG_GU = WGU // MAGW
        RAW = 24
        RAWW = (WGU + WDN) // RAW
        RAW_GU = WGU // RAWW
        ROUND_AT = {m if m < RAW_GU else (B - 2) * HP + m - RAW_GU: m for m in range(RAW)}
        mag = [cut(RG, MAGW * i, MAGW) for i in range(2)]
        raw = [cut(RB, WGU // 2 + RAWW * i, RAWW) for i in range(3)]
        mag_sum = stat[:, 350:350 + MAG]
        mag_total, w_mean, w_scale = stat[:, 400:402], stat[:, 494:496], stat[:, 492:494]
        ident16 = stat[:, 402:466].bitcast(BF16)
        w6gu = RB[:, 0:WGU // 2].bitcast(BF16)
        w6d = RC[:, 2048:2048 + WDN // 2].bitcast(BF16)
        mag_loaded = ring_loaded[0:2]
        raw_loaded = ring_loaded[1:4]
        BEFORE_MAG = 16 * NE // 4
        BEFORE_RAW = [BEFORE_MAG + 16 * MAG // 2, BEFORE_MAG, BEFORE_MAG]
        magnitudes_taken, mag_total_ready, mag_ps, w_scale_ready, rounded, clipped, ternary_ready = (
            sem(n) for n in ("magnitudes_taken", "mag_total_ready", "mag_ps", "w_scale_ready", "rounded", "clipped", "ternary_ready"))
        ROUND = 1.5 * 2.0 ** 23

        def magnitude_act(act, n):
            act.wait_ge(mag_loaded[n % 2], BEFORE_MAG + 16 * (n // 2 + 1))
            nc.scalar.activation(mag[n % 2], mag[n % 2], ACT.Abs, accum_out=mag_sum[:, n:n + 1]).then_inc(magnitudes_taken, 1)

        def weight_scales_pe(pe):
            pe.wait_ge(mag_total_ready, 1)
            nc.tensor.matmul(ps[:, 3, 0:2], ones, mag_total, start=True, stop=True).then_inc(mag_ps, 1)
            pe.wait_ge(w_scale_ready, 1)

        def weight_scales_dve(dve, link):
            dve.wait_ge(magnitudes_taken, MAG)
            nc.vector.memset(round_up, ROUND)
            nc.vector.memset(round_down, -ROUND)
            nc.vector.tensor_reduce(mag_total[:, 0:1], mag_sum[:, 0:MAG_GU], AX, ALU.add)
            link(nc.vector.tensor_reduce(mag_total[:, 1:2], mag_sum[:, MAG_GU:MAG], AX, ALU.add))
            nc.vector.tensor_copy(ident16, ident).then_inc(mag_total_ready, 1)
            dve.wait_ge(mag_ps, 1)
            nc.vector.tensor_scalar(w_mean[:, 0:1], ps[:, 3, 0:1], 1.0 / (P * WGU), 1e-5, ALU.mult, ALU.max)
            link(nc.vector.tensor_scalar(w_mean[:, 1:2], ps[:, 3, 1:2], 1.0 / (P * WDN), 1e-5, ALU.mult, ALU.max))
            nc.vector.reciprocal(w_scale, w_mean).then_inc(w_scale_ready, 1)

        def raw_sp(sp, m):
            if m >= 3:
                sp.wait_ge(ternary_ready, m - 2)
            sp.dma_start(raw[m % 3], T["w6"][:, m * RAWW:(m + 1) * RAWW]).then_inc(raw_loaded[m % 3], 16)

        round_up, round_down = stat[:, 350 + MAG:351 + MAG], stat[:, 351 + MAG:352 + MAG]

        def round_act(act, m):
            i = int(m >= RAW_GU)
            act.wait_ge(w_scale_ready, 1)
            act.wait_ge(raw_loaded[m % 3], BEFORE_RAW[m % 3] + 16 * (m // 3 + 1))
            nc.scalar.activation(raw[m % 3], raw[m % 3], ACT.Identity, bias=round_up, scale=w_scale[:, i:i + 1]).then_inc(rounded, 1)

        def clip_dve(dve, m):
            dve.wait_ge(rounded, m + 1)
            nc.vector.tensor_scalar(raw[m % 3], raw[m % 3], ROUND - 1.0, ROUND + 1.0, ALU.max, ALU.min).then_inc(clipped, 1)

        def ternary_act(act, m):
            act.wait_ge(clipped, m + 1)
            dst = w6gu[:, m * RAWW:(m + 1) * RAWW] if m < RAW_GU else w6d[:, (m - RAW_GU) * RAWW:(m - RAW_GU + 1) * RAWW]
            nc.scalar.activation(dst, raw[m % 3], ACT.Identity, bias=round_down).then_inc(ternary_ready, 1)

        def s6_pool(pool, link):
            norm_pool(pool, link, 5)
            pool.wait_ge(sq_ready, 2 * NT)
            link(nc.gpsimd.tensor_scalar(rms_in, sq, 1.0 / DM, 1e-5, ALU.mult, ALU.add))
            nc.gpsimd.tensor_tensor(rms, rms_in, power, ALU.pow).then_inc(rms_ready, 1)

        h6 = cut(RR, 0, NT, DM)
        xq = RR[:, 2048:3072].bitcast(BF16).rearrange("p (t n) -> p t n", t=NT)
        xqT = RR[:, 3072:4096].bitcast(BF16).rearrange("p (c n) -> p c n", c=KC)
        relu6 = [cut(RQ, 512 * i, 512) for i in range(2)]
        relu2 = [cut(RQ, 1024 + 512 * i, 512) for i in range(2)]
        hid = [cut(RQ, 2048 + FF * i, FF) for i in range(2)]
        hq = [RQ[:, 4864 + FF // 2 * i:4864 + FF // 2 * (i + 1)].bitcast(BF16) for i in range(2)]
        FC = FF // P
        hqT = [RQ[:, 6272 + FF // 2 * i:6272 + FF // 2 * (i + 1)].bitcast(BF16).rearrange("p (c n) -> p c n", n=P) for i in range(2)]
        top6, scale6, alpha6 = stat[:, 466:470], stat[:, 470:474], stat[:, 474:478]
        toph, scaleh, deltah = stat[:, 478:482], stat[:, 482:486], stat[:, 486:490]
        PIECE6 = [(512 * i, min(512, FF - 512 * i)) for i in range(3)]
        xq_ready, xqT_ps, xqT_ready, alpha_ready, gu6_ps, relu_ready, hid_ready, hq_ready, hqT_ps, hqT_ready, down6_ps = (
            sem(n) for n in ("xq_ready", "xqT_ps", "xqT_ready", "alpha_ready", "gu6_ps", "relu_ready",
                             "hid_ready", "hq_ready", "hqT_ps", "hqT_ready", "down6_ps"))

        def s6_pe(pe):
            pe.wait_ge(xq_ready, NT)
            for kc in range(KC):
                bank = ps[:, kc, :].bitcast(BF16)
                for t in range(NT):
                    i = nc.tensor.transpose(bank[:, t * P:(t + 1) * P], xq[:, t, kc * P:(kc + 1) * P], ident16)
                i.then_inc(xqT_ps, 1)
            pe.wait_ge(xqT_ready, KC)
            pe.wait_ge(ternary_ready, RAW)

            def down(t):
                pe.wait_ge(hq_ready, t + 1)
                for c in range(FC):
                    bank = ps[:, 4 + c // 8, :].bitcast(BF16)
                    i = nc.tensor.transpose(bank[:, (c % 8) * P:(c % 8 + 1) * P], hq[t % 2][:, c * P:(c + 1) * P], ident16)
                i.then_inc(hqT_ps, 1)
                pe.wait_ge(hqT_ready, t + 1)
                if t:
                    pe.wait_ge(x_final, t)
                for c in range(FC):
                    i = nc.tensor.matmul(ps[:, 6, :], hqT[t % 2][:, c, :], w6d[:, c * DM:(c + 1) * DM],
                                         start=(c == 0), stop=(c == FC - 1))
                i.then_inc(down6_ps, 1)
            for t in range(NT):
                for n, (at, w) in enumerate(PIECE6):
                    m = 3 * t + n
                    if m >= 2:
                        pe.wait_ge(hid_ready, m - 1)
                    for up in range(2):
                        for kc in range(KC):
                            col = (2 * kc + up) * FF + at
                            i = nc.tensor.matmul(ps[:, 2 * (m % 2) + up, 0:w], xqT[:, kc, t * P:(t + 1) * P], w6gu[:, col:col + w],
                                                 start=(kc == 0), stop=(kc == KC - 1))
                    i.then_inc(gu6_ps, 1)
                if t:
                    down(t - 1)
            down(NT - 1)

        def s6_act(act):
            for t in range(NT):
                norms[5].wait(act, "xn", t + 1)
                nc.scalar.activation(h6[:, t, :], xn[:, t, :], ACT.Square, accum_out=sq[:, t:t + 1]).then_inc(sq_ready, 1)
            act.wait_ge(alpha_ready, 1)
            for m in range(3 * NT):
                t, w = m // 3, PIECE6[m % 3][1]
                act.wait_ge(gu6_ps, m + 1)
                if m >= 2:
                    act.wait_ge(hid_ready, m - 1)
                    act.wait_ge(relu_ready, m - 1)
                nc.scalar.activation(relu6[m % 2][:, 0:w], ps[:, 2 * (m % 2), 0:w], ACT.Relu, scale=alpha6[:, t:t + 1]).then_inc(relu_done, 1)
                act.wait_ge(relu_done, m + 1)
                nc.scalar.activation(relu2[m % 2][:, 0:w], relu6[m % 2][:, 0:w], ACT.Square).then_inc(relu_ready, 1)

        relu_done = sem("relu_done")

        def quantise(link, dst, v, scale, last):
            link(nc.vector.tensor_scalar(v, v, scale, 127.0, ALU.mult, ALU.min))
            link(nc.vector.tensor_scalar(v, v, -128.0, ROUND, ALU.max, ALU.add))
            nc.vector.tensor_scalar(dst, v, -ROUND, None, ALU.add).then_inc(last, 1)

        def s6_dve(dve, link):
            norm_dve(dve, link, 5)
            dve.wait_ge(rms_ready, 2)
            dve.wait_ge(row_loaded, 48)
            for t in range(NT):
                i = nc.vector.scalar_tensor_tensor(h6[:, t, :], xn[:, t, :], rms[:, t:t + 1], row_bias[:], ALU.mult, ALU.mult)
            link(i)
            link(nc.vector.tensor_reduce(top6, h6, AX, ALU.max, apply_absolute_value=True))
            link(nc.vector.tensor_scalar(top6, top6, 1e-5, None, ALU.max))
            link(nc.vector.reciprocal(scale6, top6))
            link(nc.vector.tensor_scalar(scale6, scale6, 127.0, None, ALU.mult))
            nc.vector.tensor_scalar(alpha6, top6, 1.0 / 127.0, w_mean[:, 0:1], ALU.mult, ALU.mult).then_inc(alpha_ready, 1)
            for t in range(NT):
                quantise(link, xq[:, t, :], h6[:, t, :], scale6[:, t:t + 1], xq_ready)
            for kc in range(KC):
                dve.wait_ge(xqT_ps, kc + 1)
                nc.vector.tensor_copy(xqT[:, kc, :], ps[:, kc, :].bitcast(BF16)[:, 0:TOK]).then_inc(xqT_ready, 1)
            dve.wait_ge(alpha_ready, 1)

            def down(t):
                dve.wait_ge(hqT_ps, t + 1)
                flat = hqT[t % 2].rearrange("p c n -> p (c n)")
                nc.vector.tensor_copy(flat[:, 0:8 * P], ps[:, 4, :].bitcast(BF16))
                nc.vector.tensor_copy(flat[:, 8 * P:FF], ps[:, 5, :].bitcast(BF16)[:, 0:FF - 8 * P]).then_inc(hqT_ready, 1)
                dve.wait_ge(down6_ps, t + 1)
                nc.vector.scalar_tensor_tensor(x[:, t, :], ps[:, 6, :], deltah[:, t:t + 1], x[:, t, :], ALU.mult,
                                               ALU.add).then_inc(x_final, 1)
            for t in range(NT):
                v = hid[t % 2]
                for n, (at, w) in enumerate(PIECE6):
                    m = 3 * t + n
                    dve.wait_ge(relu_ready, m + 1)
                    nc.vector.scalar_tensor_tensor(v[:, at:at + w], ps[:, 2 * (m % 2) + 1, 0:w], alpha6[:, t:t + 1],
                                                   relu2[m % 2][:, 0:w], ALU.mult, ALU.mult).then_inc(hid_ready, 1)
                dve.wait_ge(hid_ready, 3 * t + 3)
                link(nc.vector.tensor_reduce(toph[:, t:t + 1], v, AX, ALU.max, apply_absolute_value=True))
                link(nc.vector.tensor_scalar(toph[:, t:t + 1], toph[:, t:t + 1], 1e-5, None, ALU.max))
                link(nc.vector.reciprocal(scaleh[:, t:t + 1], toph[:, t:t + 1]))
                link(nc.vector.tensor_scalar(scaleh[:, t:t + 1], scaleh[:, t:t + 1], 127.0, None, ALU.mult))
                link(nc.vector.tensor_scalar(deltah[:, t:t + 1], toph[:, t:t + 1], 1.0 / 127.0, w_mean[:, 1:2], ALU.mult, ALU.mult))
                quantise(link, hq[t % 2], v, scaleh[:, t:t + 1], hq_ready)
                if t:
                    down(t - 1)
            down(NT - 1)

        def s6_sp(sp):
            s5_sp_swap(sp)
            sp.wait_ge(x_biased, 3)
            sp.dma_start(row_bias[:], T["norm6"].unsqueeze(0).broadcast_to([P, DM])).then_inc(row_loaded, 16)

        block = ctx.enter_context(nc.Block())

        @block.sync
        def _(sp):
            sp.dma_start(x[:], T["x"].rearrange("b s h -> (b s) h").rearrange("(t p) h -> p t h", p=P)).then_inc(x_loaded, 16)
            sp.dma_start(cst[:], T["cst"]).then_inc(cst_loaded, 16)
            c64_rows = T["ctx"][:, 0:S, :].rearrange("b l d -> l b d")
            for u in range(2):
                sp.dma_start(c64[64 * u:64 * u + S, :, :], c64_rows).then_inc(c64_loaded, 16)
            sp.dma_start(w1kv, T["w1kv"]).then_inc(w1_loaded, 16)
            sp.dma_start(w1q, T["w1q"]).then_inc(w1q_loaded, 16)
            sp.dma_start(w1o, T["w1o"]).then_inc(w1o_loaded, 16)
            sp.dma_start(vecs[:, 0:18], T["vec2"]).then_inc(w2_loaded, 16)
            sp.dma_start(w2kv, T["w2kv"]).then_inc(w2_loaded, 16)
            sp.dma_start(w2q, T["w2q"]).then_inc(w2q_loaded, 16)
            sp.dma_start(row_bias[:], T["b2o"].unsqueeze(0).broadcast_to([P, DM])).then_inc(w2_loaded, 16)
            sp.dma_start(w2o, T["w2o"]).then_inc(w2o_loaded, 16)
            sp.dma_start(gate[:], T["gate"]).then_inc(gate_loaded, 16)
            if STAGES >= 3:
                s3_loads_early(sp)
            sp.wait_ge(v2_ready, 2)
            for u in range(2):
                pairs = v2.rearrange("p (t u) d -> p u t d", u=2)
                sp.dma_start(pairs[64 * (1 - u):64 * (1 - u) + S, u], pairs[64 * u:64 * u + S, u]).then_inc(v2_swapped, 16)
            if STAGES >= 4:
                s4_loads_early(sp)
            if STAGES >= 3:
                s3_sp(sp)
            if STAGES >= 4:
                s4_sp_main(sp)
            if STAGES >= 5:
                s5_sp(sp)
            if STAGES == 5:
                s5_sp_swap(sp)
            if STAGES >= 6:
                s6_sp(sp)
            for t in range(NT):
                sp.wait_ge(x_final, t + 1)
                sp.dma_start(out.rearrange("b s h -> (b s) h").rearrange("(t p) h -> p t h", p=P)[:, t, :], x[:, t, :]).then_inc(out_stored, 16)
            sp.wait_ge(out_stored, 16 * NT)

        @block.gpsimd
        def _(pool):
            link = Chain(pool, "pool_chain")
            norm_pool(pool, link, 0)
            if STAGES >= 2:
                norm_pool(pool, link, 1)
                norms[1].wait(pool, "xn", NT)
                pool.wait_ge(w2_loaded, 48)
                nc.gpsimd.tensor_tensor(x[:], x[:], row_bias[:].unsqueeze(1).broadcast_to([P, NT, DM]), ALU.add).then_inc(x_biased, 1)
            if STAGES >= 3:
                s3_pool(pool, link)
            if STAGES >= 4:
                s4_pool(pool, link)
            if STAGES >= 5:
                s5_pool(pool, link)
            if STAGES >= 6:
                s6_pool(pool, link)

        @block.tensor
        def _(pe):
            s1_pe(pe)
            if STAGES >= 2:
                s2_pe(pe)
            if STAGES >= 3:
                s3_pe(pe)
            if STAGES >= 4:
                s4_pe(pe)
            if STAGES >= 5:
                s5_pe(pe)
            if STAGES >= 6:
                s6_pe(pe)

        @block.scalar
        def _(act):
            s1_act(act)
            if STAGES >= 2:
                s2_act(act)
            if STAGES >= 3:
                s3_act(act)
            if STAGES >= 4:
                s4_act(act)
            if STAGES >= 5:
                s5_act(act)
            if STAGES >= 6:
                s6_act(act)

        @block.vector
        def _(dve):
            link = Chain(dve, "dve_chain")
            s1_dve(dve, link)
            if STAGES >= 2:
                s2_dve(dve, link)
            if STAGES >= 3:
                s3_dve(dve, link)
            if STAGES >= 4:
                s4_dve(dve, link)
            if STAGES >= 5:
                s5_dve(dve, link)
            if STAGES >= 6:
                s6_dve(dve, link)
            if STAGES < 6:
                for t in range(4):
                    nc.vector.memset(stat[:, 45:46], 0.0).then_inc(x_final, 1)


def constants():
    import numpy as np
    n = np.arange(P)
    c = np.zeros((P, 5, P), np.float32)
    c[:, 0] = n[:, None] == n[None, :]
    c[:, 1] = n[:, None] < n[None, :]
    c[:, 2] = 1.0
    c[:, 3] = n[None, :]
    for t in range(NT):
        c[:, 4, S + 2 * t], c[:, 4, S + 2 * t + 1] = n, t * P
    c[:, 4, 0:S] = np.where(n[None, :S] <= n[:, None] % S, 0.0, MASKED)
    return c


def rope_tables(length, dim):
    import numpy as np
    f32 = np.float32
    inv = f32(1.0) / f32(10000.0) ** (np.arange(0, dim, 2, dtype=f32) / f32(dim))
    f = np.arange(length, dtype=f32)[:, None] * inv[None, :]
    return np.repeat(np.sin(f), 2, -1), np.repeat(np.cos(f), 2, -1)


def rope_queries():
    import numpy as np
    sin, cos = rope_tables(S, DCQ)
    sin = np.where(np.arange(DCQ) < DCQ // 2, -sin, sin)
    cols = query_columns()[:3]
    return np.stack([tab[:, c].T for tab in (cos, sin) for c in cols], 1).reshape(P, 6 * S)


def rope_context():
    import numpy as np
    sin, cos = rope_tables(LCTX, DC)
    sin = np.where(np.arange(DC) < DC // 2, -sin, sin)
    tabs = np.zeros((2, LT * P, DC), np.float32)
    tabs[0, :LCTX], tabs[1, :LCTX] = cos, sin
    return tabs.reshape(2, LT, P, DC).transpose(0, 2, 1, 3)


def query_columns():
    import numpy as np
    h = DCQ // 2
    return [np.arange(P), np.arange(h, h + P), np.r_[P:h, h + P:DCQ], np.r_[h + P:DCQ, P:h]]


def kernel(**inputs):
    import numpy as np
    import concourse.bacc as bacc
    from concourse.bass_utils import run_bass_kernel_spmd as run

    def chunks(w):
        return w.reshape(w.shape[0] // P, P, w.shape[1]).transpose(1, 0, 2)

    I = {k: np.asarray(v) for k, v in inputs.items()}
    T = {
        "x": I["x"], "ctx": I["ctx_512"], "cst": constants(),
        "w1q": chunks(I["L0_xattn_Wq"].T), "w1kv": I["L0_xattn_Wkv_expand"].T, "w1o": chunks(I["L0_xattn_Wout"].T),
        "vec2": np.concatenate([I["L0_attn_bq"].reshape(NH, P).T, I["L0_attn_bk"][:, None], I["L0_attn_bv"][:, None]], 1),
        "w2kv": np.stack([chunks(I["L0_attn_Wk"]), chunks(I["L0_attn_Wv"])], 1),
        "w2q": chunks(I["L0_attn_Wq"]), "w2o": chunks(I["L0_attn_Wo"]), "b2o": I["L0_attn_bo"],
        "norm3": I["L0_ffn_norm_w"], "gate": chunks(I["L0_ffn_gate_w"].T),
        "w3": np.concatenate([I["L0_ffn_w13"].reshape(NE, KC, P, DM), I["L0_ffn_w2"].reshape(NE, 2, P, DM)], 1).transpose(0, 2, 1, 3),
        "w3s": np.concatenate([chunks(np.concatenate([I["L0_ffn_shared_gate_w"], I["L0_ffn_shared_up_w"]], 1)),
                               chunks(I["L0_ffn_shared_down_w"])], 1),
        "w4q": chunks(I["L1_xattn_Wq"].T),
        "w4kq": I["L1_xattn_w_kc_q"][:, :, np.concatenate(query_columns())].transpose(1, 0, 2),
        "w4qr": I["L1_xattn_W_qr"][:, np.concatenate(query_columns()[:3]), :].transpose(0, 2, 1)
                .reshape(2, NH // 2, R, DCQ).transpose(0, 2, 1, 3).reshape(P, NH // 2, DCQ),
        "w4kr": I["L1_xattn_W_kr"].transpose(0, 2, 1).reshape(2, NH // 2, R, DC).transpose(0, 2, 1, 3).reshape(P, NH // 2, DC),
        "w4kv": I["L1_xattn_w_kc_kv"].transpose(2, 0, 1), "w4o": chunks(I["L1_xattn_Wo"].T),
        "rope_q": rope_queries(), "rope_k": rope_context(),
        "w5": np.stack([chunks(I["L1_attn_" + n].T) for n in ("wq", "wk", "wv", "wo")], 1).reshape(P, 4 * KC * DM),
        "vec5": np.concatenate([I["L1_attn_" + n].reshape(KC, P).T for n in ("bq", "bk", "bv")], 1), "b5o": I["L1_attn_bo"],
        "w6": np.concatenate([chunks(I["L1_ffn_w_gate_up"].T).reshape(P, KC * 2 * FF),
                              chunks(I["L1_ffn_w_down"].T).reshape(P, FF * DM // P)], 1),
        "norm6": I["L1_ffn_norm_weight"],
    }
    nc = bacc.Bacc("TRN2", target_bir_lowering=False, num_devices=1)
    arrays, aps = {}, {}
    for name, a in T.items():
        a = np.ascontiguousarray(a)
        arrays["in_" + name] = a
        aps[name] = nc.dram_tensor("in_" + name, a.shape, mybir.dt.from_np(a.dtype), kind="ExternalInput").ap()
    o = nc.dram_tensor("out_0", (B, S, DM), F32, kind="ExternalOutput").ap()
    scratch = {"h_rows": nc.dram_tensor("h_rows", (TOK, DM), F32, kind="Internal").ap(),
               "eo_rows": nc.dram_tensor("eo_rows", (NE * CAP, DM), F32, kind="Internal").ap()}
    perceiver(nc, aps, o, scratch)
    r = run(nc, [arrays], core_ids=[0])
    return r.results[0]["out_0"]
```

```python
from contextlib import ExitStack

import concourse.bass as bass
from concourse import mybir

F32 = mybir.dt.float32
BF16 = mybir.dt.bfloat16
U32 = mybir.dt.uint32
ALU = mybir.AluOpType
ACT = mybir.ActivationFunctionType
AX = mybir.AxisListType.X

STAGES = 6

P = 128
B, S, DM = 8, 64, 512
TOK = B * S
NT = TOK // P
KC = DM // P
NH = 16
HD = DM // NH
LCTX = 1601
LT = -(-LCTX // P)
LAST = LCTX - (LT - 1) * P
DC = 128
DCQ = 384
R = 64
NE, TOPK, FI = 32, 4, 256
CAP = 2 * TOK * TOPK // NE
FF = 1408
LN_EPS = 1e-5
MASKED = -3.0e38


def perceiver(nc, T, out, scratch):
    ctx = ExitStack()
    with ctx:
        def sb(name, shape, dt=F32):
            return ctx.enter_context(nc.sbuf_tensor(name, shape, dt))

        def sem(name):
            return ctx.enter_context(nc.semaphore(name))

        ps = ctx.enter_context(nc.psum_tensor("ps", [P, 8, 512], F32))

        x = sb("x", [P, NT, DM])
        xn = sb("xn", [P, NT, DM])
        xT = sb("xT", [P, KC, TOK])
        cst = sb("cst", [P, 5, P])
        ident, before, ones, iota = (cst[:, i, :] for i in range(4))
        causal = cst[:, 4, 0:S]
        vecs = sb("vecs", [P, 64])
        row_bias = sb("row_bias", [P, DM])
        stat = sb("stat", [P, 512])

        RA = sb("RA", [P, 8192])
        RB = sb("RB", [P, 8192])
        RC = sb("RC", [P, 5120])
        RQ = sb("RQ", [P, 8192])
        RR = sb("RR", [P, 8192])
        RE = sb("RE", [P, 6144])
        RG = sb("RG", [P, 1024])

        def cut(region, at, *shape):
            n = 1
            for s in shape:
                n *= s
            v = region[:, at:at + n]
            if len(shape) == 2:
                v = v.rearrange("p (a b) -> p a b", b=shape[1])
            if len(shape) == 3:
                v = v.rearrange("p (a b c) -> p a b c", b=shape[1], c=shape[2])
            return v

        class Chain:

            def __init__(self, eng, name):
                self.eng, self.sem, self.n, self.base = eng, sem(name), 0, 0

            def __call__(self, ins):
                self.n += 1
                ins.then_inc(self.sem, 1)
                self.eng.wait_ge(self.sem, self.n + self.base)

        bst = cut(stat, 0, NT, 6)
        mv = cut(stat, 24, NT, 2)
        rstd = stat[:, 32:36]
        vare = stat[:, 36:40]
        power = stat[:, 40:44]

        class Rounds:

            def __init__(self, prefix, per, sems=None, run=0):
                self.prefix, self.per, self.run = prefix, per, run
                self.sems = sems or {n: sem(f"{prefix}_{n}") for n in per}

            def again(self):
                return Rounds(self.prefix, self.per, self.sems, self.run + 1)

            def __getitem__(self, name):
                return self.sems[name]

            def wait(self, eng, name, value):
                assert 0 < value <= self.per[name]
                eng.wait_ge(self.sems[name], self.run * self.per[name] + value)

        norms = [Rounds("norm", {"var": NT, "rstd": NT, "xn": NT, "xT_ps": NT, "xT": NT})]
        for _ in range(5):
            norms.append(norms[-1].again())

        def norm_stats_dve(dve, link, k, t):
            link(nc.vector.bn_stats(bst[:, t, :], x[:, t, :]))
            nc.vector.bn_aggr(mv[:, t, :], bst[:, t, :]).then_inc(norms[k]["var"], 1)

        def norm_rows_dve(dve, k, t):
            norms[k].wait(dve, "rstd", t + 1)
            nc.vector.tensor_scalar(xn[:, t, :], x[:, t, :], mv[:, t, 0:1], rstd[:, t:t + 1],
                                    ALU.subtract, ALU.mult).then_inc(norms[k]["xn"], 1)

        def norm_rstd_pool(pool, link, k, t):
            norms[k].wait(pool, "var", t + 1)
            link(nc.gpsimd.tensor_scalar(vare[:, t:t + 1], mv[:, t, 1:2], LN_EPS, None, ALU.add))
            nc.gpsimd.tensor_tensor(rstd[:, t:t + 1], vare[:, t:t + 1], power[:, t:t + 1], ALU.pow).then_inc(norms[k]["rstd"], 1)

        def norm_pool(pool, link, k, rms_eps=None):
            lag = int(k == 5)
            for n in range(NT + lag):
                if n < NT:
                    norm_rstd_pool(pool, link, k, n)
                t = n - lag
                if t >= 0 and rms_eps is not None:
                    pool.wait_ge(sq_ready, NT * (k == 5) + t + 1)
                    link(nc.gpsimd.tensor_scalar(rms_in[:, t:t + 1], sq[:, t:t + 1], 1.0 / DM, rms_eps, ALU.mult, ALU.add))
                    nc.gpsimd.tensor_tensor(rms[:, t:t + 1], rms_in[:, t:t + 1], power[:, t:t + 1], ALU.pow).then_inc(rms_ready, 1)

        def xT_pe(pe, k, t, bank, rows=None, ready=None):
            rows = xn if rows is None else rows
            if ready is None:
                norms[k].wait(pe, "xn", t + 1)
            else:
                pe.wait_ge(ready, t + 1)
            for kc in range(KC):
                i = nc.tensor.transpose(ps[:, bank, kc * P:(kc + 1) * P], rows[:, t, kc * P:(kc + 1) * P], ident)
            i.then_inc(norms[k]["xT_ps"], 1)

        def xT_act(act, k, t, bank):
            norms[k].wait(act, "xT_ps", t + 1)
            nc.scalar.copy(xT[:, :, t * P:(t + 1) * P], ps[:, bank, :].rearrange("p (c n) -> p c n", c=KC)).then_inc(norms[k]["xT"], 1)

        def xT_ready(pe, k):
            norms[k].wait(pe, "xT", NT)

        def residual_dve(dve, link, k, tile_ready, addend, lag=1):
            for t in range(NT + lag):
                if t < NT:
                    tile_ready(t)
                    link(nc.vector.tensor_tensor(x[:, t, :], x[:, t, :], addend(t), ALU.add))
                    norm_stats_dve(dve, link, k, t)
                if t >= lag:
                    norm_rows_dve(dve, k, t - lag)

        mh_q = cut(RQ, 0, KC, TOK)
        mh_k = cut(RQ, 2048, KC, TOK)
        mh_v = cut(RQ, 4096, B, DM)
        mh_o = mh_q
        mh_p = cut(RR, 0, B // 2, 1024)
        mh_pT = cut(RR, 4096, B // 2, 2, 512)
        mh_mx = stat[:, 64:128]
        mh_sm = stat[:, 128:192]
        mh_rs = stat[:, 192:256]

        H1 = Rounds("heads", {"q": KC, "k": KC, "v_act": NT, "v_dve": NT, "swapped": 32, "scores": 4, "shifted": 4, "exps": 4, "probs": 4, "pT_ps": 8,
                              "pT_act": B // 2, "pT_dve": B // 2, "o_ps": KC, "o": KC, "q_ps": KC, "k_ps": KC, "v_ps": NT})
        projected = [Rounds("projected", {"rows": NT})]
        for _ in range(3):
            projected.append(projected[-1].again())

        def value_half(u, t):
            own = slice(64 * u, 64 * u + S)
            return mh_v[own, 2 * t + u, :], ps[own, 4 + t, :]

        def values_act(act, H):
            for t in range(NT):
                H.wait(act, "v_ps", t + 1)
                nc.scalar.copy(*value_half(0, t)).then_inc(H["v_act"], 1)

        def values_dve(dve, H):
            for t in range(NT):
                H.wait(dve, "v_ps", t + 1)
                nc.vector.tensor_copy(*value_half(1, t)).then_inc(H["v_dve"], 1)

        def swap_values(sp, H):
            H.wait(sp, "v_act", NT)
            H.wait(sp, "v_dve", NT)
            pairs = mh_v.rearrange("p (t u) d -> p u t d", u=2)
            for u in range(2):
                sp.dma_start(pairs[64 * (1 - u):64 * (1 - u) + S, u], pairs[64 * u:64 * u + S, u]).then_inc(H["swapped"], 16)

        def rows_pe(pe, proj, t, bank, at, w):
            n = w.shape[1]
            for c in range(n):
                i = nc.tensor.matmul(ps[:, bank, :], at[:, c, t * P:(t + 1) * P], w[:, c, :], start=(c == 0), stop=(c == n - 1))
            i.then_inc(proj["rows"], 1)

        def heads_pe(pe, H, w_out, values_ready, proj, turn):
            H.wait(pe, "q", KC)
            H.wait(pe, "k", KC)
            for q in range(B // 2):
                if q >= 2:
                    H.wait(pe, "shifted", q - 1)
                for c in range(KC):
                    for b2 in range(2):
                        tok = (2 * q + b2) * S
                        for r in range(4):
                            at = ((q // 2) * KC + c) * S
                            i = nc.tensor.matmul(ps[64 * b2:64 * b2 + S, 4 * (q % 2) + r, at:at + S],
                                                 mh_q[32 * r:32 * r + HD, c, tok:tok + S],
                                                 mh_k[32 * r:32 * r + HD, c, tok:tok + S],
                                                 start=True, stop=True)
                i.then_inc(H["scores"], 1)

            def turn_probs(q):
                H.wait(pe, "probs", q + 1)
                for n in range(8):
                    i = nc.tensor.transpose(ps[:, 2 * q + n // 4, (n % 4) * P:(n % 4 + 1) * P],
                                            mh_p[:, q, n * P:(n + 1) * P], ident)
                    if n % 4 == 3:
                        i.then_inc(H["pT_ps"], 1)

            def attend(q):
                H.wait(pe, "pT_act", q + 1)
                H.wait(pe, "pT_dve", q + 1)
                for c in range(KC):
                    u = 64 * (c % 2)
                    for b2 in range(2):
                        b = 2 * q + b2
                        for r in range(4):
                            at = (2 * (r % 2) + c // 2) * P + b2 * S
                            h = 4 * c + r
                            i = nc.tensor.matmul(ps[32 * r:32 * r + HD, c, b * S:(b + 1) * S],
                                                 mh_v[u:u + S, b, h * HD:(h + 1) * HD],
                                                 mh_pT[u:u + S, q, r // 2, at:at + S], start=True, stop=True)
                    if q == B // 2 - 1:
                        i.then_inc(H["o_ps"], 1)
            H.wait(pe, "shifted", 3)
            turn_probs(0)
            turn_probs(1)
            values_ready()
            H.wait(pe, "pT_act", 2)
            H.wait(pe, "pT_dve", 2)
            attend(0)
            H.wait(pe, "shifted", 4)
            turn_probs(2)
            attend(1)
            turn_probs(3)
            attend(2)
            attend(3)
            for t in range(NT):
                for c in range(KC):
                    if t == 0:
                        H.wait(pe, "o", c + 1)
                    i = nc.tensor.matmul(ps[:, 4 + t, :], mh_o[:, c, t * P:(t + 1) * P], w_out[:, c, :],
                                         start=(c == 0), stop=(c == KC - 1))
                i.then_inc(proj["rows"], 1)
                if t >= 2 and turn:
                    turn(t - 2)

        def heads_dve(dve, link, H, masked):
            def rows(v, q):
                return v[:, 16 * q:16 * q + 16].rearrange("p (r c) -> p r c", c=KC)

            def probs(q):
                return mh_p[:, q, :].rearrange("p (r c k) -> p r c k", c=KC, k=S)

            def shift(q):
                at = (q // 2) * KC * S
                scores = ps[:, 4 * (q % 2):4 * (q % 2) + 4, at:at + KC * S].rearrange("p r (c k) -> p r c k", k=S)
                H.wait(dve, "scores", q + 1)
                if masked:
                    link(nc.vector.tensor_tensor(probs(q), scores, causal.unsqueeze(1).unsqueeze(1).broadcast_to([P, 4, KC, S]), ALU.add))
                    scores = probs(q)
                link(nc.vector.tensor_reduce(rows(mh_mx, q), scores, AX, ALU.max))
                nc.vector.tensor_tensor(probs(q), scores, rows(mh_mx, q).unsqueeze(3).broadcast_to([P, 4, KC, S]),
                                        ALU.subtract).then_inc(H["shifted"], 1)

            def scale(q):
                H.wait(dve, "exps", q + 1)
                link(nc.vector.tensor_reduce(rows(mh_sm, q), probs(q), AX, ALU.add))
                link(nc.vector.reciprocal(rows(mh_rs, q), rows(mh_sm, q)))
                nc.vector.tensor_tensor(probs(q), probs(q), rows(mh_rs, q).unsqueeze(3).broadcast_to([P, 4, KC, S]),
                                        ALU.mult).then_inc(H["probs"], 1)

            def turned(q):
                H.wait(dve, "pT_ps", 2 * q + 2)
                nc.vector.tensor_copy(mh_pT[:, q, 1, :], ps[:, 2 * q + 1, :]).then_inc(H["pT_dve"], 1)
            shift(0)
            shift(1)
            scale(0)
            shift(2)
            scale(1)
            shift(3)
            turned(0)
            scale(2)
            turned(1)
            scale(3)
            turned(2)
            turned(3)

        def heads_act(act, H, bias):
            def turned(q):
                H.wait(act, "pT_ps", 2 * q + 1)
                nc.scalar.copy(mh_pT[:, q, 0, :], ps[:, 2 * q, :]).then_inc(H["pT_act"], 1)
            for q in range(B // 2):
                H.wait(act, "shifted", q + 1)
                nc.scalar.activation(mh_p[:, q, :], mh_p[:, q, :], ACT.Exp, scale=HD ** -0.5).then_inc(H["exps"], 1)
            for q in range(B // 2):
                turned(q)
            for c in range(KC):
                H.wait(act, "o_ps", c + 1)
                if bias is None:
                    i = nc.scalar.copy(mh_o[:, c, :], ps[:, c, :])
                else:
                    i = nc.scalar.activation(mh_o[:, c, :], ps[:, c, :], ACT.Identity, bias=bias[:, c:c + 1])
                i.then_inc(H["o"], 1)

        x_loaded = sem("x_loaded")
        cst_loaded = sem("cst_loaded")
        c64_loaded = sem("c64_loaded")
        w1_loaded = sem("w1_loaded")
        w1q_loaded = sem("w1q_loaded")
        w1o_loaded = sem("w1o_loaded")
        out_stored = sem("out_stored")
        x_final = sem("x_final")

        w1q = cut(RC, 0, KC, DM)
        w1kv = cut(RC, 2048, 2 * DM)
        w1o = cut(RC, 3072, KC, DM)
        c64 = cut(RR, 0, NT, P)
        c64T = cut(RR, 1024, NT, P)
        c64T_ps, c64T_ready = sem("c64T_ps"), sem("c64T_ready")

        def s1_pe(pe):
            pe.wait_ge(cst_loaded, 16)
            pe.wait_ge(c64_loaded, 32)
            for t in range(NT):
                i = nc.tensor.transpose(ps[:, 4, t * P:(t + 1) * P], c64[:, t, :], ident)
            i.then_inc(c64T_ps, 1)
            pe.wait_ge(c64T_ready, 1)
            pe.wait_ge(w1_loaded, 16)
            for t in range(NT):
                nc.tensor.matmul(ps[:, 4 + t, :], c64T[:, t, :], w1kv[:, DM:2 * DM],
                                 start=True, stop=True).then_inc(H1["v_ps"], 1)
            for c in range(KC):
                nc.tensor.matmul(ps[:, c, :], w1kv[:, c * P:(c + 1) * P], c64T[:, :, :],
                                 start=True, stop=True).then_inc(H1["k_ps"], 1)
            H1.wait(pe, "v_act", NT)
            H1.wait(pe, "v_dve", NT)
            H1.wait(pe, "k", KC)
            for t in range(NT):
                xT_pe(pe, 0, t, t)
            xT_ready(pe, 0)
            pe.wait_ge(w1q_loaded, 16)
            for c in range(KC):
                for kc in range(KC):
                    i = nc.tensor.matmul(ps[:, 4 + c, :], w1q[:, kc, c * P:(c + 1) * P], xT[:, kc, :],
                                         start=(kc == 0), stop=(kc == KC - 1))
                i.then_inc(H1["q_ps"], 1)
            pe.wait_ge(w1o_loaded, 16)
            heads_pe(pe, H1, w1o, lambda: H1.wait(pe, "swapped", 32), projected[0], lambda t: xT_pe(pe, 1, t, 4 + t))

        def s1_act(act):
            act.wait_ge(c64T_ps, 1)
            nc.scalar.copy(c64T[:, :, :], ps[:, 4, :].rearrange("p (t n) -> p t n", t=NT)).then_inc(c64T_ready, 1)
            values_act(act, H1)
            for t in range(NT):
                xT_act(act, 0, t, t)
            for c in range(KC):
                H1.wait(act, "q_ps", c + 1)
                nc.scalar.copy(mh_q[:, c, :], ps[:, 4 + c, :]).then_inc(H1["q"], 1)
            heads_act(act, H1, None)

        def s1_dve(dve, link):
            link(nc.vector.memset(power, -0.5))
            dve.wait_ge(x_loaded, 16)
            for t in range(NT):
                norm_stats_dve(dve, link, 0, t)
            for t in range(NT):
                norm_rows_dve(dve, 0, t)
            values_dve(dve, H1)
            for c in range(KC):
                H1.wait(dve, "k_ps", c + 1)
                nc.vector.tensor_copy(mh_k[:, c, :], ps[:, c, :]).then_inc(H1["k"], 1)
            heads_dve(dve, link, H1, True)
            residual_dve(dve, link, 1, lambda t: projected[0].wait(dve, "rows", t + 1), lambda t: ps[:, 4 + t, :])

        w2q = cut(RA, 0, KC, 2048)
        w2o = cut(RB, 0, NH, DM)
        w2kv = cut(RG, 0, 2, KC, P)
        q2 = cut(RQ, 0, B, NH * S)
        o2 = cut(RA, 0, NH, TOK)
        k2 = cut(RC, 0, TOK)
        v2 = cut(RC, 512, B, P)
        p2 = cut(RR, 0, B, 512)
        p2T = cut(RR, 4096, B, 512)
        b2q, b2k, b2v = vecs[:, 0:16], vecs[:, 16:17], vecs[:, 17:18]
        mx2, sm2, rs2 = (stat[:, 256 + 64 * i:320 + 64 * i] for i in range(3))
        w2_loaded = sem("w2_loaded")
        w2q_loaded = sem("w2q_loaded")
        w2o_loaded = sem("w2o_loaded")
        x_biased, k2_ps, k2_ready, v2_ps, v2_ready = (sem(n) for n in ("x_biased", "k2_ps", "k2_ready", "v2_ps", "v2_ready"))
        v2_swapped = sem("v2_swapped")
        q2_ps, q2_act, q2_dve = sem("q2_ps"), sem("q2_act"), sem("q2_dve")
        scores2, shifted2, exps2, probs2 = (sem(n) for n in ("scores2", "shifted2", "exps2", "probs2"))
        pT2_ps, pT2, o2_ps, o2_act = (sem(n) for n in ("pT2_ps", "pT2", "o2_ps", "o2_act"))

        def by_batch(v):
            return v.rearrange("p (b s) -> p b s", s=S)

        def q2_bank(n):
            return (7 + n) % 8

        def s2_pe(pe):
            for t in (2, 3):
                xT_pe(pe, 1, t, 4 + t)
            xT_ready(pe, 1)
            pe.wait_ge(w2_loaded, 48)
            for kc in range(KC):
                i = nc.tensor.matmul(ps[:, 4, :], w2kv[:, 0, kc, :], xT[:, kc, :], start=(kc == 0), stop=(kc == KC - 1))
            i.then_inc(k2_ps, 1)
            for t in range(NT):
                for kc in range(KC):
                    i = nc.tensor.matmul(ps[:, 5, t * P:(t + 1) * P], xT[:, kc, t * P:(t + 1) * P], w2kv[:, 1, kc, :],
                                         start=(kc == 0), stop=(kc == KC - 1))
            i.then_inc(v2_ps, 1)
            pe.wait_ge(w2q_loaded, 16)
            for h in range(NH):
                if h == 5:
                    pe.wait_ge(k2_ready, 1)
                if h == 6:
                    pe.wait_ge(v2_ready, 2)
                if h >= 8:
                    pe.wait_ge(q2_act if h % 2 == 0 else q2_dve, (h - 8) // 2 + 1)
                for kc in range(KC):
                    i = nc.tensor.matmul(ps[:, q2_bank(h), :], w2q[:, kc, h * P:(h + 1) * P], xT[:, kc, :],
                                         start=(kc == 0), stop=(kc == KC - 1))
                i.then_inc(q2_ps, 1)
            pe.wait_ge(q2_act, NH // 2)
            pe.wait_ge(q2_dve, NH // 2)

            def scores(b):
                for hp in range(NH // 2):
                    i = nc.tensor.matmul(ps[:, b % 4, hp * S:(hp + 1) * S], q2[:, b, hp * P:(hp + 1) * P],
                                         k2[:, b * S:(b + 1) * S], start=True, stop=True)
                i.then_inc(scores2, 1)

            def turn_probs(b):
                pe.wait_ge(probs2, b + 1)
                for j in range(4):
                    i = nc.tensor.transpose(ps[:, b % 4, j * P:(j + 1) * P], p2[:, b, j * P:(j + 1) * P], ident)
                i.then_inc(pT2_ps, 1)

            def attend(b):
                pe.wait_ge(pT2, b + 1)
                for e in range(2):
                    if e and b >= 2:
                        pe.wait_ge(o2_act, 2 * b - 2)
                    nc.tensor.matmul(ps[:, o2_bank(b, e), :], v2[64 * e:64 * e + S, b, :], p2T[64 * e:64 * e + S, b, :],
                                     start=True, stop=True).then_inc(o2_ps, 1)
            for b in range(4):
                scores(b)
            pe.wait_ge(v2_swapped, 32)
            for t in range(NT):
                if t >= 2:
                    xT_pe(pe, 2, t - 2, o2_rows_bank(t - 2), hn, hn_ready)
                turn_probs(2 * t)
                turn_probs(2 * t + 1)
                attend(2 * t)
                attend(2 * t + 1)
                for b in (2 * t + 4, 2 * t + 5):
                    if b < B:
                        pe.wait_ge(o2_act, 2 * b - 7)
                        scores(b)
                pe.wait_ge(o2_act, 4 * t + 4)
                if t == 0:
                    pe.wait_ge(w2o_loaded, 16)
                if t >= 2:
                    norms[2].wait(pe, "xT", t - 1)
                rows_pe(pe, projected[1], t, o2_rows_bank(t), o2, w2o)

        def o2_rows_bank(t):
            return 6 + t % 2

        def o2_bank(b, e):
            return 4 + b % 2 if e else b % 4

        def o2_rows(b, e):
            return (o2.rearrange("p (j e u) n -> p e j u n", e=2, u=2)[:, e, :, :, b * S:(b + 1) * S],
                    ps[:, o2_bank(b, e), :].rearrange("p (j u s) -> p j u s", u=2, s=S))

        def s2_act(act):
            for t in range(NT):
                xT_act(act, 1, t, 4 + t)
            act.wait_ge(k2_ps, 1)
            nc.scalar.activation(k2, ps[:, 4, :], ACT.Identity, bias=b2k).then_inc(k2_ready, 1)
            for h in range(0, NH, 2):
                act.wait_ge(q2_ps, h + 1)
                nc.scalar.activation(q2[:, :, h * S:(h + 1) * S], by_batch(ps[:, q2_bank(h), :]), ACT.Identity, bias=b2q[:, h:h + 1]).then_inc(q2_act, 1)

            def exps(b):
                act.wait_ge(shifted2, b + 1)
                nc.scalar.activation(p2[:, b, :], p2[:, b, :], ACT.Exp, scale=P ** -0.5).then_inc(exps2, 1)

            def tile_out(t):
                for b in (2 * t, 2 * t + 1):
                    act.wait_ge(pT2_ps, b + 1)
                    nc.scalar.copy(p2T[:, b, :], ps[:, b % 4, :]).then_inc(pT2, 1)
                for b in (2 * t, 2 * t + 1):
                    for e in range(2):
                        act.wait_ge(o2_ps, 2 * b + e + 1)
                        dst, src = o2_rows(b, e)
                        nc.scalar.activation(dst, src, ACT.Identity, bias=b2v).then_inc(o2_act, 1)
            for b in range(3):
                exps(b)
            tile_out(0)
            for b in range(3, 6):
                exps(b)
            tile_out(1)
            squares_act(act, 0)
            exps(6)
            exps(7)
            xT_act(act, 2, 0, 6)
            tile_out(2)
            squares_act(act, 1)
            xT_act(act, 2, 1, 7)
            tile_out(3)

        def squares_act(act, t):
            norms[2].wait(act, "xn", t + 1)
            nc.scalar.activation(hn[:, t, :], xn[:, t, :], ACT.Square, accum_out=sq[:, t:t + 1]).then_inc(sq_ready, 1)

        def s2_dve(dve, link):
            dve.wait_ge(v2_ps, 1)
            for u in range(2):
                own = slice(64 * u, 64 * u + S)
                nc.vector.tensor_copy(v2.rearrange("p (t u) d -> p u t d", u=2)[own, u], ps[own, 5, :].rearrange("p (t d) -> p t d", d=P)).then_inc(v2_ready, 1)
            for h in range(1, NH, 2):
                dve.wait_ge(q2_ps, h + 1)
                nc.vector.tensor_scalar(q2[:, :, h * S:(h + 1) * S], by_batch(ps[:, q2_bank(h), :]), b2q[:, h:h + 1], None, ALU.add).then_inc(q2_dve, 1)

            def shift(b):
                dve.wait_ge(scores2, b + 1)
                mx = mx2[:, 8 * b:8 * b + 8]
                scores = ps[:, b % 4, :].rearrange("p (n k) -> p n k", k=S)
                link(nc.vector.tensor_reduce(mx, scores, AX, ALU.max))
                nc.vector.tensor_tensor(p2[:, b, :].rearrange("p (n k) -> p n k", k=S), scores,
                                        mx.unsqueeze(2).broadcast_to([P, 8, S]), ALU.subtract).then_inc(shifted2, 1)

            def scale(b):
                dve.wait_ge(exps2, b + 1)
                probs = p2[:, b, :].rearrange("p (n k) -> p n k", k=S)
                sm, rs = sm2[:, 8 * b:8 * b + 8], rs2[:, 8 * b:8 * b + 8]
                link(nc.vector.tensor_reduce(sm, probs, AX, ALU.add))
                link(nc.vector.reciprocal(rs, sm))
                nc.vector.tensor_tensor(probs, probs, rs.unsqueeze(2).broadcast_to([P, 8, S]), ALU.mult).then_inc(probs2, 1)

            def tile_rows(t):
                projected[1].wait(dve, "rows", t + 1)
                link(nc.vector.tensor_tensor(x[:, t, :], x[:, t, :], ps[:, o2_rows_bank(t), :], ALU.add))
                norm_stats_dve(dve, link, 2, t)
                norm_rows_dve(dve, 2, t)
                dve.wait_ge(rms_ready, t + 1)
                nc.vector.scalar_tensor_tensor(hn[:, t, :], xn[:, t, :], rms[:, t:t + 1], row_bias[:], ALU.mult,
                                               ALU.mult).then_inc(hn_ready, 1)
            shift(0)
            for b in range(1, 6):
                shift(b)
                scale(b - 1)
            dve.wait_ge(x_biased, 1)
            dve.wait_ge(row_loaded, 16)
            tile_rows(0)
            for b in (6, 7):
                shift(b)
                scale(b - 1)
            scale(7)
            for t in range(1, NT):
                tile_rows(t)

        ring = [cut(RE, 0, 6, DM), cut(RE, 3072, 6, DM), cut(RR, 0, 6, DM), cut(RR, 3072, 6, DM)]
        xe = [cut(RR, 6144 + 512 * i, DM) for i in range(2)]
        xeT = [cut(RR, 7168 + 512 * i, KC, P) for i in range(2)]
        hn = cut(RC, 2048, NT, DM)
        w3s = cut(RQ, 2048, 6, DM)
        sg = [cut(RQ, 5120 + 256 * i, FI) for i in range(2)]
        act3 = [cut(RQ, 5632 + 256 * i, FI) for i in range(2)]
        actT = [cut(RQ, 6144 + 256 * i, 2, P) for i in range(2)]
        eo = [cut(RQ, 6656 + 512 * i, DM) for i in range(2)]
        picked = [cut(RR, 512 * i, DM) for i in range(8)]
        OH = 8
        onehot = [RR[:, 6144 + 256 * i:6400 + 256 * i].bitcast(BF16).rearrange("p (t c) -> p t c", c=P) for i in range(OH)]
        logits, pos, mask, place = (cut(RG, 512 + 128 * i, NT, NE) for i in range(4))
        iota16 = RG[:, 512:576].bitcast(BF16)
        choice = cut(RC, 4096, NT * TOPK, NE)
        choice_pos = cut(RC, 4608, NT * TOPK, NE)
        gate = sb("gate", [P, KC, NE])
        topv = cut(stat, 64, NT, 8)
        topi = cut(stat, 96, NT, 8).bitcast(U32)
        top_e = stat[:, 128:144]
        top_w = stat[:, 144:160]
        w_sum, w_rs = stat[:, 160:164], stat[:, 164:168]
        top_pos = stat[:, 168:184]
        slot = stat[:, 200:216].bitcast(U32)
        sq, rms_in, rms = stat[:, 216:220], stat[:, 220:224], stat[:, 224:228]
        token = stat[:, 228:260].bitcast(U32)
        token_at = [stat[:, 260 + i:261 + i].bitcast(U32) for i in range(2)]
        token_parts = stat[:, 264:268].bitcast(BF16)
        w3s_loaded, row_loaded, gate_loaded = sem("w3s_loaded"), sem("row_loaded"), sem("gate_loaded")
        ring_loaded = [sem(f"ring_loaded{i}") for i in range(4)]
        sq_ready, rms_ready, hn_ready, h_stored = (sem(n) for n in ("sq_ready", "rms_ready", "hn_ready", "h_stored"))
        logits_ps, mask_ready, pos_ps, places_done = (sem(n) for n in ("logits_ps", "mask_ready", "pos_ps", "places_done"))
        top_shifted, top_exp, onehot_ready, onehot_used, token_ready = (
            sem(n) for n in ("top_shifted", "top_exp", "onehot_ready", "onehot_used", "token_ready"))
        xe_loaded = [sem(f"xe_loaded{i}") for i in range(2)]
        xeT_ps, xeT_ready, gu_ps, sg_ready, act_ready, actT_ps, actT_ready, eo_ps, eo_ready = (
            sem(n) for n in ("xeT_ps", "xeT_ready", "gu_ps", "sg_ready", "act_ready", "actT_ps", "actT_ready", "eo_ps", "eo_ready"))
        eo_stored = [sem(f"eo_stored{i}") for i in range(2)]
        picked_loaded = [sem(f"picked_loaded{i}") for i in range(8)]
        picked_used = sem("picked_used")
        SH = NT
        JOBS = SH + NE

        def act_transpose_pe(pe, j, par):
            pe.wait_ge(act_ready, j + 1)
            for f in range(2):
                i = nc.tensor.transpose(ps[:, 4 + par, f * P:(f + 1) * P], act3[par][:, f * P:(f + 1) * P], ident)
            i.then_inc(actT_ps, 1)

        def rows_transpose_pe(pe, e, par):
            pe.wait_ge(xe_loaded[par], e * 8 + 16 - 8 * par)
            for kc in range(KC):
                i = nc.tensor.transpose(ps[:, par, kc * P:(kc + 1) * P], xe[par][:, kc * P:(kc + 1) * P], ident)
            i.then_inc(xeT_ps, 1)

        def down_pe(pe, j, par, w, first=False, each=None):
            pe.wait_ge(actT_ready, j + 1)
            if not first:
                pe.wait_ge(eo_ready, j)
            for f in range(2):
                i = nc.tensor.matmul(ps[:, 6, :], actT[par][:, f, :], w[:, 4 + f, :], start=(f == 0), stop=(f == 1))
                if f:
                    i.then_inc(eo_ps, 1)
                if each:
                    each()

        def up_pe(pe, par, w, rows, between=None, each=None):
            for kc in range(KC):
                if kc == KC // 2 and between:
                    between()
                i = nc.tensor.matmul(ps[:, 2 + par, :], rows(kc), w[:, kc, :], start=(kc == 0), stop=(kc == KC - 1))
                if kc == KC - 1:
                    i.then_inc(gu_ps, 1)
                if each:
                    each()

        def expert_step_pe(pe, e, u, w_before, last=False):
            j, par = e + SH, u % 2

            def between():
                act_transpose_pe(pe, j - 1, 1 - par)
                if not last:
                    rows_transpose_pe(pe, e + 1, 1 - par)
            pe.wait_ge(xeT_ready, e + 1)
            pe.wait_ge(ring_loaded[u], e * 4 + 16 - 4 * u)
            pe.wait_ge(act_ready, j - 1)
            up_pe(pe, par, ring[u], lambda kc: xeT[par][:, kc, :], between)
            down_pe(pe, j - 1, 1 - par, w_before)

        def s3_pe(pe):

            def shared(j):
                up_pe(pe, j % 2, w3s, lambda kc: xT[:, kc, j * P:(j + 1) * P])

            def gate_logits(t):
                for kc in range(KC):
                    i = nc.tensor.matmul(ps[:, 4, t * NE:(t + 1) * NE], xT[:, kc, t * P:(t + 1) * P], gate[:, kc, :],
                                         start=(kc == 0), stop=(kc == KC - 1))
                return i
            xT_pe(pe, 2, 2, o2_rows_bank(2), hn, hn_ready)
            pe.wait_ge(gate_loaded, 16)
            norms[2].wait(pe, "xT", 2)
            gate_logits(0)
            gate_logits(1)
            pe.wait_ge(w3s_loaded, 16)
            shared(0)
            norms[2].wait(pe, "xT", 3)
            gate_logits(2)
            xT_pe(pe, 2, 3, o2_rows_bank(3), hn, hn_ready)
            xT_ready(pe, 2)
            gate_logits(3).then_inc(logits_ps, 1)
            pe.wait_ge(mask_ready, 1)
            for t in range(NT):
                for t0 in range(t + 1):
                    i = nc.tensor.matmul(ps[:, 7, t * NE:(t + 1) * NE], before if t0 == t else ones, mask[:, t0, :],
                                         start=(t0 == 0), stop=(t0 == t))
            i.then_inc(pos_ps, 1)
            counted = iter(range(NE))

            def count(n):
                for e in [next(counted) for _ in range(n)]:
                    pe.wait_ge(onehot_ready, e + 1)
                    for t in range(NT):
                        i = nc.tensor.matmul(ps[:, 7, 2 * e:2 * e + 2], onehot[e % OH][:, t, :],
                                             token_parts[:, 2 * t:2 * t + 2], start=(t == 0), stop=(t == NT - 1))
                    i.then_inc(onehot_used, 1)
            for j in range(1, SH - 1):
                act_transpose_pe(pe, j - 1, 1 - j % 2)
                up_pe(pe, j % 2, w3s, lambda kc: xT[:, kc, j * P:(j + 1) * P], each=lambda: count(3))
                down_pe(pe, j - 1, 1 - j % 2, w3s, first=(j == 1), each=lambda: count(2))
            act_transpose_pe(pe, SH - 2, 0)
            shared(SH - 1)
            down_pe(pe, SH - 2, 0, w3s)
            rows_transpose_pe(pe, 0, 0)
            for e in range(4):
                expert_step_pe(pe, e, e, ring[e - 1] if e else w3s)
            with pe.Fori(0, NE // 4 - 2) as i:
                for u in range(4):
                    expert_step_pe(pe, i * 4 + (4 + u), u, ring[(u - 1) % 4])
            for u in range(4):
                expert_step_pe(pe, NE - 4 + u, u, ring[(u - 1) % 4], last=(u == 3))
            act_transpose_pe(pe, JOBS - 1, 1)
            down_pe(pe, JOBS - 1, 1, ring[3])
            if STAGES >= 4:
                w_products_pe(pe)

        def s3_act(act):
            for t in (2, 3):
                squares_act(act, t)
                xT_act(act, 2, t, 6 + t % 2)
            act.wait_ge(top_shifted, 1)
            nc.scalar.activation(top_w, top_w, ACT.Exp).then_inc(top_exp, 1)

            def silu(j, par, first=False):
                act.wait_ge(gu_ps, j + 1)
                if not first:
                    act.wait_ge(act_ready, j - 1)
                nc.scalar.activation(sg[par], ps[:, 2 + par, 0:FI], ACT.Silu).then_inc(sg_ready, 1)

            def rows(e, par):
                act.wait_ge(xeT_ps, e + 1)
                nc.scalar.copy(xeT[par].rearrange("p a b -> p (a b)"), ps[:, par, :]).then_inc(xeT_ready, 1)
            for j in range(SH):
                silu(j, j % 2, first=(j < 2))
            rows(0, 0)
            for e in range(4):
                rows(e + 1, 1 - e % 2)
                silu(e + SH, e % 2)
            with act.Fori(0, NE // 4 - 2) as i:
                for u in range(4):
                    rows(i * 4 + (5 + u), 1 - u % 2)
                    silu(i * 4 + (4 + u + SH), u % 2)
            for u in range(4):
                if u < 3:
                    rows(NE - 4 + u + 1, 1 - u % 2)
                silu(NE - 4 + u + SH, u % 2)
            if STAGES >= 4:
                w_products_act(act)

        def s3_dve(dve, link):
            def gated(j, par):
                dve.wait_ge(sg_ready, j + 1)
                nc.vector.tensor_tensor(act3[par], sg[par], ps[:, 2 + par, FI:2 * FI], ALU.mult).then_inc(act_ready, 1)

            def turned(j, par):
                dve.wait_ge(actT_ps, j + 1)
                nc.vector.tensor_copy(actT[par].rearrange("p a b -> p (a b)"), ps[:, 4 + par, 0:2 * P]).then_inc(actT_ready, 1)

            def shared_out(j):
                dve.wait_ge(eo_ps, j + 1)
                if j == 0:
                    dve.wait_ge(x_biased, 2)
                nc.vector.tensor_tensor(x[:, j, :], x[:, j, :], ps[:, 6, :], ALU.add).then_inc(eo_ready, 1)

            def routed_out(e, par, first=False):
                dve.wait_ge(eo_ps, e + (SH + 1))
                if not first:
                    dve.wait_ge(eo_stored[par], e * 8 - 8 * par)
                nc.vector.tensor_copy(eo[par], ps[:, 6, :]).then_inc(eo_ready, 1)

            link(nc.vector.tensor_copy(token_parts, cst[:, 4, 64:72]))
            dve.wait_ge(logits_ps, 1)
            link(nc.vector.tensor_copy(logits.rearrange("p t e -> p (t e)"), ps[:, 4, 0:NT * NE]))
            for t in range(NT):
                i = nc.vector.max(topv[:, t, :], logits[:, t, :])
            link(i)
            for t in range(NT):
                i = nc.vector.max_index(topi[:, t, :], topv[:, t, :], logits[:, t, :])
            link(i)
            nc.vector.tensor_tensor(top_w.rearrange("p (t k) -> p t k", k=TOPK), topv[:, :, 0:TOPK],
                                    topv[:, :, 0:1].broadcast_to([P, NT, TOPK]), ALU.subtract).then_inc(top_shifted, 1)
            link(nc.vector.tensor_copy(top_e.rearrange("p (t k) -> p t k", k=TOPK), topi[:, :, 0:TOPK]))
            link(nc.vector.tensor_tensor(choice, iota[:, 0:NE].unsqueeze(1).broadcast_to([P, NT * TOPK, NE]),
                                         top_e.unsqueeze(2).broadcast_to([P, NT * TOPK, NE]), ALU.is_equal))
            nc.vector.tensor_reduce(mask, choice.rearrange("p (t k) e -> p t e k", k=TOPK), AX, ALU.add).then_inc(mask_ready, 1)
            dve.wait_ge(top_exp, 1)
            link(nc.vector.tensor_reduce(w_sum, top_w.rearrange("p (t k) -> p t k", k=TOPK), AX, ALU.add))
            link(nc.vector.reciprocal(w_rs, w_sum))
            link(nc.vector.tensor_tensor(top_w.rearrange("p (t k) -> p t k", k=TOPK),
                                         top_w.rearrange("p (t k) -> p t k", k=TOPK),
                                         w_rs.unsqueeze(2).broadcast_to([P, NT, TOPK]), ALU.mult))
            dve.wait_ge(pos_ps, 1)
            link(nc.vector.tensor_copy(pos.rearrange("p t e -> p (t e)"), ps[:, 7, 0:NT * NE]))
            link(nc.vector.scalar_tensor_tensor(place, pos, 1.0, mask, ALU.add, ALU.mult))
            nc.vector.tensor_copy(iota16, iota)
            link(nc.vector.tensor_scalar(place, place, -1.0, None, ALU.add))
            gated(0, 0)
            link(nc.vector.tensor_tensor(choice_pos.rearrange("p (t k) e -> p t k e", k=TOPK),
                                         choice.rearrange("p (t k) e -> p t k e", k=TOPK),
                                         pos.unsqueeze(2).broadcast_to([P, NT, TOPK, NE]), ALU.mult))
            link(nc.vector.tensor_reduce(top_pos, choice_pos, AX, ALU.add))
            link(nc.vector.tensor_scalar(top_pos, top_pos, float(CAP - 1), None, ALU.min))
            link(nc.vector.scalar_tensor_tensor(slot, top_e, float(CAP), top_pos, ALU.mult, ALU.add))

            def slots(e0, e1):
                for e in range(e0, e1):
                    if e >= OH:
                        dve.wait_ge(onehot_used, e - OH + 1)
                    for t in range(NT):
                        i = nc.vector.tensor_scalar(onehot[e % OH][:, t, :], iota16, place[:, t, e:e + 1], None, ALU.is_equal)
                    i.then_inc(onehot_ready, 1)
            for j in range(1, SH - 1):
                turned(j - 1, 1 - j % 2)
                slots(16 * j - 16, 16 * j - 4)
                gated(j, j % 2)
                slots(16 * j - 4, 16 * j)
                if j == 1:
                    shared_out(0)
            dve.wait_ge(onehot_used, NE)
            token_ps = ps[:, 7, 0:2 * NE].rearrange("p (e a) -> p e a", a=2)
            token_low = stat[:, 300:332]
            link(nc.vector.tensor_copy(token_low, token_ps[:, :, 0]))
            nc.vector.tensor_tensor(token, token_low, token_ps[:, :, 1], ALU.add).then_inc(token_ready, 1)
            shared_out(1)
            turned(SH - 2, 0)
            gated(SH - 1, 1)
            shared_out(SH - 2)
            for e in range(4):
                turned(e + (SH - 1), 1 - e % 2)
                gated(e + SH, e % 2)
                if e:
                    routed_out(e - 1, 1 - e % 2, first=(e < 3))
                else:
                    shared_out(SH - 1)
            with dve.Fori(0, NE // 4 - 1) as i:
                for u in range(4):
                    turned(i * 4 + (u + 4 + SH - 1), 1 - u % 2)
                    gated(i * 4 + (u + 4 + SH), u % 2)
                    routed_out(i * 4 + (u + 3), 1 - u % 2)
            turned(JOBS - 1, 1)
            routed_out(NE - 1, 1)
            for n in range(NT * TOPK):
                t = n // TOPK
                dve.wait_ge(picked_loaded[n % 8], 16 * (n // 8 + 1))
                if n % TOPK:
                    dve.wait_ge(picked_used, n)
                nc.vector.scalar_tensor_tensor(x[:, t, :], picked[n % 8], top_w[:, n:n + 1], x[:, t, :], ALU.mult,
                                               ALU.add).then_inc(picked_used, 1)
                if n % TOPK == TOPK - 1:
                    dve.wait_ge(picked_used, n + 1)
                    norm_stats_dve(dve, link, 3, t)
                if n % TOPK == 2 and t:
                    norm_rows_dve(dve, 3, t - 1)
            norm_rows_dve(dve, 3, NT - 1)

        def s3_pool(pool, link):
            norm_pool(pool, link, 2, 1e-6)
            nc.gpsimd.tensor_tensor(x[:], x[:], xn[:], ALU.add).then_inc(x_biased, 1)
            pool.wait_ge(token_ready, 1)
            pool.wait_ge(h_stored, 16)

            def gather(e, par, first=False):
                if not first:
                    pool.wait_ge(xeT_ps, e - 1)
                    pool.wait_ge(xe_loaded[par], e * 8 - 8 * par)
                col = token[:, e:e + 1] if type(e) is int else token[:, bass.ds(e, 1)]
                link(nc.gpsimd.tensor_copy(token_at[par], col))
                nc.gpsimd.tensor_tensor(stat[:, 262:263], power[:, 0:1], power[:, 0:1], ALU.add)
                nc.gpsimd.indirect_dma_start(xe[par], None, scratch["h_rows"],
                                             bass.IndirectOffsetOnAxis(token_at[par], 0)).then_inc(xe_loaded[par], 16)
            for e in range(4):
                gather(e, e % 2, first=(e < 2))
            steps = NE // 4 - 1
            n0 = link.n
            with pool.Fori(0, steps) as i:
                link.base = i * 4
                for u in range(4):
                    gather(i * 4 + (4 + u), u % 2)
            link.n, link.base = n0 + 4 * steps, 0
            for par in range(2):
                pool.wait_ge(eo_stored[par], 16 * NE // 2)
            for n in range(NT * TOPK):
                if n >= 8:
                    pool.wait_ge(picked_used, n - 7)
                nc.gpsimd.indirect_dma_start(picked[n % 8], None, scratch["eo_rows"],
                                             bass.IndirectOffsetOnAxis(slot[:, n:n + 1], 0)).then_inc(picked_loaded[n % 8], 16)
                if n % TOPK == TOPK - 1 and n >= 2 * TOPK - 1:
                    norm_rstd_pool(pool, link, 3, n // TOPK - 1)
            norm_rstd_pool(pool, link, 3, NT - 1)

        def s3_loads_early(sp):
            for e in range(2):
                sp.dma_start(ring[e], T["w3"][e]).then_inc(ring_loaded[e], 16)

        def s3_sp(sp):
            sp.wait_ge(x_biased, 1)
            sp.dma_start(row_bias[:], T["norm3"].unsqueeze(0).broadcast_to([P, DM])).then_inc(row_loaded, 16)
            sp.wait_ge(scores2, B)
            sp.dma_start(w3s, T["w3s"]).then_inc(w3s_loaded, 16)
            sp.wait_ge(o2_ps, 2 * B)
            for e in range(2, 4):
                sp.dma_start(ring[e], T["w3"][e]).then_inc(ring_loaded[e], 16)
            projected[1].wait(sp, "rows", NT)
            sp.wait_ge(hn_ready, NT)
            sp.dma_start(scratch["h_rows"].rearrange("(t p) h -> p t h", p=P), hn).then_inc(h_stored, 16)
            if STAGES >= 4:
                s4_sp(sp)
            with sp.Fori(0, NE // 4 - 1) as i:
                for u in range(4):
                    e = i * 4 + u
                    sp.wait_ge(eo_ps, e + (SH + 1))
                    sp.dma_start(ring[u], T["w3"][bass.ds(e + 4, 1)].rearrange("a p c n -> p (a c) n")).then_inc(ring_loaded[u], 16)
                    sp.wait_ge(eo_ready, e + (SH + 1))
                    sp.dma_start(scratch["eo_rows"][bass.ds(e * CAP, CAP), :], eo[u % 2]).then_inc(eo_stored[u % 2], 16)
            for e in range(NE - 4, NE):
                sp.wait_ge(eo_ready, e + SH + 1)
                sp.dma_start(scratch["eo_rows"][e * CAP:(e + 1) * CAP, :], eo[e % 2]).then_inc(eo_stored[e % 2], 16)

        AT1 = LT * (DC + 1) + LT * DC + 7 * DC
        FIRST = AT1 // (3 * P)
        w4q = cut(RA, 0, KC, 2048)
        w4kq = cut(RB, 0, NH, 4 * P)
        w4qr = cut(RC, 0, NH // 2, 3 * P)
        w4kr = cut(RC, 3072, NH // 2, P)
        w_abs = ([cut(RE, 3 * P * h, 3, P) for h in range(FIRST)] +
                 [cut(RE, AT1 + 3 * P * h, 3, P) for h in range(NH - 1 - FIRST)] + [cut(RC, 4096, 3, P)])
        q_hk = [cut(RR, 512 * i, TOK) for i in range(2)]
        by_cos = cut(RR, 1024, 3, TOK)
        by_sin = cut(RR, 2560, 3, TOK)
        q_rot = [cut(RR, 4096 + 1536 * i, 3, TOK) for i in range(2)]
        cos_q = cut(RR, 7168, 3, S)
        sin_q = cut(RR, 7360, 3, S)
        q4 = cut(RQ, 0, B, NH * S)
        w4q_loaded, w4kq_loaded, w4r_loaded, rope_q_loaded, rope_k_loaded, w4o_loaded = (
            sem(n) for n in ("w4q_loaded", "w4kq_loaded", "w4r_loaded", "rope_q_loaded", "rope_k_loaded", "w4o_loaded"))
        qhk_ps, qhk_ready, wabs_ps, wabs_ready, qbig_ps, rope_taken, qrot_ready, qabs_ps, qabs_ready = (
            sem(n) for n in ("qhk_ps", "qhk_ready", "wabs_ps", "wabs_ready", "qbig_ps", "rope_taken", "qrot_ready", "qabs_ps", "qabs_ready"))

        def w_products_pe(pe):
            pe.wait_ge(w4r_loaded, 32)
            for h in range(NH):
                if h >= 2:
                    pe.wait_ge(wabs_ready, h - 1)
                half = slice(64 * (h // 8), 64 * (h // 8) + R)
                for c in range(3):
                    i = nc.tensor.matmul(ps[:, 2 + h % 2, c * P:(c + 1) * P], w4qr[half, h % 8, c * P:(c + 1) * P],
                                         w4kr[half, h % 8, :], start=True, stop=True)
                i.then_inc(wabs_ps, 1)

        def w_products_act(act):
            for h in range(NH):
                act.wait_ge(wabs_ps, h + 1)
                nc.scalar.copy(w_abs[h].rearrange("p c d -> p (c d)"), ps[:, 2 + h % 2, 0:3 * P]).then_inc(wabs_ready, 1)

        def heads4_pe(pe):
            def q_head(h):
                for kc in range(KC):
                    i = nc.tensor.matmul(ps[:, h % 2, :], w4q[:, kc, h * P:(h + 1) * P], xT[:, kc, :],
                                         start=(kc == 0), stop=(kc == KC - 1))
                i.then_inc(qhk_ps, 1)

            def q_big(h):
                pe.wait_ge(qhk_ready, h + 1)
                if h:
                    pe.wait_ge(rope_taken, h)
                for c in range(4):
                    i = nc.tensor.matmul(ps[:, 4 + c, :], w4kq[:, h, c * P:(c + 1) * P], q_hk[h % 2], start=True, stop=True)
                i.then_inc(qbig_ps, 1)

            def q_abs(h):
                pe.wait_ge(qrot_ready, h + 1)
                if h >= 2:
                    pe.wait_ge(qabs_ready, h - 1)
                for c in range(3):
                    i = nc.tensor.matmul(ps[:, 2 + h % 2, :], w_abs[h][:, c, :], q_rot[h % 2][:, c, :], start=(c == 0), stop=(c == 2))
                i.then_inc(qabs_ps, 1)
            pe.wait_ge(wabs_ready, NH)
            for t in range(NT):
                xT_pe(pe, 3, t, t)
            xT_ready(pe, 3)
            pe.wait_ge(w4q_loaded, 16)
            q_head(0)
            pe.wait_ge(w4kq_loaded, 16)
            for h in range(NH):
                if h + 1 < NH:
                    q_head(h + 1)
                q_big(h)
                if h:
                    q_abs(h - 1)
            for g in range(KG):
                keys_pe(pe, 0, 0, g, 2 + g % 2)
            q_abs(NH - 1)

        def heads4_act(act):
            for t in range(NT):
                xT_act(act, 3, t, t)

            def q_out(h):
                act.wait_ge(qabs_ps, h + 1)
                nc.scalar.copy(q4[:, :, h * S:(h + 1) * S], by_batch(ps[:, 2 + h % 2, :])).then_inc(qabs_ready, 1)
            for h in range(NH):
                act.wait_ge(qhk_ps, h + 1)
                if h >= 2:
                    act.wait_ge(qbig_ps, h - 1)
                nc.scalar.copy(q_hk[h % 2], ps[:, h % 2, :]).then_inc(qhk_ready, 1)
                if h >= 2:
                    q_out(h - 2)
                for n in range(3 * h, 3 * h + 3):
                    magnitude_act(act, n)
            q_out(NH - 2)
            for g in range(KG):
                keys_act(act, 0, 0, g, 2 + g % 2)
            q_out(NH - 1)

        def heads4_dve(dve, link):
            dve.wait_ge(rope_q_loaded, 16)
            all_batches = [P, 3, B, S]
            for h in range(NH):
                dve.wait_ge(qbig_ps, h + 1)
                if h:
                    dve.wait_ge(qrot_ready, h)
                nc.vector.tensor_tensor(by_cos.rearrange("p c (b s) -> p c b s", s=S),
                                        ps[:, 4:7, :].rearrange("p c (b s) -> p c b s", s=S),
                                        cos_q.unsqueeze(2).broadcast_to(all_batches), ALU.mult)
                for c, partner in ((0, 1), (1, 0), (2, 3)):
                    i = nc.vector.tensor_tensor(by_batch(by_sin[:, c, :]), by_batch(ps[:, 4 + partner, :]),
                                                sin_q[:, c, :].unsqueeze(1).broadcast_to([P, B, S]), ALU.mult)
                i.then_inc(rope_taken, 1)
                dve.wait_ge(rope_taken, h + 1)
                if h >= 2:
                    dve.wait_ge(qabs_ps, h - 1)
                nc.vector.tensor_tensor(q_rot[h % 2], by_cos, by_sin, ALU.add).then_inc(qrot_ready, 1)

        keys = [RA[:, P * LT * i:P * LT * (i + 1)] for i in range(2)]
        p4 = [cut(RA, P * LT * (2 + i), LT, P) for i in range(2)]
        key_max = [cut(RA, P * (4 * LT + i), P) for i in range(2)]
        diag = cut(RA, P * (4 * LT + 2), P)
        shift = cut(RA, P * (4 * LT + 3), P)
        w4kv = cut(RC, 0, NH, P)
        o_rows = [cut(RC, 4864 + P * i, P) for i in range(2)]
        vals = [cut(RE, AT1 * i, LT, DC + 1) for i in range(2)]
        cos_k = cut(RE, LT * (DC + 1), LT, DC)
        turned_half = cut(RE, LT * (DC + 1) + LT * DC, 7, DC)
        sin_k = xn[:].rearrange("p a b -> p (a b)")[:, 0:LT * DC].rearrange("p (j d) -> p j d", d=DC)
        o4 = cut(RR, 0, NH, TOK)
        l4 = cut(RQ, 0, NH, TOK)
        w4o = cut(RA, 0, NH, DM)
        row_rs = stat[:, 348:350]
        query_max = stat[:, 340:341]
        last_ps = ps[0:LAST, 6, 0:P]
        turn_ps = ps[:, 6, P:2 * P]
        max_ps = ps[:, 6, P:3 * P]
        o_ps = ps[:, 7, 0:DC + 1]
        keys_at = [ps[:, 7, :], ps[:, 6, 2 * P:4 * P], ps[:, 0, :], ps[:, 1, :]]
        ctx_loaded = [sem(f"ctx_loaded{i}") for i in range(2)]
        vals_ready, keys_ps, keys_ready, scores4, key_max_ready, max_turned, diag_ready, shift_ps, shift_ready, shifted4, exps4 = (
            sem(n) for n in ("vals_ready", "keys_ps", "keys_ready", "scores4", "key_max_ready", "max_turned", "diag_ready",
                             "shift_ps", "shift_ready", "shifted4", "exps4"))
        o_rows_ps, row_rs_ready, o_rows_ready, o4_ps, o4_ready = (sem(n) for n in ("o_rows_ps", "row_rs_ready", "o_rows_ready", "o4_ps", "o4_ready"))
        l4_ps, l4_act, l4_dve = (sem(n) for n in ("l4_ps", "l4_act", "l4_dve"))
        HP = NH // 2
        SPLIT = 6
        MAXIMA_AFTER = 7
        KEYS = [range(0, 4), range(4, 6), range(6, 10), range(10, 12), range(12, 13)]
        KG = len(KEYS)
        KEYS_AT = {5: (0, 1), 6: (2, 3), 7: (4,)}

        def key_rows(j):
            return P if j < LT - 1 else LAST

        def keys_pe(pe, b, u, g, k=0):
            if g == 0:
                pe.wait_ge(vals_ready, b + 1)
            if k >= 2 and g >= 2:
                pe.wait_ge(keys_ready, g - 1)
            for n, j in enumerate(KEYS[g]):
                r = key_rows(j)
                i = nc.tensor.transpose(keys_at[k][:, n * P:n * P + r], vals[u][0:r, j, 0:DC], ident[0:r, 0:r])
            i.then_inc(keys_ps, 1)

        def keys_act(act, b, u, g, k=0):
            act.wait_ge(keys_ps, b * KG + (g + 1))
            at, w = P * KEYS[g][0], P * len(KEYS[g]) if g < KG - 1 else LAST
            nc.scalar.copy(keys[u][:, at:at + w], keys_at[k][:, 0:w]).then_inc(keys_ready, 1)

        def turn_out_pe(pe, n, par):
            pe.wait_ge(o_rows_ready, n + 1)
            nc.tensor.transpose(turn_ps, o_rows[par], ident).then_inc(o4_ps, 1)

        def values_pe(pe, n, u, par, js):
            if 0 in js:
                pe.wait_ge(exps4, n * 2 + 1)
            for j in js:
                if j == SPLIT:
                    pe.wait_ge(exps4, n * 2 + 2)
                r = key_rows(j)
                i = nc.tensor.matmul(o_ps, p4[par][0:r, j, :], vals[u][0:r, j, :], start=(j == 0), stop=(j == LT - 1))
            if LT - 1 in js:
                i.then_inc(o_rows_ps, 1)

        def tile_pe(pe, b, u, hp, back=2, more=True):
            n, par = b * HP + hp, hp % 2
            turns = KEYS_AT.get(hp, ()) if more else ()
            before = (n - 1, u if hp else 1 - u, 1 - par)
            if hp == 0:
                pe.wait_ge(keys_ready, b * KG + KG)
            if back >= 2:
                pe.wait_ge(shifted4, n * 3 - 3)
            q = q4[:, b, hp * P:(hp + 1) * P] if type(b) is int else q4[:, bass.ds(b, 1), hp * P:(hp + 1) * P].rearrange("p a n -> p (a n)")
            for j in range(LT - 1):
                i = nc.tensor.matmul(ps[:, 3 * par + j // 4, (j % 4) * P:(j % 4 + 1) * P], keys[u][:, j * P:(j + 1) * P], q,
                                     start=True, stop=True)
                if j == 7:
                    i.then_inc(scores4, 1)
                if j == 3 and turns:
                    pe.wait_ge(o_rows_ready, n - 1)
                    keys_pe(pe, b + 1, 1 - u, turns[0], 0)
                if j == 4 and back >= 2:
                    pe.wait_ge(shifted4, n * 3 - 2)
                    if turns[1:]:
                        keys_pe(pe, b + 1, 1 - u, turns[1], 1)
                    turn_out_pe(pe, n - 2, par)
            if back >= 1:
                pe.wait_ge(shifted4, n * 3 - 2)
            if back >= 2:
                pe.wait_ge(o4_ready, n - 1)
            if turns:
                pe.wait_ge(keys_ready, b * KG + (KG + turns[-1] + 1))
            nc.tensor.matmul(last_ps, keys[u][:, LCTX - LAST:LCTX], q, start=True, stop=True).then_inc(scores4, 1)
            if back >= 1:
                values_pe(pe, *before, range(0, MAXIMA_AFTER))
            pe.wait_ge(key_max_ready, n + 1)
            nc.tensor.transpose(max_ps[:, 0:P], key_max[0], ident)
            nc.tensor.transpose(max_ps[:, P:2 * P], key_max[1], ident).then_inc(max_turned, 1)
            if back >= 1:
                values_pe(pe, *before, range(MAXIMA_AFTER, LT))
            pe.wait_ge(diag_ready, n + 1)
            nc.tensor.matmul(turn_ps, ones, diag, start=True, stop=True).then_inc(shift_ps, 1)

        def head_out_act(act, b, hp):
            act.wait_ge(o4_ps, b * HP + (hp + 1))
            nc.scalar.activation(o4[:, 2 * hp:2 * hp + 2, bass.ds(b * S, S)], turn_ps.rearrange("p (u s) -> p u s", s=S),
                                 ACT.Copy).then_inc(o4_ready, 1)

        def tile_act(act, b, u, hp, back=2, more=True):
            n, par = b * HP + hp, hp % 2
            turns = KEYS_AT.get(hp + 1, ()) if more else ()
            if type(b) is int and n in ROUND_AT:
                round_act(act, ROUND_AT[n])
            act.wait_ge(shift_ps, n + 1)
            nc.scalar.copy(shift, turn_ps).then_inc(shift_ready, 1)
            if back >= 1:
                rows_out_act(act, n - 1, 1 - par)
            for k, g in enumerate(turns[0:1]):
                keys_act(act, b + 1, 1 - u, g, k)
            if back >= 1:
                head_out_act(act, b if hp >= 1 else b - 1, (hp - 1) % HP)
            for k, g in enumerate(turns[1:]):
                keys_act(act, b + 1, 1 - u, g, k + 1)
            act.wait_ge(shifted4, n * 3 + 2)
            nc.scalar.activation(p4[par][:, 0:SPLIT, :], p4[par][:, 0:SPLIT, :], ACT.Exp)
            nc.scalar.activation(p4[par][0:LAST, LT - 1, :], p4[par][0:LAST, LT - 1, :], ACT.Exp).then_inc(exps4, 1)
            act.wait_ge(shifted4, n * 3 + 3)
            nc.scalar.activation(p4[par][:, SPLIT:LT - 1, :], p4[par][:, SPLIT:LT - 1, :], ACT.Exp).then_inc(exps4, 1)
            if type(b) is int and n in ROUND_AT:
                ternary_act(act, ROUND_AT[n])

        def sums_dve(dve, n, par):
            dve.wait_ge(o_rows_ps, n + 1)
            nc.vector.reciprocal(row_rs[:, par:par + 1], o_ps[:, DC:DC + 1]).then_inc(row_rs_ready, 1)

        def rows_out_act(act, n, par):
            act.wait_ge(row_rs_ready, n + 1)
            nc.scalar.activation(o_rows[par], o_ps[:, 0:DC], ACT.Copy, scale=row_rs[:, par:par + 1]).then_inc(o_rows_ready, 1)

        def tile_dve(dve, link, b, u, hp, back=2):
            n, par = b * HP + hp, hp % 2
            scores = ps[:, 3 * par:3 * par + 3, :].rearrange("p a (j q) -> p (a j) q", q=P)
            by_query = scores.rearrange("p j q -> p q j")
            if back >= 1:
                dve.wait_ge(max_turned, n)
            dve.wait_ge(scores4, n * 2 + 1)
            nc.vector.tensor_reduce(key_max[0], by_query[:, :, 0:8], AX, ALU.max)
            dve.wait_ge(scores4, n * 2 + 2)
            link(nc.vector.tensor_reduce(key_max[1], by_query[:, :, 8:LT - 1], AX, ALU.max))
            nc.vector.tensor_tensor(key_max[1][0:LAST], key_max[1][0:LAST], last_ps, ALU.max).then_inc(key_max_ready, 1)
            if type(b) is int and n in ROUND_AT:
                clip_dve(dve, ROUND_AT[n])
            dve.wait_ge(max_turned, n + 1)
            link(nc.vector.tensor_reduce(query_max, max_ps, AX, ALU.max))
            nc.vector.tensor_scalar(diag, ident, query_max, None, ALU.mult).then_inc(diag_ready, 1)
            if back >= 1:
                sums_dve(dve, n - 1, 1 - par)
            dve.wait_ge(shift_ready, n + 1)
            if back >= 2:
                dve.wait_ge(o_rows_ps, n - 1)
            nc.vector.tensor_tensor(p4[par][0:LAST, LT - 1, :], last_ps, shift[0:LAST], ALU.subtract).then_inc(shifted4, 1)
            for j0, j1 in ((0, SPLIT), (SPLIT, LT - 1)):
                nc.vector.tensor_tensor(p4[par][:, j0:j1, :], scores[:, j0:j1, :],
                                        shift.unsqueeze(1).broadcast_to([P, j1 - j0, P]), ALU.subtract).then_inc(shifted4, 1)

        def all_tiles(eng, tile, links=None):
            for u in range(2):
                for hp in range(HP):
                    tile(u, u, hp, back=min(2, u * HP + hp))
            n0 = links.n if links else 0
            per = LINKS * 2 * HP
            with eng.Fori(0, B // 2 - 2) as i:
                if links:
                    links.base = i * per
                for u in range(2):
                    for hp in range(HP):
                        tile(i * 2 + (2 + u), u, hp)
            if links:
                assert links.n == n0 + per
                links.n, links.base = n0 + per * (B // 2 - 2), 0
            for u in range(2):
                for hp in range(HP):
                    tile(B - 2 + u, u, hp, **({"more": False} if u and not links else {}))
        LINKS = 2

        def s4_pe(pe):
            heads4_pe(pe)
            pe.wait_ge(qabs_ready, NH)
            weight_scales_pe(pe)
            all_tiles(pe, lambda b, u, hp, **kw: tile_pe(pe, b, u, hp, **kw))
            n = B * HP
            pe.wait_ge(shifted4, n * 3 - 2)
            turn_out_pe(pe, n - 2, 0)
            values_pe(pe, n - 1, 1, 1, range(LT))
            pe.wait_ge(o4_ready, n - 1)
            turn_out_pe(pe, n - 1, 1)
            pe.wait_ge(o4_ready, n)
            pe.wait_ge(w4r_loaded, 48)
            for h in range(NH):
                if h >= 8:
                    pe.wait_ge(l4_dve if h % 2 else l4_act, (h - 8) // 2 + 1)
                nc.tensor.matmul(ps[:, h % 8, :], w4kv[:, h, :], o4[:, h, :], start=True, stop=True).then_inc(l4_ps, 1)
            pe.wait_ge(l4_act, NH // 2)
            pe.wait_ge(l4_dve, NH // 2)
            pe.wait_ge(w4o_loaded, 16)
            for t in range(NT):
                rows_pe(pe, projected[2], t, t, l4, w4o)
                if t >= 1:
                    xT_pe(pe, 4, t - 1, t - 1)

        def s4_act(act):
            heads4_act(act)
            all_tiles(act, lambda b, u, hp, **kw: tile_act(act, b, u, hp, **kw))
            rows_out_act(act, B * HP - 1, 1)
            head_out_act(act, B - 1, HP - 1)
            for h in range(0, NH, 2):
                act.wait_ge(l4_ps, h + 1)
                nc.scalar.copy(l4[:, h, :], ps[:, h % 8, :]).then_inc(l4_act, 1)

        def s4_dve(dve, link):
            heads4_dve(dve, link)
            weight_scales_dve(dve, link)
            all_tiles(dve, lambda b, u, hp, **kw: tile_dve(dve, link, b, u, hp, **kw), link)
            n = B * HP
            sums_dve(dve, n - 1, 1)
            for h in range(1, NH, 2):
                dve.wait_ge(l4_ps, h + 1)
                nc.vector.tensor_copy(l4[:, h, :], ps[:, h % 8, :]).then_inc(l4_dve, 1)
            residual_dve(dve, link, 4, lambda t: projected[2].wait(dve, "rows", t + 1), lambda t: ps[:, t, :], lag=0)

        def s4_pool(pool, link):
            pool.wait_ge(rope_k_loaded, 32)

            def batch(b, u, first=False):
                pool.wait_ge(ctx_loaded[u], b * 16 + 32 - 16 * u)
                v = vals[u]
                if first:
                    nc.gpsimd.memset(v[:, :, DC:DC + 1], 1.0)
                for j0, j1 in ((0, 7), (7, LT)):
                    half, n = turned_half[:, 0:j1 - j0, :], DC // 2
                    part = v[:, j0:j1, 0:DC]
                    link(nc.gpsimd.tensor_tensor(half[:, :, 0:n], part[:, :, n:DC], sin_k[:, j0:j1, 0:n], ALU.mult))
                    link(nc.gpsimd.tensor_tensor(half[:, :, n:DC], part[:, :, 0:n], sin_k[:, j0:j1, n:DC], ALU.mult))
                    link(nc.gpsimd.tensor_tensor(part, part, cos_k[:, j0:j1, :], ALU.mult))
                    i = nc.gpsimd.tensor_tensor(part, part, half, ALU.add)
                    if j0 == 0:
                        link(i)
                i.then_inc(vals_ready, 1)
                pool.wait_ge(vals_ready, b + 1)
            for u in range(2):
                batch(u, u, first=True)
            n0, per = link.n, 2 * 7
            with pool.Fori(0, B // 2 - 1) as i:
                link.base = i * per
                for u in range(2):
                    batch(i * 2 + (2 + u), u)
            assert link.n == n0 + per
            link.n, link.base = n0 + per * (B // 2 - 1), 0

        def ctx_rows(b):
            rows = T["ctx"][b] if type(b) is int else T["ctx"][bass.ds(b, 1)].rearrange("a l d -> (a l) d")
            return (rows[0:(LT - 1) * P, :].rearrange("(j p) d -> p j d", p=P), rows[(LT - 1) * P:LCTX, :])

        def ctx_sp(sp, b, u):
            full, rest = ctx_rows(b)
            sp.dma_start(vals[u][:, 0:LT - 1, 0:DC], full).then_inc(ctx_loaded[u], 16)
            sp.dma_start(vals[u][0:LAST, LT - 1, 0:DC], rest).then_inc(ctx_loaded[u], 16)

        def s4_sp(sp):
            sp.dma_start(w4kq, T["w4kq"]).then_inc(w4kq_loaded, 16)
            sp.dma_start(w4q, T["w4q"]).then_inc(w4q_loaded, 16)
            sp.wait_ge(h_stored, 16)
            norms[2].wait(sp, "xT_ps", NT)
            sp.dma_start(w4qr, T["w4qr"]).then_inc(w4r_loaded, 16)
            sp.dma_start(w4kr, T["w4kr"]).then_inc(w4r_loaded, 16)

        def s4_sp_main(sp):
            sp.wait_ge(picked_used, NT * TOPK)
            sp.dma_start(RR[:, 7168:7168 + 6 * S], T["rope_q"]).then_inc(rope_q_loaded, 16)
            norms[3].wait(sp, "xT_ps", NT)
            sp.dma_start(sin_k, T["rope_k"][1]).then_inc(rope_k_loaded, 16)
            for n in range(MAG):
                if n == 3 * (FIRST + 1):
                    sp.wait_ge(qabs_ps, FIRST)
                    ctx_sp(sp, 0, 0)
                    sp.dma_start(cos_k, T["rope_k"][0]).then_inc(rope_k_loaded, 16)
                if n >= 2:
                    sp.wait_ge(magnitudes_taken, n - 1)
                sp.dma_start(mag[n % 2], T["w6"][:, n * MAGW:(n + 1) * MAGW]).then_inc(mag_loaded[n % 2], 16)
            sp.wait_ge(qbig_ps, NH)
            sp.dma_start(w4kv, T["w4kv"]).then_inc(w4r_loaded, 16)
            sp.wait_ge(qabs_ps, NH)
            ctx_sp(sp, 1, 1)
            sp.wait_ge(magnitudes_taken, MAG)
            for m in range(0, 11):
                raw_sp(sp, m)
            for u in range(2):
                sp.wait_ge(o_rows_ps, 8 + 8 * u)
                ctx_sp(sp, 2 + u, u)
                if u == 0:
                    for m in range(11, 19):
                        raw_sp(sp, m)
            with sp.Fori(0, B // 2 - 2) as i:
                for u in range(2):
                    sp.wait_ge(o_rows_ps, i * 16 + (24 + 8 * u))
                    ctx_sp(sp, i * 2 + (4 + u), u)
            for m in range(19, RAW):
                raw_sp(sp, m)
            sp.wait_ge(o_rows_ps, B * HP)
            sp.dma_start(w4o, T["w4o"]).then_inc(w4o_loaded, 16)

        w5 = cut(RE, 0, 3, KC * DM).rearrange("p w (c n) -> p w c n", n=DM)
        w5o = cut(RC, 0, KC, DM)
        b5q, b5k, b5v = (vecs[:, 18 + 4 * i:22 + 4 * i] for i in range(3))
        H5 = H1.again()
        w5_loaded, b5_loaded = sem("w5_loaded"), sem("b5_loaded")

        def s5_pe(pe):
            xT_pe(pe, 4, NT - 1, NT - 1)
            xT_ready(pe, 4)
            pe.wait_ge(w5_loaded, 16)
            for t in range(NT):
                for kc in range(KC):
                    i = nc.tensor.matmul(ps[:, 4 + t, :], xT[:, kc, t * P:(t + 1) * P], w5[:, 2, kc, :],
                                         start=(kc == 0), stop=(kc == KC - 1))
                i.then_inc(H5["v_ps"], 1)
            for which, base, done in ((0, 0, H5["q_ps"]), (1, 4, H5["k_ps"])):
                for c in range(KC):
                    if which:
                        H5.wait(pe, "v_act", c + 1)
                        H5.wait(pe, "v_dve", c + 1)
                    for kc in range(KC):
                        i = nc.tensor.matmul(ps[:, base + c, :], w5[:, which, kc, c * P:(c + 1) * P], xT[:, kc, :],
                                             start=(kc == 0), stop=(kc == KC - 1))
                    i.then_inc(done, 1)
            heads_pe(pe, H5, w5o, lambda: [H5.wait(pe, "swapped", 32), pe.wait_ge(w5_loaded, 32)], projected[3], None)

        def s5_act(act):
            for t in range(NT):
                xT_act(act, 4, t, t)
            values_act(act, H5)
            act.wait_ge(b5_loaded, 16)
            for c in range(KC):
                H5.wait(act, "q_ps", c + 1)
                nc.scalar.activation(mh_q[:, c, :], ps[:, c, :], ACT.Identity, bias=b5q[:, c:c + 1]).then_inc(H5["q"], 1)
            heads_act(act, H5, b5v)

        def s5_dve(dve, link):
            values_dve(dve, H5)
            dve.wait_ge(b5_loaded, 16)
            for c in range(KC):
                H5.wait(dve, "k_ps", c + 1)
                nc.vector.tensor_scalar(mh_k[:, c, :], ps[:, 4 + c, :], b5k[:, c:c + 1], None, ALU.add).then_inc(H5["k"], 1)
            heads_dve(dve, link, H5, False)
            dve.wait_ge(x_biased, 3)
            if STAGES < 6:
                residual_dve(dve, link, 5, lambda t: projected[3].wait(dve, "rows", t + 1), lambda t: ps[:, 4 + t, :])

        def s5_pool(pool, link):
            norm_pool(pool, link, 4)
            norms[4].wait(pool, "xn", NT)
            pool.wait_ge(row_loaded, 32)
            nc.gpsimd.tensor_tensor(x[:], x[:], row_bias[:].unsqueeze(1).broadcast_to([P, NT, DM]), ALU.add).then_inc(x_biased, 1)

        def s5_sp(sp):
            sp.wait_ge(row_loaded, 16)
            sp.wait_ge(hn_ready, NT)
            sp.dma_start(row_bias[:], T["b5o"].unsqueeze(0).broadcast_to([P, DM])).then_inc(row_loaded, 16)
            sp.dma_start(vecs[:, 18:30], T["vec5"]).then_inc(b5_loaded, 16)
            sp.dma_start(RE[:], T["w5"][:, 0:3 * KC * DM]).then_inc(w5_loaded, 16)
            sp.wait_ge(w5_loaded, 16)
            sp.wait_ge(l4_ps, NH)
            sp.dma_start(RC[:, 0:KC * DM], T["w5"][:, 3 * KC * DM:]).then_inc(w5_loaded, 16)

        WGU, WDN = KC * 2 * FF, FF * DM // P
        MAG = 48
        MAGW = (WGU + WDN) // MAG
        MAG_GU = WGU // MAGW
        RAW = 24
        RAWW = (WGU + WDN) // RAW
        RAW_GU = WGU // RAWW
        ROUND_AT = {m if m < RAW_GU else (B - 2) * HP + m - RAW_GU: m for m in range(RAW)}
        mag = [cut(RG, MAGW * i, MAGW) for i in range(2)]
        raw = [cut(RB, WGU // 2 + RAWW * i, RAWW) for i in range(3)]
        mag_sum = stat[:, 350:350 + MAG]
        mag_total, w_mean, w_scale = stat[:, 400:402], stat[:, 494:496], stat[:, 492:494]
        ident16 = stat[:, 402:466].bitcast(BF16)
        w6gu = RB[:, 0:WGU // 2].bitcast(BF16)
        w6d = RC[:, 2048:2048 + WDN // 2].bitcast(BF16)
        mag_loaded = ring_loaded[0:2]
        raw_loaded = ring_loaded[1:4]
        BEFORE_MAG = 16 * NE // 4
        BEFORE_RAW = [BEFORE_MAG + 16 * MAG // 2, BEFORE_MAG, BEFORE_MAG]
        magnitudes_taken, mag_total_ready, mag_ps, w_scale_ready, rounded, clipped, ternary_ready = (
            sem(n) for n in ("magnitudes_taken", "mag_total_ready", "mag_ps", "w_scale_ready", "rounded", "clipped", "ternary_ready"))
        ROUND = 1.5 * 2.0 ** 23

        def magnitude_act(act, n):
            act.wait_ge(mag_loaded[n % 2], BEFORE_MAG + 16 * (n // 2 + 1))
            nc.scalar.activation(mag[n % 2], mag[n % 2], ACT.Abs, accum_out=mag_sum[:, n:n + 1]).then_inc(magnitudes_taken, 1)

        def weight_scales_pe(pe):
            pe.wait_ge(mag_total_ready, 1)
            nc.tensor.matmul(ps[:, 3, 0:2], ones, mag_total, start=True, stop=True).then_inc(mag_ps, 1)
            pe.wait_ge(w_scale_ready, 1)

        def weight_scales_dve(dve, link):
            dve.wait_ge(magnitudes_taken, MAG)
            nc.vector.memset(round_up, ROUND)
            nc.vector.memset(round_down, -ROUND)
            nc.vector.tensor_reduce(mag_total[:, 0:1], mag_sum[:, 0:MAG_GU], AX, ALU.add)
            link(nc.vector.tensor_reduce(mag_total[:, 1:2], mag_sum[:, MAG_GU:MAG], AX, ALU.add))
            nc.vector.tensor_copy(ident16, ident).then_inc(mag_total_ready, 1)
            dve.wait_ge(mag_ps, 1)
            nc.vector.tensor_scalar(w_mean[:, 0:1], ps[:, 3, 0:1], 1.0 / (P * WGU), 1e-5, ALU.mult, ALU.max)
            link(nc.vector.tensor_scalar(w_mean[:, 1:2], ps[:, 3, 1:2], 1.0 / (P * WDN), 1e-5, ALU.mult, ALU.max))
            nc.vector.reciprocal(w_scale, w_mean).then_inc(w_scale_ready, 1)

        def raw_sp(sp, m):
            if m >= 3:
                sp.wait_ge(ternary_ready, m - 2)
            sp.dma_start(raw[m % 3], T["w6"][:, m * RAWW:(m + 1) * RAWW]).then_inc(raw_loaded[m % 3], 16)

        round_up, round_down = stat[:, 350 + MAG:351 + MAG], stat[:, 351 + MAG:352 + MAG]

        def round_act(act, m):
            i = int(m >= RAW_GU)
            act.wait_ge(w_scale_ready, 1)
            act.wait_ge(raw_loaded[m % 3], BEFORE_RAW[m % 3] + 16 * (m // 3 + 1))
            nc.scalar.activation(raw[m % 3], raw[m % 3], ACT.Identity, bias=round_up, scale=w_scale[:, i:i + 1]).then_inc(rounded, 1)

        def clip_dve(dve, m):
            dve.wait_ge(rounded, m + 1)
            nc.vector.tensor_scalar(raw[m % 3], raw[m % 3], ROUND - 1.0, ROUND + 1.0, ALU.max, ALU.min).then_inc(clipped, 1)

        def ternary_act(act, m):
            act.wait_ge(clipped, m + 1)
            dst = w6gu[:, m * RAWW:(m + 1) * RAWW] if m < RAW_GU else w6d[:, (m - RAW_GU) * RAWW:(m - RAW_GU + 1) * RAWW]
            nc.scalar.activation(dst, raw[m % 3], ACT.Identity, bias=round_down).then_inc(ternary_ready, 1)

        def s6_pool(pool, link):
            norm_pool(pool, link, 5, 1e-5)

        h6 = cut(RR, 0, NT, DM)
        xq = RR[:, 2048:3072].bitcast(BF16).rearrange("p (t n) -> p t n", t=NT)
        xqT = RR[:, 3072:4096].bitcast(BF16).rearrange("p (c n) -> p c n", c=KC)
        relu6 = [cut(RQ, 512 * i, 512) for i in range(2)]
        relu2 = [cut(RQ, 1024 + 512 * i, 512) for i in range(2)]
        hid = [cut(RQ, 2048 + FF * i, FF) for i in range(2)]
        hq = [RQ[:, 4864 + FF // 2 * i:4864 + FF // 2 * (i + 1)].bitcast(BF16) for i in range(2)]
        FC = FF // P
        hqT = [RQ[:, 6272 + FF // 2 * i:6272 + FF // 2 * (i + 1)].bitcast(BF16).rearrange("p (c n) -> p c n", n=P) for i in range(2)]
        top6, scale6, alpha6 = stat[:, 466:470], stat[:, 470:474], stat[:, 474:478]
        toph, scaleh, deltah = stat[:, 478:482], stat[:, 482:486], stat[:, 486:490]
        HALVES = [(0, 6), (6, FC)]
        piece_top = stat[:, 64:67]
        PIECE6 = [(512 * i, min(512, FF - 512 * i)) for i in range(3)]
        xq_ready, xqT_ps, xqT_ready, alpha_ready, gu6_ps, relu_ready, hid_ready, hq_ready, hqT_ps, hqT_ready, down6_ps = (
            sem(n) for n in ("xq_ready", "xqT_ps", "xqT_ready", "alpha_ready", "gu6_ps", "relu_ready",
                             "hid_ready", "hq_ready", "hqT_ps", "hqT_ready", "down6_ps"))

        def s6_pe(pe):
            pe.wait_ge(ternary_ready, RAW)

            def turn_rows(t):
                pe.wait_ge(xq_ready, t + 1)
                for kc in range(KC):
                    i = nc.tensor.transpose(ps[:, 4 + t, :].bitcast(BF16)[:, kc * P:(kc + 1) * P], xq[:, t, kc * P:(kc + 1) * P], ident16)
                i.then_inc(xqT_ps, 1)

            def down(t):
                for k, (c0, c1) in enumerate(HALVES):
                    pe.wait_ge(hq_ready, 2 * t + k + 1)
                    for c in range(c0, c1):
                        i = nc.tensor.transpose(ps[:, 4 + k, :].bitcast(BF16)[:, (c - c0) * P:(c - c0 + 1) * P],
                                                hq[t % 2][:, c * P:(c + 1) * P], ident16)
                    i.then_inc(hqT_ps, 1)
                if t:
                    pe.wait_ge(x_final, t)
                for c in range(FC):
                    if c in (HALVES[0][0], HALVES[1][0]):
                        pe.wait_ge(hqT_ready, 2 * t + 1 + (c > 0))
                    i = nc.tensor.matmul(ps[:, 6, :], hqT[t % 2][:, c, :], w6d[:, c * DM:(c + 1) * DM],
                                         start=(c == 0), stop=(c == FC - 1))
                i.then_inc(down6_ps, 1)
            turn_rows(0)
            turn_rows(1)
            for t in range(NT):
                for n, (at, w) in enumerate(PIECE6):
                    m = 3 * t + n
                    if m == 1:
                        turn_rows(2)
                        turn_rows(3)
                    if m >= 2:
                        pe.wait_ge(hid_ready, m - 1)
                    if n == 0:
                        pe.wait_ge(xqT_ready, t + 1)
                    for up in range(2):
                        for kc in range(KC):
                            col = (2 * kc + up) * FF + at
                            i = nc.tensor.matmul(ps[:, 2 * (m % 2) + up, 0:w], xqT[:, kc, t * P:(t + 1) * P], w6gu[:, col:col + w],
                                                 start=(kc == 0), stop=(kc == KC - 1))
                    i.then_inc(gu6_ps, 1)
                if t:
                    down(t - 1)
            down(NT - 1)

        def s6_act(act):
            for n in range(NT + 3):
                if n < NT:
                    norms[5].wait(act, "xn", n + 1)
                    nc.scalar.activation(h6[:, n, :], xn[:, n, :], ACT.Square, accum_out=sq[:, n:n + 1]).then_inc(sq_ready, 1)
                t = n - 1
                if 0 <= t < NT:
                    act.wait_ge(scaleh_ready, t + 1)
                    nc.scalar.activation(h6[:, t, :], h6[:, t, :], ACT.Identity, bias=round_up, scale=scale6[:, t:t + 1]).then_inc(rounded, 1)
                t = n - 2
                if 0 <= t < NT:
                    act.wait_ge(clipped, RAW + t + 1)
                    nc.scalar.activation(xq[:, t, :], h6[:, t, :], ACT.Identity, bias=round_down).then_inc(xq_ready, 1)
                t = n - 3
                if 0 <= t < NT:
                    act.wait_ge(xqT_ps, t + 1)
                    nc.scalar.copy(xqT[:, :, t * P:(t + 1) * P],
                                   ps[:, 4 + t, :].bitcast(BF16)[:, 0:DM].rearrange("p (c n) -> p c n", n=P)).then_inc(xqT_ready, 1)
            act.wait_ge(alpha_ready, NT)

            def quantise(t):
                v = hid[t % 2]
                act.wait_ge(scaleh_ready, NT + t + 1)
                for c0, c1 in HALVES:
                    part = v[:, c0 * P:c1 * P]
                    nc.scalar.activation(part, part, ACT.Identity, bias=round_up, scale=scaleh[:, t:t + 1]).then_inc(rounded, 1)
                for k, (c0, c1) in enumerate(HALVES):
                    act.wait_ge(clipped, RAW + NT + 2 * t + k + 1)
                    nc.scalar.activation(hq[t % 2][:, c0 * P:c1 * P], v[:, c0 * P:c1 * P], ACT.Identity, bias=round_down).then_inc(hq_ready, 1)

            def turned(t):
                for k, (c0, c1) in enumerate(HALVES):
                    act.wait_ge(hqT_ps, 2 * t + k + 1)
                    nc.scalar.copy(hqT[t % 2][:, c0:c1, :].rearrange("p c n -> p (c n)"),
                                   ps[:, 4 + k, :].bitcast(BF16)[:, 0:(c1 - c0) * P]).then_inc(hqT_ready, 1)
            for m in range(3 * NT):
                t, w = m // 3, PIECE6[m % 3][1]
                act.wait_ge(gu6_ps, m + 1)
                if m >= 2:
                    act.wait_ge(hid_ready, m - 1)
                    act.wait_ge(relu_ready, m - 1)
                nc.scalar.activation(relu6[m % 2][:, 0:w], ps[:, 2 * (m % 2), 0:w], ACT.Relu, scale=alpha6[:, t:t + 1]).then_inc(relu_done, 1)
                act.wait_ge(relu_done, m + 1)
                nc.scalar.activation(relu2[m % 2][:, 0:w], relu6[m % 2][:, 0:w], ACT.Square).then_inc(relu_ready, 1)
                if m % 3 == 2:
                    if t:
                        turned(t - 1)
                    quantise(t)
            turned(NT - 1)

        relu_done, scaleh_ready = sem("relu_done"), sem("scaleh_ready")

        def s6_dve(dve, link):
            for n in range(NT + 3):
                if n < NT:
                    projected[3].wait(dve, "rows", n + 1)
                    link(nc.vector.tensor_tensor(x[:, n, :], x[:, n, :], ps[:, 4 + n, :], ALU.add))
                    norm_stats_dve(dve, link, 5, n)
                if 0 <= n - 1 < NT:
                    norm_rows_dve(dve, 5, n - 1)
                t = n - 2
                if 0 <= t < NT:
                    if t == 0:
                        dve.wait_ge(row_loaded, 48)
                    dve.wait_ge(rms_ready, NT + t + 1)
                    top, scale = top6[:, t:t + 1], scale6[:, t:t + 1]
                    link(nc.vector.scalar_tensor_tensor(h6[:, t, :], xn[:, t, :], rms[:, t:t + 1], row_bias[:], ALU.mult, ALU.mult))
                    link(nc.vector.tensor_reduce(top, h6[:, t, :], AX, ALU.max, apply_absolute_value=True))
                    link(nc.vector.tensor_scalar(top, top, 1e-5, None, ALU.max))
                    link(nc.vector.reciprocal(scale, top))
                    nc.vector.tensor_scalar(scale, scale, 127.0, None, ALU.mult).then_inc(scaleh_ready, 1)
                    nc.vector.tensor_scalar(alpha6[:, t:t + 1], top, 1.0 / 127.0, w_mean[:, 0:1], ALU.mult, ALU.mult).then_inc(alpha_ready, 1)
                t = n - 3
                if 0 <= t < NT:
                    dve.wait_ge(rounded, RAW + t + 1)
                    nc.vector.tensor_scalar(h6[:, t, :], h6[:, t, :], ROUND - 128.0, ROUND + 127.0, ALU.max, ALU.min).then_inc(clipped, 1)
            dve.wait_ge(alpha_ready, NT)

            def down(t):
                dve.wait_ge(down6_ps, t + 1)
                nc.vector.scalar_tensor_tensor(x[:, t, :], ps[:, 6, :], deltah[:, t:t + 1], x[:, t, :], ALU.mult,
                                               ALU.add).then_inc(x_final, 1)
            def clip(t):
                v = hid[t % 2]
                for k, (c0, c1) in enumerate(HALVES):
                    dve.wait_ge(rounded, RAW + NT + 2 * t + k + 1)
                    nc.vector.tensor_scalar(v[:, c0 * P:c1 * P], v[:, c0 * P:c1 * P], ROUND - 128.0, ROUND + 127.0,
                                            ALU.max, ALU.min).then_inc(clipped, 1)
            for t in range(NT):
                v = hid[t % 2]
                for n, (at, w) in enumerate(PIECE6):
                    m = 3 * t + n
                    dve.wait_ge(relu_ready, m + 1)
                    nc.vector.scalar_tensor_tensor(v[:, at:at + w], ps[:, 2 * (m % 2) + 1, 0:w], alpha6[:, t:t + 1],
                                                   relu2[m % 2][:, 0:w], ALU.mult, ALU.mult).then_inc(hid_ready, 1)
                    dve.wait_ge(hid_ready, m + 1)
                    i = nc.vector.tensor_reduce(piece_top[:, n:n + 1], v[:, at:at + w], AX, ALU.max, apply_absolute_value=True)
                link(i)
                link(nc.vector.tensor_reduce(toph[:, t:t + 1], piece_top, AX, ALU.max))
                link(nc.vector.tensor_scalar(toph[:, t:t + 1], toph[:, t:t + 1], 1e-5, None, ALU.max))
                link(nc.vector.reciprocal(scaleh[:, t:t + 1], toph[:, t:t + 1]))
                nc.vector.tensor_scalar(scaleh[:, t:t + 1], scaleh[:, t:t + 1], 127.0, None, ALU.mult).then_inc(scaleh_ready, 1)
                link(nc.vector.tensor_scalar(deltah[:, t:t + 1], toph[:, t:t + 1], 1.0 / 127.0, w_mean[:, 1:2], ALU.mult, ALU.mult))
                clip(t)
                if t:
                    down(t - 1)
            down(NT - 1)

        def s6_sp(sp):
            swap_values(sp, H5)
            sp.wait_ge(x_biased, 3)
            sp.dma_start(row_bias[:], T["norm6"].unsqueeze(0).broadcast_to([P, DM])).then_inc(row_loaded, 16)

        block = ctx.enter_context(nc.Block())

        @block.sync
        def _(sp):
            sp.dma_start(cst[:], T["cst"]).then_inc(cst_loaded, 16)
            for u in range(2):
                sp.dma_start(c64[64 * u:64 * u + S, :, :],
                             T["ctx"][:, 0:S, :].rearrange("(t u) l d -> u l t d", u=2)[u]).then_inc(c64_loaded, 16)
            sp.dma_start(w1kv, T["w1kv"]).then_inc(w1_loaded, 16)
            sp.dma_start(x[:], T["x"].rearrange("b s h -> (b s) h").rearrange("(t p) h -> p t h", p=P)).then_inc(x_loaded, 16)
            sp.dma_start(w1q, T["w1q"]).then_inc(w1q_loaded, 16)
            sp.dma_start(w1o, T["w1o"]).then_inc(w1o_loaded, 16)
            sp.dma_start(vecs[:, 0:18], T["vec2"]).then_inc(w2_loaded, 16)
            sp.dma_start(w2kv, T["w2kv"]).then_inc(w2_loaded, 16)
            sp.dma_start(w2q, T["w2q"]).then_inc(w2q_loaded, 16)
            sp.dma_start(row_bias[:], T["b2o"].unsqueeze(0).broadcast_to([P, DM])).then_inc(w2_loaded, 16)
            sp.dma_start(w2o, T["w2o"]).then_inc(w2o_loaded, 16)
            sp.dma_start(gate[:], T["gate"]).then_inc(gate_loaded, 16)
            if STAGES >= 3:
                s3_loads_early(sp)
            swap_values(sp, H1)
            sp.wait_ge(v2_ready, 2)
            for u in range(2):
                pairs = v2.rearrange("p (t u) d -> p u t d", u=2)
                sp.dma_start(pairs[64 * (1 - u):64 * (1 - u) + S, u], pairs[64 * u:64 * u + S, u]).then_inc(v2_swapped, 16)
            if STAGES >= 3:
                s3_sp(sp)
            if STAGES >= 4:
                s4_sp_main(sp)
            if STAGES >= 5:
                s5_sp(sp)
            if STAGES == 5:
                swap_values(sp, H5)
            if STAGES >= 6:
                s6_sp(sp)
            for t in range(NT):
                sp.wait_ge(x_final, t + 1)
                sp.dma_start(out.rearrange("b s h -> (b s) h").rearrange("(t p) h -> p t h", p=P)[:, t, :], x[:, t, :]).then_inc(out_stored, 16)
            sp.wait_ge(out_stored, 16 * NT)

        @block.gpsimd
        def _(pool):
            link = Chain(pool, "pool_chain")
            norm_pool(pool, link, 0)
            if STAGES >= 2:
                norm_pool(pool, link, 1)
                norms[1].wait(pool, "xn", NT)
                pool.wait_ge(w2_loaded, 48)
                nc.gpsimd.tensor_tensor(x[:], x[:], row_bias[:].unsqueeze(1).broadcast_to([P, NT, DM]), ALU.add).then_inc(x_biased, 1)
            if STAGES >= 3:
                s3_pool(pool, link)
            if STAGES >= 4:
                s4_pool(pool, link)
            if STAGES >= 5:
                s5_pool(pool, link)
            if STAGES >= 6:
                s6_pool(pool, link)

        @block.tensor
        def _(pe):
            s1_pe(pe)
            if STAGES >= 2:
                s2_pe(pe)
            if STAGES >= 3:
                s3_pe(pe)
            if STAGES >= 4:
                s4_pe(pe)
            if STAGES >= 5:
                s5_pe(pe)
            if STAGES >= 6:
                s6_pe(pe)

        @block.scalar
        def _(act):
            s1_act(act)
            if STAGES >= 2:
                s2_act(act)
            if STAGES >= 3:
                s3_act(act)
            if STAGES >= 4:
                s4_act(act)
            if STAGES >= 5:
                s5_act(act)
            if STAGES >= 6:
                s6_act(act)

        @block.vector
        def _(dve):
            link = Chain(dve, "dve_chain")
            s1_dve(dve, link)
            if STAGES >= 2:
                s2_dve(dve, link)
            if STAGES >= 3:
                s3_dve(dve, link)
            if STAGES >= 4:
                s4_dve(dve, link)
            if STAGES >= 5:
                s5_dve(dve, link)
            if STAGES >= 6:
                s6_dve(dve, link)
            if STAGES < 6:
                for t in range(4):
                    nc.vector.memset(stat[:, 45:46], 0.0).then_inc(x_final, 1)


def constants():
    import numpy as np
    n = np.arange(P)
    c = np.zeros((P, 5, P), np.float32)
    c[:, 0] = n[:, None] == n[None, :]
    c[:, 1] = n[:, None] < n[None, :]
    c[:, 2] = 1.0
    c[:, 3] = n[None, :]
    for t in range(NT):
        c[:, 4, S + 2 * t], c[:, 4, S + 2 * t + 1] = n, t * P
    c[:, 4, 0:S] = np.where(n[None, :S] <= n[:, None] % S, 0.0, MASKED)
    return c


def rope_tables(length, dim):
    import numpy as np
    f32 = np.float32
    inv = f32(1.0) / f32(10000.0) ** (np.arange(0, dim, 2, dtype=f32) / f32(dim))
    f = np.arange(length, dtype=f32)[:, None] * inv[None, :]
    return np.repeat(np.sin(f), 2, -1), np.repeat(np.cos(f), 2, -1)


def rope_queries():
    import numpy as np
    sin, cos = rope_tables(S, DCQ)
    sin = np.where(np.arange(DCQ) < DCQ // 2, -sin, sin)
    cols = query_columns()[:3]
    return np.stack([tab[:, c].T for tab in (cos, sin) for c in cols], 1).reshape(P, 6 * S)


def rope_context():
    import numpy as np
    sin, cos = rope_tables(LCTX, DC)
    sin = np.where(np.arange(DC) < DC // 2, -sin, sin)
    tabs = np.zeros((2, LT * P, DC), np.float32)
    tabs[0, :LCTX], tabs[1, :LCTX] = cos, sin
    return tabs.reshape(2, LT, P, DC).transpose(0, 2, 1, 3)


def query_columns():
    import numpy as np
    h = DCQ // 2
    return [np.arange(P), np.arange(h, h + P), np.r_[P:h, h + P:DCQ], np.r_[h + P:DCQ, P:h]]


def kernel(**inputs):
    import numpy as np
    import concourse.bacc as bacc
    from concourse.bass_utils import run_bass_kernel_spmd as run

    def chunks(w):
        return w.reshape(w.shape[0] // P, P, w.shape[1]).transpose(1, 0, 2)

    I = {k: np.asarray(v) for k, v in inputs.items()}
    T = {
        "x": I["x"], "ctx": I["ctx_512"], "cst": constants(),
        "w1q": chunks(I["L0_xattn_Wq"].T), "w1kv": I["L0_xattn_Wkv_expand"].T, "w1o": chunks(I["L0_xattn_Wout"].T),
        "vec2": np.concatenate([I["L0_attn_bq"].reshape(NH, P).T, I["L0_attn_bk"][:, None], I["L0_attn_bv"][:, None]], 1),
        "w2kv": np.stack([chunks(I["L0_attn_Wk"]), chunks(I["L0_attn_Wv"])], 1),
        "w2q": chunks(I["L0_attn_Wq"]), "w2o": chunks(I["L0_attn_Wo"]), "b2o": I["L0_attn_bo"],
        "norm3": I["L0_ffn_norm_w"], "gate": chunks(I["L0_ffn_gate_w"].T),
        "w3": np.concatenate([I["L0_ffn_w13"].reshape(NE, KC, P, DM), I["L0_ffn_w2"].reshape(NE, 2, P, DM)], 1).transpose(0, 2, 1, 3),
        "w3s": np.concatenate([chunks(np.concatenate([I["L0_ffn_shared_gate_w"], I["L0_ffn_shared_up_w"]], 1)),
                               chunks(I["L0_ffn_shared_down_w"])], 1),
        "w4q": chunks(I["L1_xattn_Wq"].T),
        "w4kq": I["L1_xattn_w_kc_q"][:, :, np.concatenate(query_columns())].transpose(1, 0, 2),
        "w4qr": I["L1_xattn_W_qr"][:, np.concatenate(query_columns()[:3]), :].transpose(0, 2, 1)
                .reshape(2, NH // 2, R, DCQ).transpose(0, 2, 1, 3).reshape(P, NH // 2, DCQ),
        "w4kr": I["L1_xattn_W_kr"].transpose(0, 2, 1).reshape(2, NH // 2, R, DC).transpose(0, 2, 1, 3).reshape(P, NH // 2, DC),
        "w4kv": I["L1_xattn_w_kc_kv"].transpose(2, 0, 1), "w4o": chunks(I["L1_xattn_Wo"].T),
        "rope_q": rope_queries(), "rope_k": rope_context(),
        "w5": np.stack([chunks(I["L1_attn_" + n].T) for n in ("wq", "wk", "wv", "wo")], 1).reshape(P, 4 * KC * DM),
        "vec5": np.concatenate([I["L1_attn_" + n].reshape(KC, P).T for n in ("bq", "bk", "bv")], 1), "b5o": I["L1_attn_bo"],
        "w6": np.concatenate([chunks(I["L1_ffn_w_gate_up"].T).reshape(P, KC * 2 * FF),
                              chunks(I["L1_ffn_w_down"].T).reshape(P, FF * DM // P)], 1),
        "norm6": I["L1_ffn_norm_weight"],
    }
    nc = bacc.Bacc("TRN2", target_bir_lowering=False, num_devices=1)
    arrays, aps = {}, {}
    for name, a in T.items():
        a = np.ascontiguousarray(a)
        arrays["in_" + name] = a
        aps[name] = nc.dram_tensor("in_" + name, a.shape, mybir.dt.from_np(a.dtype), kind="ExternalInput").ap()
    o = nc.dram_tensor("out_0", (B, S, DM), F32, kind="ExternalOutput").ap()
    scratch = {"h_rows": nc.dram_tensor("h_rows", (TOK, DM), F32, kind="Internal").ap(),
               "eo_rows": nc.dram_tensor("eo_rows", (NE * CAP, DM), F32, kind="Internal").ap()}
    perceiver(nc, aps, o, scratch)
    r = run(nc, [arrays], core_ids=[0])
    return r.results[0]["out_0"]
```
